# Optimizing a Trainium2 kernel written in Bass

```python
import numpy as np
import jax
import jax.numpy as jnp

def _softmax(x, axis=-1):
    return jax.nn.softmax(x, axis=axis)

def _gelu(x):
    return jax.nn.gelu(x, approximate=True)

def _silu(x):
    return jax.nn.silu(x)

def _sigmoid(x):
    return jax.nn.sigmoid(x)

def _layernorm(x, axis=-1, eps=1e-05):
    m = jnp.mean(x, axis=axis, keepdims=True)
    v = jnp.var(x, axis=axis, keepdims=True)
    return (x - m) / jnp.sqrt(v + eps)

def _scatter_add(tgt, idx, src, axis=0):
    return tgt.at[idx].add(src)

def _segment_sum(src, seg, n):
    return jax.ops.segment_sum(src, seg, n)
kernel_name = 'mk_decoder_preln_d1_seqx_r4_190f8e'

def setup_inputs(seed: int=0):
    np.random.seed(seed)
    _w = jnp.asarray

    def _rec_inputs():
        import jax
        import jax.numpy as jnp
        _rk = jax.random.key(seed)
        x = 6.313e-05 + 0.9998 * jax.random.normal(jax.random.fold_in(_rk, 1), (64, 128, 256), jnp.float32)
        _lenS = 128 - jax.random.randint(jax.random.fold_in(_rk, 7), (64,), 0, max(1, 128 // 4) + 1, jnp.int32)
        _lenS2 = 128 - jax.random.randint(jax.random.fold_in(_rk, 8), (64,), 0, max(1, 128 // 4) + 1, jnp.int32)
        _ctx_1024P = jax.random.normal(jax.random.fold_in(_rk, 11), (64, 16, 256), jnp.float32)
        _ctx_1024c = jax.random.dirichlet(jax.random.fold_in(_rk, 511), 0.3 * jnp.ones((16,), jnp.float32), (64, 128))
        _ctx_1024t = jnp.einsum('bsk,bkd->bsd', _ctx_1024c, _ctx_1024P)
        _ctx_1024t = _ctx_1024t * jax.lax.rsqrt(jnp.mean(jnp.square(_ctx_1024t)) + 1e-12) * 0.953939
        ctx_1024 = -0.000214406 + 1.00034 * (_ctx_1024t + 0.3 * jax.random.normal(jax.random.fold_in(_rk, 611), (64, 128, 256), jnp.float32))
        return (x, ctx_1024)
    x, ctx_1024 = _rec_inputs()

    def _L0_attn_setup():
        import jax, jax.numpy as jnp
        import numpy as np
        D_MODEL = 256
        N_HEADS = 16
        D_K = D_MODEL // N_HEADS
        MIN_F = 3
        MAX_F = 10

        def _sparsity_score(Q):
            l2 = jnp.linalg.norm(Q, axis=-1)
            logp = jax.nn.log_softmax(Q, axis=-1)
            prob = jnp.exp(logp)
            entropy = -jnp.sum(prob * jnp.log(prob + 1e-09), axis=-1)
            var = jnp.var(Q, axis=-1, ddof=1)
            return 0.5 * l2 + 0.3 * entropy + 0.2 * var
        key = jax.random.key(seed)
        ks = jax.random.split(key, 9)
        B, L = (4, 2048)
        x = jax.random.normal(ks[0], (B, L, D_MODEL), jnp.float32)

        def w(k):
            return jax.random.normal(k, (D_MODEL, D_MODEL), jnp.float32) * 0.02

        def b(k):
            return jax.random.normal(k, (D_MODEL,), jnp.float32) * 0.02
        return {'x': x, 'wq': w(ks[1]), 'bq': b(ks[2]), 'wk': w(ks[3]), 'bk': b(ks[4]), 'wv': w(ks[5]), 'bv': b(ks[6]), 'wo': w(ks[7]), 'bo': b(ks[8])}
    _L0_attn_all = _L0_attn_setup()
    _L0_attn_in = {k: v for k, v in _L0_attn_all.items() if k in ('wq', 'bq', 'wk', 'bk', 'wv', 'bv', 'wo', 'bo')}
    del _L0_attn_all

    def _L0_xattn_setup():
        import jax, jax.numpy as jnp
        import numpy as np
        from jax import lax
        BIG = jnp.float32(1e+30)

        def _pairwise_euclidean(a, b):
            aa = jnp.sum(a * a, axis=-1)[:, None]
            bb = jnp.sum(b * b, axis=-1)[None, :]
            ab = a @ b.T
            return jnp.sqrt(jnp.maximum(aa + bb - 2.0 * ab, 0.0))

        def _dtw_cost(D):
            row0 = jnp.cumsum(D[0])

            def row_step(prev_row, d_row):
                first = d_row[0] + prev_row[0]

                def col_step(left, inp):
                    d_ij, up, diag = inp
                    r = d_ij + jnp.minimum(jnp.minimum(up, left), diag)
                    return (r, r)
                _, rest = lax.scan(col_step, first, (d_row[1:], prev_row[1:], prev_row[:-1]))
                row = jnp.concatenate([first[None], rest])
                return (row, row)
            _, rows = lax.scan(row_step, row0, D[1:])
            return jnp.concatenate([row0[None], rows], axis=0)

        def _backtrack(R, T1, T2):
            L = T1 + T2 - 1

            def step(carry, _):
                i, j, done = carry
                valid = jnp.logical_not(done)
                cd = jnp.where((i > 0) & (j > 0), R[jnp.maximum(i - 1, 0), jnp.maximum(j - 1, 0)], BIG)
                cu = jnp.where(i > 0, R[jnp.maximum(i - 1, 0), j], BIG)
                cl = jnp.where(j > 0, R[i, jnp.maximum(j - 1, 0)], BIG)
                choice = jnp.argmin(jnp.stack([cd, cu, cl]))
                ni = jnp.where(choice <= 1, i - 1, i)
                nj = jnp.where((choice == 0) | (choice == 2), j - 1, j)
                at_origin = (i == 0) & (j == 0)
                ni = jnp.where(at_origin, 0, ni)
                nj = jnp.where(at_origin, 0, nj)
                return ((ni, nj, done | at_origin), (i, j, valid))
            init = (jnp.int32(T1 - 1), jnp.int32(T2 - 1), jnp.bool_(False))
            _, (i_idx, j_idx, valid) = lax.scan(step, init, None, length=L)
            return (i_idx, j_idx, valid)

        def _align_one(small, large):
            T_small, d = small.shape
            T_large = large.shape[0]
            D = _pairwise_euclidean(small, large)
            R = _dtw_cost(D)
            i_idx, j_idx, valid = _backtrack(R, T_small, T_large)
            contrib = small[i_idx] * valid[:, None].astype(small.dtype)
            expanded = jnp.zeros((T_large, d), dtype=small.dtype).at[j_idx].add(contrib)
            return expanded
        key = jax.random.key(seed)
        k1, k2 = jax.random.split(key)
        teacher = jax.random.normal(k1, (16, 100, 256), dtype=jnp.float32)
        student = jax.random.normal(k2, (16, 150, 256), dtype=jnp.float32)
        return {'teacher_features': teacher, 'student_features': student}
    _L0_xattn_all = _L0_xattn_setup()
    _L0_xattn_in = {k: v for k, v in _L0_xattn_all.items() if k in ()}
    del _L0_xattn_all

    def _L0_ffn_setup():
        import jax, jax.numpy as jnp
        import numpy as np
        DIM = 256
        E = 8
        K = 2
        EPS = 1e-05

        def _ln(x, g, b):
            mu = jnp.mean(x, axis=-1, keepdims=True)
            var = jnp.mean(jnp.square(x - mu), axis=-1, keepdims=True)
            return (x - mu) * jax.lax.rsqrt(var + EPS) * g + b
        key = jax.random.key(seed)
        ks = jax.random.split(key, 8)
        H = 2 * DIM
        s_in = 1.0 / np.sqrt(DIM)
        s_h = 1.0 / np.sqrt(H)
        return {'x': jax.random.normal(ks[0], (2, 512, DIM), dtype=jnp.float32), 'gate_w': jax.random.uniform(ks[1], (DIM, E), minval=-s_in, maxval=s_in, dtype=jnp.float32), 'w1': jax.random.uniform(ks[2], (E, DIM, H), minval=-s_in, maxval=s_in, dtype=jnp.float32), 'b1': jax.random.uniform(ks[3], (E, H), minval=-s_in, maxval=s_in, dtype=jnp.float32), 'ln1_g': jnp.ones((E, H), dtype=jnp.float32), 'ln1_b': jnp.zeros((E, H), dtype=jnp.float32), 'w2': jax.random.uniform(ks[4], (E, H, DIM), minval=-s_h, maxval=s_h, dtype=jnp.float32), 'b2': jax.random.uniform(ks[5], (E, DIM), minval=-s_h, maxval=s_h, dtype=jnp.float32), 'ln_g': jnp.ones((DIM,), dtype=jnp.float32), 'ln_b': jnp.zeros((DIM,), dtype=jnp.float32)}
    _L0_ffn_all = _L0_ffn_setup()
    _L0_ffn_in = {k: v for k, v in _L0_ffn_all.items() if k in ('gate_w', 'w1', 'b1', 'ln1_g', 'ln1_b', 'w2', 'b2', 'ln_g', 'ln_b')}
    del _L0_ffn_all
    return {'x': x, 'ctx_1024': ctx_1024, 'L0_attn_wq': _L0_attn_in['wq'], 'L0_attn_bq': _L0_attn_in['bq'], 'L0_attn_wk': _L0_attn_in['wk'], 'L0_attn_bk': _L0_attn_in['bk'], 'L0_attn_wv': _L0_attn_in['wv'], 'L0_attn_bv': _L0_attn_in['bv'], 'L0_attn_wo': _L0_attn_in['wo'], 'L0_attn_bo': _L0_attn_in['bo'], 'L0_ffn_gate_w': _L0_ffn_in['gate_w'], 'L0_ffn_w1': _L0_ffn_in['w1'], 'L0_ffn_b1': _L0_ffn_in['b1'], 'L0_ffn_ln1_g': _L0_ffn_in['ln1_g'], 'L0_ffn_ln1_b': _L0_ffn_in['ln1_b'], 'L0_ffn_w2': _L0_ffn_in['w2'], 'L0_ffn_b2': _L0_ffn_in['b2'], 'L0_ffn_ln_g': _L0_ffn_in['ln_g'], 'L0_ffn_ln_b': _L0_ffn_in['ln_b']}

def reference(x, ctx_1024, L0_attn_wq, L0_attn_bq, L0_attn_wk, L0_attn_bk, L0_attn_wv, L0_attn_bv, L0_attn_wo, L0_attn_bo, L0_ffn_gate_w, L0_ffn_w1, L0_ffn_b1, L0_ffn_ln1_g, L0_ffn_ln1_b, L0_ffn_w2, L0_ffn_b2, L0_ffn_ln_g, L0_ffn_ln_b):
    import jax
    import jax.numpy as jnp

    def _L0_attn_ref(x, wq, bq, wk, bk, wv, bv, wo, bo):
        import jax, jax.numpy as jnp
        import numpy as np
        D_MODEL = 256
        N_HEADS = 16
        D_K = D_MODEL // N_HEADS
        MIN_F = 3
        MAX_F = 10

        def _sparsity_score(Q):
            l2 = jnp.linalg.norm(Q, axis=-1)
            logp = jax.nn.log_softmax(Q, axis=-1)
            prob = jnp.exp(logp)
            entropy = -jnp.sum(prob * jnp.log(prob + 1e-09), axis=-1)
            var = jnp.var(Q, axis=-1, ddof=1)
            return 0.5 * l2 + 0.3 * entropy + 0.2 * var
        B, L, D = x.shape
        H, dk = (N_HEADS, D_K)
        Q = (x @ wq.T + bq).reshape(B, L, H, dk).transpose(0, 2, 1, 3)
        K = (x @ wk.T + bk).reshape(B, L, H, dk).transpose(0, 2, 1, 3)
        V = (x @ wv.T + bv).reshape(B, L, H, dk).transpose(0, 2, 1, 3)
        q_scores = _sparsity_score(Q)
        q_std = jnp.std(q_scores, axis=2, keepdims=True, ddof=1)
        q_mean = jnp.mean(q_scores, axis=2, keepdims=True)
        factor = jnp.clip(jnp.round(q_std / (q_mean + 1e-06) * MAX_F).astype(jnp.int32), MIN_F, MAX_F)
        u = factor[:, 0, 0]
        _, top_idx = jax.lax.top_k(q_scores, MAX_F)
        mask = jnp.arange(MAX_F)[None, None, :] < u[:, None, None]
        Q_sparse = jnp.take_along_axis(Q, top_idx[..., None], axis=2)
        scores = jnp.einsum('bhud,bhld->bhul', Q_sparse, K) / np.sqrt(dk).astype(np.float32)
        attn = jax.nn.softmax(scores, axis=-1)
        out = jnp.einsum('bhul,bhld->bhud', attn, V)
        out = out * mask[..., None].astype(out.dtype)
        bi = jnp.arange(B)[:, None, None]
        hi = jnp.arange(H)[None, :, None]
        full = jnp.zeros((B, H, L, dk), out.dtype).at[bi, hi, top_idx].set(out)
        merged = full.transpose(0, 2, 1, 3).reshape(B, L, D)
        return merged @ wo.T + bo

    def _L0_xattn_ref(teacher_features, student_features):
        import jax, jax.numpy as jnp
        import numpy as np
        from jax import lax
        BIG = jnp.float32(1e+30)

        def _pairwise_euclidean(a, b):
            aa = jnp.sum(a * a, axis=-1)[:, None]
            bb = jnp.sum(b * b, axis=-1)[None, :]
            ab = a @ b.T
            return jnp.sqrt(jnp.maximum(aa + bb - 2.0 * ab, 0.0))

        def _dtw_cost(D):
            row0 = jnp.cumsum(D[0])

            def row_step(prev_row, d_row):
                first = d_row[0] + prev_row[0]

                def col_step(left, inp):
                    d_ij, up, diag = inp
                    r = d_ij + jnp.minimum(jnp.minimum(up, left), diag)
                    return (r, r)
                _, rest = lax.scan(col_step, first, (d_row[1:], prev_row[1:], prev_row[:-1]))
                row = jnp.concatenate([first[None], rest])
                return (row, row)
            _, rows = lax.scan(row_step, row0, D[1:])
            return jnp.concatenate([row0[None], rows], axis=0)

        def _backtrack(R, T1, T2):
            L = T1 + T2 - 1

            def step(carry, _):
                i, j, done = carry
                valid = jnp.logical_not(done)
                cd = jnp.where((i > 0) & (j > 0), R[jnp.maximum(i - 1, 0), jnp.maximum(j - 1, 0)], BIG)
                cu = jnp.where(i > 0, R[jnp.maximum(i - 1, 0), j], BIG)
                cl = jnp.where(j > 0, R[i, jnp.maximum(j - 1, 0)], BIG)
                choice = jnp.argmin(jnp.stack([cd, cu, cl]))
                ni = jnp.where(choice <= 1, i - 1, i)
                nj = jnp.where((choice == 0) | (choice == 2), j - 1, j)
                at_origin = (i == 0) & (j == 0)
                ni = jnp.where(at_origin, 0, ni)
                nj = jnp.where(at_origin, 0, nj)
                return ((ni, nj, done | at_origin), (i, j, valid))
            init = (jnp.int32(T1 - 1), jnp.int32(T2 - 1), jnp.bool_(False))
            _, (i_idx, j_idx, valid) = lax.scan(step, init, None, length=L)
            return (i_idx, j_idx, valid)

        def _align_one(small, large):
            T_small, d = small.shape
            T_large = large.shape[0]
            D = _pairwise_euclidean(small, large)
            R = _dtw_cost(D)
            i_idx, j_idx, valid = _backtrack(R, T_small, T_large)
            contrib = small[i_idx] * valid[:, None].astype(small.dtype)
            expanded = jnp.zeros((T_large, d), dtype=small.dtype).at[j_idx].add(contrib)
            return expanded
        return jax.vmap(_align_one)(teacher_features, student_features)

    def _L0_ffn_ref(x, gate_w, w1, b1, ln1_g, ln1_b, w2, b2, ln_g, ln_b):
        import jax, jax.numpy as jnp
        import numpy as np
        DIM = 256
        E = 8
        K = 2
        EPS = 1e-05

        def _ln(x, g, b):
            mu = jnp.mean(x, axis=-1, keepdims=True)
            var = jnp.mean(jnp.square(x - mu), axis=-1, keepdims=True)
            return (x - mu) * jax.lax.rsqrt(var + EPS) * g + b
        shape = x.shape
        xf = x.reshape(-1, shape[-1])
        gates = jax.nn.softmax(xf @ gate_w, axis=-1)
        topw, topi = jax.lax.top_k(gates, K)
        topw = topw / jnp.sum(topw, axis=-1, keepdims=True)
        combine = jnp.sum(topw[:, :, None] * jax.nn.one_hot(topi, E, dtype=xf.dtype), axis=1)
        h = jnp.einsum('td,edh->teh', xf, w1) + b1
        h = _ln(h, ln1_g, ln1_b)
        h = jax.nn.gelu(h, approximate=False)
        y = jnp.einsum('teh,ehd->ted', h, w2) + b2
        out = jnp.einsum('ted,te->td', y, combine)
        out = _ln(out + xf, ln_g, ln_b)
        return out.reshape(shape)
    x = x + _L0_attn_ref(_layernorm(x, axis=-1), L0_attn_wq, L0_attn_bq, L0_attn_wk, L0_attn_bk, L0_attn_wv, L0_attn_bv, L0_attn_wo, L0_attn_bo)
    x = x + _L0_xattn_ref(ctx_1024, _layernorm(x, axis=-1))
    x = x + _L0_ffn_ref(_layernorm(x, axis=-1), L0_ffn_gate_w, L0_ffn_w1, L0_ffn_b1, L0_ffn_ln1_g, L0_ffn_ln1_b, L0_ffn_w2, L0_ffn_b2, L0_ffn_ln_g, L0_ffn_ln_b)
    return x

_drawn_inputs = setup_inputs


def setup_inputs(seed=0):
    import zlib

    import numpy as np

    out = dict(_drawn_inputs(seed))
    spreads = {'L0_ffn_ln1_g': (1.0, 0.594),
     'L0_ffn_ln1_b': (0.0, 0.684),
     'L0_ffn_ln_g': (1.0, 0.2),
     'L0_ffn_ln_b': (0.0, 0.1)}
    factors = {'L0_attn_wq': 8.0,
     'L0_attn_bq': 8.0,
     'L0_attn_wk': 8.0,
     'L0_attn_bk': 8.0,
     'L0_attn_wv': 8.0,
     'L0_attn_bv': 8.0,
     'L0_attn_wo': 8.0,
     'L0_attn_bo': 3.365,
     'L0_ffn_b1': 7.289,
     'L0_ffn_b2': 7.151}
    for name, (base, spread) in spreads.items():
        noise = np.random.default_rng([zlib.crc32(name.encode()), seed]).standard_normal(out[name].shape)
        drawn = base * np.exp(spread * noise) if base else spread * noise
        out[name] = jnp.asarray(drawn.astype(out[name].dtype))
    for name, factor in factors.items():
        out[name] = (out[name] * factor).astype(out[name].dtype)
    return out
```

```python
from contextlib import ExitStack

import concourse.bass as bass
from concourse import mybir

F32 = mybir.dt.float32
BF16 = mybir.dt.bfloat16
I32 = mybir.dt.int32
U32 = mybir.dt.uint32
ALU = mybir.AluOpType
ACT = mybir.ActivationFunctionType
AX = mybir.AxisListType

P = 128
D = 256
KC = D // P
HEADS = 16
DK = D // HEADS
HC = HEADS // KC
TOP = 10
MIN_TOP = 3
HU = HC * TOP
G = 8
EXPERTS = 8
HID = 512
HK = HID // P
EPS = 1e-5
BIG = 1e30
MAGIC = 12582912.0
MOE_UNROLL = 4
PATH_UNROLL = 14
FREE = 16
ROWS = 16


def decoder_layer(nc, x, ctx_rows, ctx_cols, w_qkv, b_qv, b_k, w_o, b_o, gate_w, w1, b1, ln1_g, ln1_b,
                  w2, b2, ln_g, ln_b, out):
    B = x.shape[0]
    NG = B // G
    NS = 2 * B + EXPERTS
    NS += -NS % MOE_UNROLL
    x1_dram = nc.dram_tensor("x1_scratch", [B, P, D], F32)
    dist_dram = nc.dram_tensor("dist_scratch", [B, P, P], F32)
    x2_dram = nc.dram_tensor("x2_scratch", [B, P, D], F32)
    xn_dram = nc.dram_tensor("ffn_in_scratch", [B, P, D], F32)
    slots_in = nc.dram_tensor("slots_in_scratch", [NS * P, D], F32)
    slots_out = nc.dram_tensor("slots_out_scratch", [NS * P, D], F32)

    es = ExitStack()
    with es:
        def sb(name, shape, dt=F32):
            return es.enter_context(nc.sbuf_tensor(name, shape, dt))

        phase = []

        def sem(name, start=0):
            phase.append(nc.alloc_semaphore(name=name))
            if start:
                nc.gpsimd.sem_inc(phase[-1], start)
            return phase[-1]

        def next_phase():
            nc.clear_and_free_semaphores(phase)
            nc.all_engine_barrier()
            phase.clear()

        def apart(eng):
            eng.nop(nofuse=True)

        ps = [es.enter_context(nc.psum_tensor(f"bank{i}", [P, 512], F32)) for i in range(8)]

        ident = sb("ident", [P, P])
        iota_f1 = sb("iota_f1", [P, P])
        iota_p1 = sb("iota_p1", [P, 1])
        iota_2j = sb("iota_2j", [P, P])
        iota_256 = sb("iota_256", [P, 2 * P])
        iota_small = sb("iota_small", [P, TOP])
        iota_slot = sb("iota_slot", [P, NS])
        head_block = sb("head_block", [P, KC, HC, TOP])
        head_block2 = sb("head_block2", [HU, HC, DK])
        seq_rows = sb("seq_rows", [P, G, P], BF16)
        first_head = sb("first_head", [P, P], BF16)
        head_of_row = sb("head_of_row", [P, HEADS])
        neg_half = sb("neg_half", [P, P])
        before = sb("before", [P, P], BF16)
        ones_bf = sb("ones_bf", [P, P], BF16)
        tiny = sb("tiny", [P, 1])
        ones8 = sb("ones8", [P, EXPERTS])
        codes = sb("codes", [B, P + 1])
        row_code = sb("row_code", [P, 2, B])
        top_val = sb("top_val", [P, B, 2])
        top_exp = sb("top_exp", [P, B, 2])
        slot_f = sb("slot_f", [P, B, 2])
        slot_i = sb("slot_i", [P, B, 2], I32)
        pair_w = sb("pair_w", [P, 2, B])
        tile_expert = sb("tile_expert", [P, NS], I32)
        stats = sb("stats", [P, G, 6])
        moments = sb("moments", [P, G, 2])
        rstd = sb("rstd", [P, G])
        exponents = sb("exponents", [P, G + 1])

        ARENA = 41600
        arena = sb("arena", [P, ARENA])

        def carver():
            at = [0]

            def carve(*shape, dt=F32, rows=P):
                n = 1
                for s in shape:
                    n *= s
                words = n if dt != BF16 else (n + 1) // 2
                v = arena[0:rows, at[0]:at[0] + words]
                at[0] += words
                assert at[0] <= ARENA, at[0]
                if dt != F32:
                    v = v.bitcast(dt)
                if len(shape) > 1:
                    names = "abcd"[:len(shape)]
                    v = v.rearrange(f"p ({' '.join(names)}) -> p {' '.join(names)}",
                                    **dict(zip(names, shape)))
                return v
            return carve

        made = sem("const_made")
        with nc.Block() as block:
            @block.gpsimd
            def _(pool):
                n = 0

                def step(ins):
                    nonlocal n
                    ins.then_inc(made, 1)
                    n += 1
                    pool.wait_ge(made, n)

                def iota(t, pattern, base, mult):
                    step(pool.iota(t, pattern=pattern, base=base, channel_multiplier=mult,
                                   allow_small_or_imprecise_dtypes=True))

                def keep(t, pattern, base, mult, op, fill):
                    step(pool.affine_select(out=t, in_=t, pattern=pattern, compare_op=op, fill=fill,
                                            base=base, channel_multiplier=mult))

                iota(iota_slot[:, :], [[1, NS]], 0, 0)
                iota(iota_f1[:, :], [[1, P]], 1, 0)
                iota(iota_p1[:, :], [[1, 1]], 1, 1)
                iota(iota_2j[:, :], [[2, P]], 0, 0)
                iota(iota_256[:, :], [[1, 2 * P]], 1, 0)
                iota(iota_small[:, :], [[1, TOP]], 0, 0)
                step(pool.memset(ident[:, :], 0.0))
                keep(ident[:, :], [[-1, P]], 0, 1, ALU.not_equal, 1.0)
                step(pool.memset(head_block[:, :, :, :], float(DK) ** -0.5))
                for c in range(KC):
                    v = head_block[:, c, :, :]
                    keep(v, [[-DK, HC], [0, TOP]], 0, 1, ALU.is_ge, 0.0)
                    keep(v, [[DK, HC], [0, TOP]], DK - 1, -1, ALU.is_ge, 0.0)
                step(pool.memset(head_block2[:, :, :], 1.0))
                keep(head_block2[:, :, :], [[-TOP, HC], [0, DK]], 0, 1, ALU.is_ge, 0.0)
                keep(head_block2[:, :, :], [[TOP, HC], [0, DK]], TOP - 1, -1, ALU.is_ge, 0.0)
                step(pool.memset(seq_rows[:, :, :], 1.0))
                keep(seq_rows[:, :, :], [[-HEADS, G], [0, P]], 0, 1, ALU.is_ge, 0.0)
                keep(seq_rows[:, :, :], [[HEADS, G], [0, P]], HEADS - 1, -1, ALU.is_ge, 0.0)
                step(pool.memset(first_head[:, :], 1.0))
                keep(first_head[:, :], [[-HEADS, G], [0, HEADS]], 0, 1, ALU.is_equal, 0.0)
                step(pool.memset(before[:, :], 1.0))
                keep(before[:, :], [[1, P]], 0, -1, ALU.is_gt, 0.0)
                step(pool.memset(ones_bf[:, :], 1.0))
                step(pool.memset(neg_half[:, :], -0.5))
                step(pool.memset(tiny[:, :], 1e-9))
                step(pool.memset(ones8[:, :], 1.0))
                step(pool.memset(exponents[:, 0:G], -0.5))
                step(pool.memset(exponents[:, G:G + 1], 0.5))

            @block.vector
            def _(dve):
                dve.wait_ge(made, 8)
                dve.tensor_reduce(head_of_row[:, :], ident[:, :].rearrange("p (s h) -> p h s", h=HEADS),
                                  AX.X, ALU.max).then_inc(sem("head_of_row_made"), 1)

        next_phase()
        carve = carver()
        x_in = carve(G, D)
        x_res = carve(G, D)
        xn = carve(G, D)
        xn_t = carve(G, KC, P)
        qv = carve(G, 2 * D)
        k_t = carve(G, KC, P)
        c1 = carve(G, D)
        c2 = carve(G, D)
        c3 = carve(G, D)
        sel = carve(G, KC * HU)
        q_sel = carve(G, KC * HU)
        a_t = carve(G, KC * HU)
        sel_t = carve(G, KC, P, rows=HU)
        dist = carve(G, P)
        ctx_t = carve(G, KC, P)
        ctx_sq = carve(G, KC, P)
        w_qkv_sb = carve(KC, 3 * D)
        w_o_sb = carve(KC, D)
        b_qv_sb = carve(2 * D)
        b_k_sb = carve(KC)
        b_o_sb = carve(D)
        zeros = carve(4 * D)
        sum_q = carve(P)
        max_q = carve(P)
        mean_q = carve(P)
        sum_sq = carve(P)
        sum_e = carve(P)
        rec_e = carve(P)
        sum_pl = carve(P)
        mean_sq = carve(P)
        l2 = carve(P)
        score = carve(P)
        score_t = carve(P)
        score_u = carve(P)
        t_stats = carve(6)
        t_mom = carve(2)
        t_a = carve(1)
        t_b = carve(1)
        t_c = carve(1)
        t_dev = carve(1)
        factor = carve(2, dt=BF16)[:, 0:1]
        keep_n = carve(1)
        top8 = carve(2, 8)
        idx_u = carve(2, 8, dt=U32)
        idx_f = carve(2 * 8)
        kept = carve(TOP)
        idx1 = carve(TOP)
        idx_rows = carve(HEADS, TOP, dt=BF16)
        idx_cols = carve(KC, G, rows=HU)
        neg_max = carve(G, KC, rows=HU)
        e_sum = carve(G, KC, rows=HU)
        e_rec = carve(G, KC, rows=HU)
        e_buf, o_sel, m_t = (c.rearrange("p g (c n) -> p g c n", c=KC) for c in (c1, c2, c3))

        zero_made = sem("zero_made")
        slots_zeroed = sem("slots_zeroed")
        weights_in = sem("attn_weights_in")
        x_loaded, ctx_loaded = sem("x_loaded"), sem("ctx_loaded")
        x1_stored, dist_stored = sem("x1_stored", FREE), sem("dist_stored", FREE)
        stats_a, moments_a, rstd_a, xn_ready = sem("stats_a"), sem("moments_a"), sem("rstd_a"), sem("xn_ready")
        x_res_ready = sem("x_res_ready")
        xnt_psum, xnt_ready = sem("xnt_psum"), sem("xnt_ready")
        qv_psum, qv_ready = sem("qv_psum"), sem("qv_ready")
        kt_psum, kt_ready = sem("kt_psum"), sem("kt_ready")
        sum_q_done, max_q_done, mean_q_done = sem("sum_q_done"), sem("max_q_done"), sem("mean_q_done")
        centred, shifted, expd, squared = sem("centred"), sem("shifted"), sem("expd"), sem("squared")
        sum_sq_done, rec_e_done, sum_e_done = sem("sum_sq_done"), sem("rec_e_done"), sem("sum_e_done")
        prob_done, logp_done, plogp_done = sem("prob_done"), sem("logp_done"), sem("plogp_done")
        score_step = sem("score_step")
        l2_in_done, l2_done = sem("l2_in_done"), sem("l2_done")
        score_ready, score_psum = sem("score_ready"), sem("score_psum")
        top_step = sem("top_step")
        sample_var = sem("sample_var")
        eps_a, eps_b = sem("eps_a"), sem("eps_b")
        variance_ready, deviation_ready = sem("variance_ready"), sem("deviation_ready")
        factor_ready, keep_psum = sem("factor_ready"), sem("keep_psum")
        idx_rows_ready, idx_cols_psum, idx_cols_ready = (
            sem("idx_rows_ready"), sem("idx_cols_psum"), sem("idx_cols_ready"))
        sel_t_ready = sem("sel_t_ready")
        idx_psum, sel_ready = sem("idx_psum"), sem("sel_ready")
        qs_psum, qs_ready = sem("qs_psum"), sem("qs_ready")
        s_psum, max_ready, e_ready = sem("s_psum"), sem("max_ready"), sem("e_ready")
        at_psum, at_ready = sem("at_psum"), sem("at_ready")
        o_psum, e_rec_done, o_ready = sem("o_psum"), sem("e_rec_done"), sem("o_ready")
        mt_psum, mt_ready = sem("mt_psum"), sem("mt_ready")
        attn_psum, x1_ready = sem("attn_psum"), sem("x1_ready")
        stats_b, moments_b, rstd_b, yn_ready = sem("stats_b"), sem("moments_b"), sem("rstd_b"), sem("yn_ready")
        ynt_psum, ynt_ready = sem("ynt_psum"), sem("ynt_ready")
        ctx_sq_ready = sem("ctx_sq_ready")
        sem_idx1 = sem("idx1_done")
        dist_psum, dist_sq_ready, dist_ready = sem("dist_psum"), sem("dist_sq_ready"), sem("dist_ready", FREE)

        def layer_norm(dve, g, src, dst, s_stats, s_mom, s_rstd, s_out, before_tile=None):
            for b in range(G):
                if before_tile:
                    before_tile(b)
                dve.bn_stats(stats[:, b, :], src(b)).then_inc(s_stats, 1)
            for b in range(G):
                dve.wait_ge(s_stats, g * G + (b + 1))
                apart(dve)
                dve.bn_aggr(moments[:, b, :], stats[:, b, :]).then_inc(s_mom, 1)
            dve.wait_ge(s_rstd, g + 1)
            for b in range(G):
                dve.tensor_scalar(dst(b), src(b), moments[:, b, 0:1], rstd[:, b:b + 1],
                                  ALU.subtract, ALU.mult).then_inc(s_out, 1)

        def inverse_deviation(pool, g, s_mom, s_eps, s_rstd):
            pool.wait_ge(s_mom, g * G + G)
            apart(pool)
            pool.tensor_scalar(rstd[:, :], moments[:, :, 1], EPS, None, ALU.add).then_inc(s_eps, 1)
            pool.wait_ge(s_eps, g + 1)
            pool.tensor_tensor(rstd[:, :], rstd[:, :], exponents[:, 0:G], ALU.pow).then_inc(s_rstd, 1)

        def load_group(eng, tile, dram, g, done, pattern="g p d -> p g d"):
            for half in range(2):
                eng.dma_start(tile[:, half * G // 2:(half + 1) * G // 2],
                              dram[bass.ds(g * G + half * G // 2, G // 2)].rearrange(pattern, **(
                                  {"p": P} if "(" in pattern else {}))).then_inc(done, 16)

        def heads(t):
            return t.rearrange("p g (h d) -> p g h d", h=HEADS)

        def per_head(t):
            return t.rearrange("p (g h) -> p g h", g=G).unsqueeze(3).to_broadcast([P, G, HEADS, DK])

        with nc.Block() as block:
            @block.sync
            def _(sp):
                sp.dma_start(w_qkv_sb, w_qkv.rearrange("(c p) n -> p c n", p=P)).then_inc(weights_in, 16)
                sp.dma_start(w_o_sb, w_o.rearrange("(c p) n -> p c n", p=P)).then_inc(weights_in, 16)
                sp.dma_start(b_qv_sb, b_qv.partition_broadcast(P)).then_inc(weights_in, 16)
                sp.dma_start(b_o_sb, b_o.partition_broadcast(P)).then_inc(weights_in, 16)
                with nc.allow_non_contiguous_dma(reason="256 biases, one per partition"):
                    sp.dma_start(b_k_sb, b_k.rearrange("(c p) -> p c", p=P)).then_inc(weights_in, 16)
                load_group(sp, x_in, x, 0, x_loaded)
                with sp.Fori(0, NG) as g:
                    following = sp.snap((g + 1) % NG)
                    sp.wait_ge(dist_ready, g * G + FREE)
                    load_group(sp, ctx_t, ctx_cols, g, ctx_loaded, "g (c p) n -> p g c n")
                    sp.wait_ge(xn_ready, g * G + G)
                    apart(sp)
                    sp.wait_ge(x_res_ready, g + 1)
                    apart(sp)
                    load_group(sp, x_in, x, following, x_loaded)
                    sp.wait_ge(x1_ready, g * G + G)
                    sp.dma_start(x1_dram[bass.ds(g * G, G)].rearrange("g p d -> p g d"), x_res)\
                      .then_inc(x1_stored, 16)
                    sp.wait_ge(dist_ready, g * G + G + FREE)
                    sp.dma_start(dist_dram[bass.ds(g * G, G)].rearrange("g p d -> p g d"), dist)\
                      .then_inc(dist_stored, 16)
                sp.wait_ge(x_loaded, 32 * (NG + 1))
                sp.wait_ge(x1_stored, 16 * NG + FREE)
                sp.wait_ge(dist_stored, 16 * NG + FREE)

            @block.gpsimd
            def _(pool):
                pool.memset(zeros, 0.0).then_inc(zero_made, 1)
                pool.wait_ge(zero_made, 1)
                with pool.Fori(0, NS // 4) as i:
                    pool.dma_start(slots_in[bass.ds(i * 4 * P, 4 * P)].rearrange("(p r) d -> p (r d)", p=P),
                                   zeros).then_inc(slots_zeroed, 16)
                pool.wait_ge(weights_in, 16 * 5)
                with pool.Fori(0, NG) as g:
                    inverse_deviation(pool, g, moments_a, eps_a, rstd_a)
                    pool.wait_ge(x_loaded, g * 32 + 32)
                    pool.wait_ge(x1_stored, g * 16 + FREE)
                    pool.tensor_tensor(x_res, x_in, b_o_sb.unsqueeze(1).to_broadcast([P, G, D]), ALU.add)\
                        .then_inc(x_res_ready, 1)
                    pool.wait_ge(ctx_loaded, g * 32 + 32)
                    pool.tensor_tensor(ctx_sq, ctx_t, ctx_t, ALU.mult).then_inc(ctx_sq_ready, 1)
                    q = heads(qv[:, :, 0:D])
                    pool.wait_ge(mean_q_done, g + 1)
                    pool.tensor_tensor(heads(c1), q, per_head(mean_q), ALU.subtract).then_inc(centred, 1)
                    pool.wait_ge(max_q_done, g + 1)
                    pool.tensor_tensor(heads(c2), q, per_head(max_q), ALU.subtract).then_inc(shifted, 1)
                    pool.wait_ge(rec_e_done, g + 1)
                    pool.tensor_tensor(heads(c2), heads(c2), per_head(rec_e), ALU.mult).then_inc(prob_done, 1)
                    pool.wait_ge(prob_done, g + 1)
                    pool.wait_ge(logp_done, g + 1)
                    pool.tensor_tensor(c3, c3, c2, ALU.mult).then_inc(plogp_done, 1)
                    pool.wait_ge(variance_ready, g + 1)
                    apart(pool)
                    pool.tensor_scalar(t_dev, t_mom[:, 1:2], P / (P - 1), None, ALU.mult).then_inc(sample_var, 1)
                    pool.wait_ge(sample_var, g + 1)
                    pool.tensor_tensor(t_dev, t_dev, exponents[:, G:G + 1], ALU.pow).then_inc(deviation_ready, 1)
                    inverse_deviation(pool, g, moments_b, eps_b, rstd_b)
                pool.wait_ge(slots_zeroed, 16 * (NS // 4))

            @block.tensor
            def _(pe):
                pe.wait_ge(weights_in, 16 * 5)
                with pe.Fori(0, NG) as g:
                    def transposes(src, b, done):
                        for c in range(KC):
                            ins = pe.transpose(ps[b][:, c * P:(c + 1) * P], src[:, b, c * P:(c + 1) * P],
                                               ident[:, :])
                        ins.then_inc(done, 1)

                    for b in range(G):
                        pe.wait_ge(xn_ready, g * G + (b + 1))
                        transposes(xn, b, xnt_psum)
                    for b in range(G):
                        pe.wait_ge(xnt_ready, g * G + (b + 1))
                        for c in range(KC):
                            ins = pe.matmul(ps[b][:, :], xn_t[:, b, c, :], w_qkv_sb[:, c, 0:2 * D],
                                            start=(c == 0), stop=(c == KC - 1))
                        ins.then_inc(qv_psum, 1)
                    for b in range(G):
                        pe.wait_ge(qv_ready, g * G + (b + 1))
                        for m in range(KC):
                            for c in range(KC):
                                ins = pe.matmul(ps[b][:, m * P:(m + 1) * P],
                                                w_qkv_sb[:, c, 2 * D + m * P:2 * D + (m + 1) * P],
                                                xn_t[:, b, c, :], start=(c == 0), stop=(c == KC - 1))
                        ins.then_inc(kt_psum, 1)
                    pe.wait_ge(kt_ready, g * G + G)
                    pe.wait_ge(score_ready, g + 1)
                    pe.transpose(ps[0][:, 0:P], score, ident[:, :]).then_inc(score_psum, 1)
                    pe.wait_ge(factor_ready, g + 1)
                    pe.matmul(ps[1][:, 0:1], first_head[:, :], factor, start=True, stop=True)\
                      .then_inc(keep_psum, 1)
                    pe.wait_ge(idx_rows_ready, g + 1)
                    flat_idx = idx_rows.rearrange("p h u -> p (h u)")
                    for c in range(KC):
                        ins = pe.matmul(ps[7][0:HU, c * G:(c + 1) * G], flat_idx[:, c * HU:(c + 1) * HU],
                                        seq_rows[:, :, 0], start=True, stop=True)
                    ins.then_inc(idx_cols_psum, 1)
                    for b in range(G):
                        if b == 7:
                            pe.wait_ge(idx_cols_ready, g + 1)
                        pe.matmul(ps[b][:, 0:KC * HU], seq_rows[:, b, :], flat_idx, start=True, stop=True)\
                          .then_inc(idx_psum, 1)
                    for b in range(G):
                        pe.wait_ge(sel_ready, g * G + (b + 1))
                        for c in range(KC):
                            ins = pe.matmul(ps[b][:, c * HU:(c + 1) * HU], qv[:, b, c * P:(c + 1) * P],
                                            sel[:, b, c * HU:(c + 1) * HU], start=True, stop=True)
                        ins.then_inc(qs_psum, 1)
                    for b in range(G):
                        pe.wait_ge(qs_ready, g * G + (b + 1))
                        for c in range(KC):
                            ins = pe.matmul(ps[b][0:HU, c * P:(c + 1) * P], q_sel[:, b, c * HU:(c + 1) * HU],
                                            k_t[:, b, c, :], start=True, stop=True)
                        ins.then_inc(s_psum, 1)
                    for b in range(G):
                        pe.wait_ge(e_ready, g * G + (b + 1))
                        for c in range(KC):
                            ins = pe.transpose(ps[b][:, c * HU:(c + 1) * HU], e_buf[0:HU, b, c, :],
                                               ident[0:HU, 0:HU])
                        ins.then_inc(at_psum, 1)
                    for b in range(G):
                        pe.wait_ge(at_ready, g * G + (b + 1))
                        for c in range(KC):
                            ins = pe.matmul(ps[b][0:HU, c * P:(c + 1) * P], a_t[:, b, c * HU:(c + 1) * HU],
                                            qv[:, b, D + c * P:D + (c + 1) * P], start=True, stop=True)
                        ins.then_inc(o_psum, 1)
                    pe.wait_ge(sel_t_ready, g + 1)
                    for b in range(G):
                        pe.wait_ge(o_ready, g * G + (b + 1))
                        for c in range(KC):
                            ins = pe.matmul(ps[b][:, c * P:(c + 1) * P], o_sel[0:HU, b, c, :],
                                            sel_t[:, b, c, :], start=True, stop=True)
                        ins.then_inc(mt_psum, 1)
                    for b in range(G):
                        pe.wait_ge(mt_ready, g * G + (b + 1))
                        for c in range(KC):
                            ins = pe.matmul(ps[b][:, 0:D], m_t[:, b, c, :], w_o_sb[:, c, :],
                                            start=(c == 0), stop=(c == KC - 1))
                        ins.then_inc(attn_psum, 1)
                    for b in range(G):
                        pe.wait_ge(yn_ready, g * G + (b + 1))
                        transposes(xn, b, ynt_psum)
                    pe.wait_ge(ctx_sq_ready, g + 1)
                    for b in range(G):
                        pe.wait_ge(ynt_ready, g * G + (b + 1))
                        for c in range(KC):
                            pe.matmul(ps[b][:, P:P + 1], ctx_sq[:, b, c, :], neg_half[:, 0:1],
                                      start=(c == 0), stop=(c == KC - 1))
                        for c in range(KC):
                            pe.matmul(ps[b][:, 0:P], ctx_t[:, b, c, :], xn_t[:, b, c, :],
                                      start=(c == 0), stop=False)
                        for c in range(KC):
                            ins = pe.matmul(ps[b][:, 0:P], neg_half[:, :], e_buf[:, b, c, :],
                                            start=False, stop=(c == KC - 1))
                        ins.then_inc(dist_psum, 1)

            @block.scalar
            def _(act):
                act.wait_ge(weights_in, 16 * 5)
                with act.Fori(0, NG) as g:
                    for b in range(G):
                        act.wait_ge(xnt_psum, g * G + (b + 1))
                        act.activation(xn_t[:, b, :, :].rearrange("p c n -> p (c n)"), ps[b][:, 0:D], ACT.Copy)\
                           .then_inc(xnt_ready, 1)
                    for b in range(G):
                        act.wait_ge(kt_psum, g * G + (b + 1))
                        for c in range(KC):
                            ins = act.activation(k_t[:, b, c, :], ps[b][:, c * P:(c + 1) * P], ACT.Identity,
                                                 bias=b_k_sb[:, c:c + 1])
                        ins.then_inc(kt_ready, 1)
                    act.wait_ge(centred, g + 1)
                    act.activation(c1, c1, ACT.Square).then_inc(squared, 1)
                    act.wait_ge(shifted, g + 1)
                    act.activation(c2, c2, ACT.Exp).then_inc(expd, 1)
                    act.wait_ge(prob_done, g + 1)
                    act.activation(c3, c2, ACT.Ln, bias=tiny[:, 0:1]).then_inc(logp_done, 1)
                    act.wait_ge(l2_in_done, g + 1)
                    act.activation(l2, mean_sq, ACT.Sqrt).then_inc(l2_done, 1)
                    for b in range(G):
                        act.wait_ge(max_ready, g * G + (b + 1))
                        for c in range(KC):
                            ins = act.activation(e_buf[0:HU, b, c, :], ps[b][0:HU, c * P:(c + 1) * P], ACT.Exp,
                                                 bias=neg_max[:, b, c:c + 1], accum_out=e_sum[:, b, c:c + 1])
                        ins.then_inc(e_ready, 1)
                    for b in range(G):
                        act.wait_ge(at_psum, g * G + (b + 1))
                        act.activation(a_t[:, b, :], ps[b][:, 0:KC * HU], ACT.Copy).then_inc(at_ready, 1)
                    for b in range(G):
                        act.wait_ge(mt_psum, g * G + (b + 1))
                        act.activation(m_t[:, b, :, :].rearrange("p c n -> p (c n)"), ps[b][:, 0:D], ACT.Copy)\
                           .then_inc(mt_ready, 1)
                    for b in range(G):
                        act.wait_ge(ynt_psum, g * G + (b + 1))
                        act.activation(xn_t[:, b, :, :].rearrange("p c n -> p (c n)"), ps[b][:, 0:D], ACT.Copy)
                        act.activation(e_buf[:, b, :, :].rearrange("p c n -> p (c n)"), ps[b][:, 0:D],
                                       ACT.Square).then_inc(ynt_ready, 1)
                    act.wait_ge(dist_stored, g * 16 + FREE)
                    for b in range(G):
                        act.wait_ge(dist_sq_ready, g * G + (b + 1))
                        act.activation(dist[:, b, :], dist[:, b, :], ACT.Sqrt, scale=-2.0).then_inc(dist_ready, 1)

            @block.vector
            def _(dve):
                dve.wait_ge(weights_in, 16 * 5)
                with dve.Fori(0, NG) as g:
                    dve.wait_ge(x_loaded, g * 32 + 32)
                    layer_norm(dve, g, lambda b: x_in[:, b, :], lambda b: xn[:, b, :],
                               stats_a, moments_a, rstd_a, xn_ready)
                    for b in range(G):
                        dve.wait_ge(qv_psum, g * G + (b + 1))
                        dve.tensor_tensor(qv[:, b, :], ps[b][:, :], b_qv_sb, ALU.add).then_inc(qv_ready, 1)
                    dve.wait_ge(qv_ready, g * G + G)
                    q = heads(qv[:, :, 0:D])
                    head_grid = lambda t: t.rearrange("p (g h) -> p g h", g=G)
                    dve.tensor_reduce(head_grid(sum_q), q, AX.X, ALU.add).then_inc(sum_q_done, 1)
                    dve.wait_ge(sum_q_done, g + 1)
                    dve.tensor_scalar(mean_q, sum_q, 1.0 / DK, None, ALU.mult).then_inc(mean_q_done, 1)
                    dve.tensor_reduce(head_grid(max_q), q, AX.X, ALU.max).then_inc(max_q_done, 1)
                    dve.wait_ge(squared, g + 1)
                    dve.tensor_reduce(head_grid(sum_sq), heads(c1), AX.X, ALU.add).then_inc(sum_sq_done, 1)
                    dve.wait_ge(expd, g + 1)
                    dve.tensor_reduce(head_grid(sum_e), heads(c2), AX.X, ALU.add).then_inc(sum_e_done, 1)
                    dve.wait_ge(sum_e_done, g + 1)
                    dve.reciprocal(rec_e, sum_e).then_inc(rec_e_done, 1)
                    dve.wait_ge(mean_q_done, g + 1)
                    dve.scalar_tensor_tensor(mean_sq, mean_q, float(DK), mean_q, ALU.mult, ALU.mult)\
                       .then_inc(score_step, 1)
                    dve.wait_ge(score_step, g * 3 + 1)
                    dve.wait_ge(sum_sq_done, g + 1)
                    dve.tensor_tensor(mean_sq, mean_sq, sum_sq, ALU.add).then_inc(l2_in_done, 1)
                    dve.wait_ge(l2_done, g + 1)
                    dve.scalar_tensor_tensor(score, sum_sq, 0.4 / (DK - 1), l2, ALU.mult, ALU.add)\
                       .then_inc(score_step, 1)
                    dve.wait_ge(plogp_done, g + 1)
                    dve.tensor_reduce(head_grid(sum_pl), heads(c3), AX.X, ALU.add).then_inc(score_step, 1)
                    dve.wait_ge(score_step, g * 3 + 3)
                    dve.scalar_tensor_tensor(score, sum_pl, -0.6, score, ALU.mult, ALU.add)\
                       .then_inc(score_ready, 1)
                    TS = 13
                    k = 0

                    def step(ins):
                        nonlocal k
                        ins.then_inc(top_step, 1)
                        k += 1
                        dve.wait_ge(top_step, g * TS + k)
                    dve.wait_ge(score_psum, g + 1)
                    step(dve.tensor_scalar(score_t, ps[0][:, 0:P], 0.5, None, ALU.mult))
                    step(dve.bn_stats(t_stats, score_t))
                    apart(dve)
                    dve.bn_aggr(t_mom, t_stats).then_inc(variance_ready, 1)
                    dve.wait_ge(variance_ready, g + 1)
                    step(dve.tensor_scalar(t_b, t_mom[:, 0:1], 1e-6, None, ALU.add))
                    step(dve.reciprocal(t_b, t_b))
                    dve.wait_ge(deviation_ready, g + 1)
                    step(dve.tensor_tensor(t_c, t_dev, t_b, ALU.mult))
                    step(dve.tensor_scalar(t_a, t_c, float(TOP), float(TOP), ALU.mult, ALU.min))
                    step(dve.tensor_scalar(t_b, t_a, float(MIN_TOP), MAGIC, ALU.max, ALU.add))
                    dve.tensor_scalar(factor, t_b, MAGIC, None, ALU.subtract).then_inc(factor_ready, 1)
                    apart(dve)
                    step(dve.max(top8[:, 0, :], score_t))
                    apart(dve)
                    step(dve.match_replace(score_u, top8[:, 0, :], score_t, -3e38))
                    apart(dve)
                    step(dve.max(top8[:, 1, :], score_u))
                    apart(dve)
                    dve.max_index(idx_u[:, 0, :], top8[:, 0, :], score_t)
                    step(dve.max_index(idx_u[:, 1, :], top8[:, 1, :], score_u))
                    step(dve.tensor_copy(idx_f, idx_u.rearrange("p a b -> p (a b)")))
                    dve.wait_ge(keep_psum, g + 1)
                    step(dve.tensor_scalar(kept, iota_small[:, :], ps[1][:, 0:1], None, ALU.is_lt))
                    assert k == TS
                    dve.scalar_tensor_tensor(idx1, idx_f[:, 0:TOP], 1.0, kept, ALU.add, ALU.mult)\
                       .then_inc(sem_idx1, 1)
                    dve.wait_ge(sem_idx1, g + 1)
                    dve.tensor_tensor(idx_rows, idx1.unsqueeze(1).to_broadcast([P, HEADS, TOP]),
                                      head_of_row[:, :].unsqueeze(2).to_broadcast([P, HEADS, TOP]), ALU.mult)\
                       .then_inc(idx_rows_ready, 1)
                    dve.wait_ge(idx_cols_psum, g + 1)
                    dve.tensor_copy(idx_cols, ps[7][0:HU, 0:KC * G].rearrange("p (c g) -> p c g", c=KC))\
                       .then_inc(idx_cols_ready, 1)
                    for b in range(G):
                        dve.wait_ge(idx_psum, g * G + (b + 1))
                        dve.tensor_scalar(sel[:, b, :], ps[b][:, 0:KC * HU], iota_p1[:, 0:1], None,
                                          ALU.is_equal).then_inc(sel_ready, 1)
                    dve.wait_ge(idx_cols_ready, g + 1)
                    for c in range(KC):
                        ins = dve.tensor_tensor(sel_t[:, :, c, :],
                                                iota_f1[0:HU, :].unsqueeze(1).to_broadcast([HU, G, P]),
                                                idx_cols[:, c, :].unsqueeze(2).to_broadcast([HU, G, P]),
                                                ALU.is_equal)
                    ins.then_inc(sel_t_ready, 1)
                    for b in range(G):
                        dve.wait_ge(qs_psum, g * G + (b + 1))
                        dve.tensor_tensor(q_sel[:, b, :], ps[b][:, 0:KC * HU],
                                          head_block[:, :, :, :].rearrange("p c h u -> p (c h u)"),
                                          ALU.mult).then_inc(qs_ready, 1)
                    for b in range(G):
                        dve.wait_ge(s_psum, g * G + (b + 1))
                        dve.tensor_reduce(neg_max[:, b, :], ps[b][0:HU, 0:D].rearrange("p (c n) -> p c n", c=KC),
                                          AX.X, ALU.max, negate=True).then_inc(max_ready, 1)
                    dve.wait_ge(e_ready, g * G + G)
                    dve.reciprocal(e_rec, e_sum).then_inc(e_rec_done, 1)
                    dve.wait_ge(e_rec_done, g + 1)
                    for b in range(G):
                        dve.wait_ge(o_psum, g * G + (b + 1))
                        for c in range(KC):
                            ins = dve.scalar_tensor_tensor(
                                o_sel[0:HU, b, c, :], ps[b][0:HU, c * P:(c + 1) * P], e_rec[:, b, c:c + 1],
                                head_block2[:, :, :].rearrange("p h d -> p (h d)"), ALU.mult, ALU.mult)
                        ins.then_inc(o_ready, 1)
                    dve.wait_ge(x_res_ready, g + 1)
                    for b in range(G):
                        dve.wait_ge(attn_psum, g * G + (b + 1))
                        dve.tensor_tensor(x_res[:, b, :], x_res[:, b, :], ps[b][:, 0:D], ALU.add)\
                           .then_inc(x1_ready, 1)
                    layer_norm(dve, g, lambda b: x_res[:, b, :], lambda b: xn[:, b, :],
                               stats_b, moments_b, rstd_b, yn_ready,
                               before_tile=lambda b: dve.wait_ge(x1_ready, g * G + (b + 1)))
                    dve.wait_ge(dist_stored, g * 16 + FREE)
                    for b in range(G):
                        dve.wait_ge(dist_psum, g * G + (b + 1))
                        dve.tensor_scalar(dist[:, b, :], ps[b][:, 0:P], ps[b][:, P:P + 1], 0.0,
                                          ALU.add, ALU.min).then_inc(dist_sq_ready, 1)
        next_phase()
        carve = carver()
        cost = carve(P + 1, P + 1, rows=B)
        upper = carve(P, P, rows=B)
        code = carve(P, P, dt=BF16, rows=B)
        junk = carve(P, 2, rows=B)
        upper_flat = upper.rearrange("p i j -> p (i j)")
        code_flat = code.rearrange("p i j -> p (i j)")
        TURNS = P // ROWS

        edge_made = sem("edge_made")
        cost_loaded = [sem(f"cost_loaded{c}") for c in range(TURNS)]
        sem_sign = sem("sign_done")
        upper_done, row_done = sem("upper_done"), sem("row_done", FREE)
        diff_done, is_up_done, code_done = sem("diff_done"), sem("is_up_done"), sem("code_done")
        left_done, gated_done, scan_done, path_step = (
            sem("left_done"), sem("gated_done"), sem("scan_done"), sem("path_step"))

        with nc.Block() as block:
            @block.sync
            def _(sp):
                for c in range(TURNS):
                    sp.dma_start(cost[:, 1 + c * ROWS:1 + (c + 1) * ROWS, 1:P + 1],
                                 dist_dram[:, c * ROWS:(c + 1) * ROWS, :]).then_inc(cost_loaded[c], 16)

            @block.gpsimd
            def _(pool):
                pool.memset(cost[:, 0, 1:P + 1], BIG).then_inc(edge_made, 1)
                pool.memset(cost[:, 1:P + 1, 0], BIG).then_inc(edge_made, 1)
                pool.memset(cost[:, 0, 0:1], 0.0).then_inc(edge_made, 1)
                pool.memset(codes[:, 0:1], 0.0).then_inc(edge_made, 1)
                pool.memset(codes[:, P:P + 1], 2.0 * P - 1).then_inc(edge_made, 1)
                with pool.Fori(0, TURNS) as t:
                    pool.wait_ge(row_done, t * ROWS + ROWS + FREE)
                    apart(pool)
                    rows = bass.ds(t * ROWS, ROWS)
                    pool.tensor_tensor(code[:, rows, :], cost[:, rows, 1:P + 1], cost[:, rows, 0:P],
                                       ALU.subtract).then_inc(diff_done, 1)
                    pool.wait_ge(is_up_done, t + 1)
                    apart(pool)
                    pool.tensor_tensor(code[:, rows, :], code[:, rows, :],
                                       iota_2j[0:B, :].unsqueeze(1).to_broadcast([B, ROWS, P]), ALU.add)\
                        .then_inc(code_done, 1)

            @block.scalar
            def _(act):
                with act.Fori(0, TURNS) as t:
                    flat = code_flat[:, bass.ds(t * ROWS * P, ROWS * P)]
                    act.wait_ge(diff_done, t + 1)
                    apart(act)
                    act.activation(flat, flat, ACT.Sign, scale=-1.0).then_inc(sem_sign, 1)
                    act.wait_ge(sem_sign, t + 1)
                    apart(act)
                    act.activation(flat, flat, ACT.Relu).then_inc(is_up_done, 1)

            @block.vector
            def _(dve):
                dve.wait_ge(edge_made, 5)
                for c in range(TURNS):
                    dve.wait_ge(cost_loaded[c], 16)
                with dve.Fori(0, TURNS) as t:
                    for r in range(ROWS):
                        i = t * ROWS + r
                        if r == 0:
                            dve.wait_ge(row_done, t * ROWS + FREE)
                        else:
                            dve.wait_ge(row_done, t * ROWS + r + FREE)
                        dve.tensor_tensor(upper[:, i, :], cost[:, i, 1:P + 1], cost[:, i, 0:P], ALU.min)\
                           .then_inc(upper_done, 1)
                        dve.wait_ge(upper_done, t * ROWS + (r + 1))
                        dve.tensor_tensor_scan(cost[:, i + 1, 1:P + 1], upper[:, i, :], cost[:, i + 1, 1:P + 1],
                                               BIG, ALU.min, ALU.add).then_inc(row_done, 1)
                dve.wait_ge(row_done, P + FREE)
                for h in range(4):
                    rows = slice(h * P // 4, (h + 1) * P // 4)
                    at = slice(h * P * P // 4, (h + 1) * P * P // 4)
                    dve.tensor_tensor(upper[:, rows, :], upper[:, rows, :],
                                      cost[:, 1 + h * P // 4:1 + (h + 1) * P // 4, 0:P], ALU.is_gt)\
                       .then_inc(left_done, 1)
                    dve.wait_ge(left_done, h + 1)
                    dve.wait_ge(code_done, (h + 1) * TURNS // 4)
                    dve.scalar_tensor_tensor(code_flat[:, at], upper_flat[:, at], 1.0, code_flat[:, at],
                                             ALU.is_lt, ALU.mult).then_inc(gated_done, 1)
                    dve.wait_ge(gated_done, h + 1)
                    dve.tensor_tensor_scan(upper_flat[:, at], upper_flat[:, at], code_flat[:, at],
                                           0.0, ALU.mult, ALU.add).then_inc(scan_done, 1)
                dve.wait_ge(scan_done, 4)

                def follow(i, before_it):
                    dve.wait_ge(path_step, before_it)
                    if not isinstance(i, int):
                        apart(dve)
                    dve.scalar_tensor_tensor(
                        junk, iota_256[0:B, :].rearrange("p (j t) -> p j t", t=2), codes[:, at_col(i + 1)],
                        upper[:, at_row(i), :].unsqueeze(2).to_broadcast([B, P, 2]),
                        ALU.is_equal, ALU.mult, accum_out=codes[:, at_col(i)]).then_inc(path_step, 1)

                def at_col(i):
                    return bass.ds(i, 1) if not isinstance(i, int) else slice(i, i + 1)

                def at_row(i):
                    return i
                for i in range(P - 1, P - 1 - (P - 1) % PATH_UNROLL, -1):
                    follow(i, P - 1 - i)
                done = (P - 1) % PATH_UNROLL
                with dve.Fori(0, (P - 1) // PATH_UNROLL) as t:
                    for k in range(PATH_UNROLL):
                        follow(P - 1 - done - k - t * PATH_UNROLL, t * PATH_UNROLL + (done + k))
                dve.wait_ge(path_step, P - 1)

        next_phase()
        carve = carver()
        w1_sb = carve(EXPERTS, KC, HID)
        w2_sb = carve(EXPERTS, HK, D)
        b1_sb = carve(EXPERTS, HID)
        g1_sb = carve(EXPERTS, HID)
        be1_sb = carve(EXPERTS, HID)
        b2_sb = carve(EXPERTS, D)
        ctx = carve(G, D)
        x2 = carve(G, D)
        xf = carve(G, D)
        xf_t = carve(G, KC, P)
        mask = carve(G, P)
        gate_sb = carve(KC, EXPERTS)
        logits = carve(G, EXPERTS)
        best = carve(G, EXPERTS)
        best_i = carve(G, EXPERTS, dt=U32)

        gate_in, moe_weights_in = sem("gate_in"), sem("moe_weights_in")
        ctx_in, x1_in = sem("ctx_in"), sem("x1_in")
        x2_stored, xf_stored = sem("x2_stored", FREE), sem("xf_stored", FREE)
        codes_psum, codes_ready = sem("codes_psum"), sem("codes_ready")
        mask_half, mask_ready = sem("mask_half"), sem("mask_ready")
        warp_psum, x2_ready = sem("warp_psum"), sem("x2_ready", FREE)
        stats_c, moments_c, rstd_c, xf_ready = sem("stats_c"), sem("moments_c"), sem("rstd_c"), sem("xf_ready", FREE)
        xft_psum, xft_ready = sem("xft_psum"), sem("xft_ready")
        logit_psum, logit_ready = sem("logit_psum"), sem("logit_ready", FREE)
        eps_c = sem("eps_c")
        best_ready, best_i_ready, top_ready = sem("best_ready"), sem("best_i_ready"), sem("top_ready")

        with nc.Block() as block:
            @block.sync
            def _(sp):
                sp.dma_start(gate_sb, gate_w.rearrange("(c p) e -> p c e", p=P)).then_inc(gate_in, 16)
                with sp.Fori(0, NG) as g:
                    seqs = bass.ds(g * G, G)
                    sp.wait_ge(x2_ready, g * G + FREE)
                    load_group(sp, ctx, ctx_rows, g, ctx_in)
                    sp.wait_ge(x2_stored, g * 16 + FREE)
                    sp.wait_ge(xf_ready, g * G + FREE)
                    load_group(sp, x2, x1_dram, g, x1_in)
                    sp.wait_ge(x2_ready, g * G + G + FREE)
                    sp.dma_start(x2_dram[seqs].rearrange("g p d -> p g d"), x2).then_inc(x2_stored, 16)
                    sp.wait_ge(xf_ready, g * G + G + FREE)
                    sp.dma_start(xn_dram[seqs].rearrange("g p d -> p g d"), xf).then_inc(xf_stored, 16)
                sp.wait_ge(x2_stored, 16 * NG + FREE)
                sp.wait_ge(xf_stored, 16 * NG + FREE)

            @block.gpsimd
            def _(pool):
                for t, src in ((b1_sb, b1), (g1_sb, ln1_g), (be1_sb, ln1_b), (b2_sb, b2)):
                    pool.dma_start(t, src.partition_broadcast(P)).then_inc(moe_weights_in, 16)
                for e in range(EXPERTS):
                    pool.dma_start(w1_sb[:, e, :, :], w1[e].rearrange("(c p) n -> p c n", p=P))\
                        .then_inc(moe_weights_in, 16)
                    pool.dma_start(w2_sb[:, e, :, :], w2[e].rearrange("(c p) n -> p c n", p=P))\
                        .then_inc(moe_weights_in, 16)
                with pool.Fori(0, NG) as g:
                    inverse_deviation(pool, g, moments_c, eps_c, rstd_c)
                pool.wait_ge(moe_weights_in, 16 * (4 + 2 * EXPERTS))

            @block.tensor
            def _(pe):
                pe.transpose(ps[0][:, 0:B], codes[:, 1:P + 1], ident[0:B, 0:B]).then_inc(codes_psum, 1)
                pe.transpose(ps[1][:, 0:B], codes[:, 0:P], ident[0:B, 0:B]).then_inc(codes_psum, 1)
                pe.wait_ge(gate_in, 16)
                pe.wait_ge(codes_ready, 2)
                with pe.Fori(0, NG) as g:
                    pe.wait_ge(ctx_in, g * 32 + 32)
                    pe.wait_ge(logit_ready, g * G + FREE)
                    for b in range(G):
                        pe.wait_ge(mask_ready, g * G + (b + 1))
                        pe.matmul(ps[b][:, 0:D], mask[:, b, :], ctx[:, b, :], start=True, stop=True)\
                          .then_inc(warp_psum, 1)
                    for b in range(G):
                        pe.wait_ge(xf_ready, g * G + (b + 1) + FREE)
                        for c in range(KC):
                            ins = pe.transpose(ps[b][:, c * P:(c + 1) * P], xf[:, b, c * P:(c + 1) * P],
                                               ident[:, :])
                        ins.then_inc(xft_psum, 1)
                    for b in range(G):
                        pe.wait_ge(xft_ready, g * G + (b + 1))
                        for c in range(KC):
                            ins = pe.matmul(ps[b][:, 0:EXPERTS], xf_t[:, b, c, :], gate_sb[:, c, :],
                                            start=(c == 0), stop=(c == KC - 1))
                        ins.then_inc(logit_psum, 1)

            @block.scalar
            def _(act):
                with act.Fori(0, NG) as g:
                    for b in range(G):
                        act.wait_ge(xft_psum, g * G + (b + 1))
                        act.activation(xf_t[:, b, :, :].rearrange("p c n -> p (c n)"), ps[b][:, 0:D], ACT.Copy)\
                           .then_inc(xft_ready, 1)

            @block.vector
            def _(dve):
                dve.wait_ge(codes_psum, 2)
                for k in range(2):
                    dve.tensor_copy(row_code[:, k, :], ps[k][:, 0:B]).then_inc(codes_ready, 1)
                dve.wait_ge(codes_ready, 2)
                odd = iota_256[:, :].rearrange("p (j t) -> p j t", t=2)[:, :, 0]
                with dve.Fori(0, NG) as g:
                    for b in range(G):
                        dve.tensor_scalar(mask[:, b, :], iota_2j[:, :], row_code[:, 0, bass.ds(g * G + b, 1)],
                                          None, ALU.is_lt).then_inc(mask_half, 1)
                    for b in range(G):
                        dve.wait_ge(mask_half, g * G + (b + 1))
                        dve.scalar_tensor_tensor(mask[:, b, :], odd, row_code[:, 1, bass.ds(g * G + b, 1)],
                                                 mask[:, b, :], ALU.is_ge, ALU.mult).then_inc(mask_ready, 1)
                    dve.wait_ge(x1_in, g * 32 + 32)
                    for b in range(G):
                        dve.wait_ge(warp_psum, g * G + (b + 1))
                        dve.tensor_tensor(x2[:, b, :], x2[:, b, :], ps[b][:, 0:D], ALU.add).then_inc(x2_ready, 1)
                    dve.wait_ge(xf_stored, g * 16 + FREE)
                    layer_norm(dve, g, lambda b: x2[:, b, :], lambda b: xf[:, b, :],
                               stats_c, moments_c, rstd_c, xf_ready,
                               before_tile=lambda b: dve.wait_ge(x2_ready, g * G + (b + 1) + FREE))
                    for b in range(G):
                        dve.wait_ge(logit_psum, g * G + (b + 1))
                        dve.tensor_copy(logits[:, b, :], ps[b][:, 0:EXPERTS]).then_inc(logit_ready, 1)
                    for b in range(G):
                        dve.wait_ge(logit_ready, g * G + (b + 1) + FREE)
                        apart(dve)
                        dve.max(best[:, b, :], logits[:, b, :]).then_inc(best_ready, 1)
                    for b in range(G):
                        dve.wait_ge(best_ready, g * G + (b + 1))
                        apart(dve)
                        dve.max_index(best_i[:, b, :], best[:, b, :], logits[:, b, :]).then_inc(best_i_ready, 1)
                    dve.wait_ge(best_i_ready, g * G + G)
                    dve.tensor_copy(top_val[:, bass.ds(g * G, G), :], best[:, :, 0:2]).then_inc(top_ready, 1)
                    dve.tensor_copy(top_exp[:, bass.ds(g * G, G), :], best_i[:, :, 0:2]).then_inc(top_ready, 1)
                dve.wait_ge(top_ready, 2 * NG)

        next_phase()
        hot = [carve(B, EXPERTS, dt=BF16) for _ in range(2)]
        hot_both = carve(B, EXPERTS, dt=BF16)
        total = ctx.rearrange("p g d -> p (g d)")[:, 0:EXPERTS * B].rearrange("p (e t) -> p e t", t=B)
        upto = ctx.rearrange("p g d -> p (g d)")[:, 1024:1024 + EXPERTS * B].rearrange("p (e t) -> p e t", t=B)
        grid = x2.rearrange("p g d -> p (g d)")[:, 0:EXPERTS * B].rearrange("p (t e) -> p t e", e=EXPERTS)
        picked = x2.rearrange("p g d -> p (g d)")[:, 1024:1024 + EXPERTS * B].rearrange(
            "p (t e) -> p t e", e=EXPERTS)
        starts = carve(EXPERTS)
        count = carve(EXPERTS)
        tiles = carve(EXPERTS)
        tile_end = carve(EXPERTS)
        base = carve(EXPERTS)
        tile_f = carve(NS)
        gap = carve(B)
        ratio = carve(B)
        route_step = sem("route_step")
        hot_ready, rank_psum, gap_ready, ratio_ready = (
            sem("hot_ready"), sem("rank_psum"), sem("gap_ready"), sem("ratio_ready"))

        with nc.Block() as block:
            @block.tensor
            def _(pe):
                pe.wait_ge(hot_ready, 1)
                flat = hot_both.rearrange("p t e -> p (t e)")
                pe.matmul(ps[0][:, 0:B * EXPERTS], before[:, :], flat, start=True, stop=True)\
                  .then_inc(rank_psum, 1)
                pe.matmul(ps[1][:, 0:B * EXPERTS], ones_bf[:, :], flat, start=True, stop=True)\
                  .then_inc(rank_psum, 1)

            @block.scalar
            def _(act):
                act.wait_ge(gap_ready, 1)
                act.activation(ratio, gap, ACT.Exp).then_inc(ratio_ready, 1)

            @block.vector
            def _(dve):
                n = 0

                def step(ins):
                    nonlocal n
                    ins.then_inc(route_step, 1)
                    n += 1
                    dve.wait_ge(route_step, n)
                for k in range(2):
                    step(dve.tensor_tensor(hot[k], iota_small[:, 0:EXPERTS].unsqueeze(1).to_broadcast([P, B, EXPERTS]),
                                           top_exp[:, :, k].unsqueeze(2).to_broadcast([P, B, EXPERTS]),
                                           ALU.is_equal))
                dve.tensor_tensor(hot_both, hot[0], hot[1], ALU.add).then_inc(hot_ready, 1)
                dve.tensor_tensor(gap, top_val[:, :, 1], top_val[:, :, 0], ALU.subtract).then_inc(gap_ready, 1)
                dve.wait_ge(rank_psum, 2)
                step(dve.tensor_copy(total, ps[1][:, 0:B * EXPERTS].rearrange("p (t e) -> p e t", e=EXPERTS)))
                flat_total, flat_upto = (t.rearrange("p e t -> p (e t)") for t in (total, upto))
                step(dve.tensor_tensor_scan(flat_upto, ones8[:, 0:1].to_broadcast([P, EXPERTS * B]),
                                            flat_total, 0.0, ALU.mult, ALU.add))
                step(dve.memset(starts[:, 0:1], 0.0))
                step(dve.tensor_copy(starts[:, 1:EXPERTS], upto[:, 0:EXPERTS - 1, B - 1]))
                step(dve.tensor_tensor(count, upto[:, :, B - 1], starts, ALU.subtract))
                step(dve.tensor_scalar(tiles, count, 1.0 / P, (P - 1) / (2.0 * P), ALU.mult, ALU.add))
                step(dve.tensor_scalar(tiles, tiles, MAGIC, None, ALU.add))
                step(dve.tensor_scalar(tiles, tiles, MAGIC, None, ALU.subtract))
                step(dve.tensor_tensor_scan(tile_end, ones8[:, :], tiles, 0.0, ALU.mult, ALU.add))
                step(dve.tensor_tensor(base, tile_end, tiles, ALU.subtract))
                step(dve.scalar_tensor_tensor(base, base, float(P), starts, ALU.mult, ALU.subtract))
                step(dve.tensor_tensor(upto, upto, total, ALU.subtract))
                step(dve.tensor_tensor(upto, upto, base.unsqueeze(2).to_broadcast([P, EXPERTS, B]), ALU.add))
                step(dve.tensor_tensor(grid, ps[0][:, 0:B * EXPERTS].rearrange("p (t e) -> p t e", e=EXPERTS),
                                       upto.rearrange("p e t -> p t e"), ALU.add))
                for k in range(2):
                    step(dve.tensor_tensor(picked, grid, hot[k], ALU.mult))
                    step(dve.tensor_reduce(slot_f[:, :, k], picked, AX.X, ALU.add))
                step(dve.tensor_copy(slot_i[:, :, :], slot_f[:, :, :]))
                step(dve.tensor_scalar(tile_f, iota_slot[:, :], tile_end[:, 0:1], None, ALU.is_ge))
                for e in range(1, EXPERTS):
                    step(dve.scalar_tensor_tensor(tile_f, iota_slot[:, :], tile_end[:, e:e + 1], tile_f,
                                                  ALU.is_ge, ALU.add))
                step(dve.tensor_scalar(tile_f, tile_f, EXPERTS - 1.0, None, ALU.min))
                step(dve.tensor_copy(tile_expert[:, :], tile_f))
                dve.wait_ge(ratio_ready, 1)
                step(dve.tensor_scalar(gap, ratio, 1.0, None, ALU.add))
                step(dve.reciprocal(pair_w[:, 0, :], gap))
                step(dve.tensor_tensor(pair_w[:, 1, :], ratio, pair_w[:, 0, :], ALU.mult))

        next_phase()
        slot_now = [sb(f"slot_now{k}", [P, G], I32) for k in range(2)]
        tok_in = [sem(f"tok_in{b}") for b in range(G)]
        tok_out = [sem(f"tok_out{b}") for b in range(G)]
        slot_copied = sem("slot_copied")
        with nc.Block() as block:
            @block.sync
            def _(sp):
                def load_tokens(g, first=False):
                    for b in range(G):
                        if not first:
                            sp.wait_ge(tok_out[b], g * 32)
                        sp.dma_start(xf[:, b, :], xn_dram[bass.ds(g * G + b, 1)].rearrange("g p d -> p (g d)"))\
                          .then_inc(tok_in[b], 16)
                load_tokens(0, first=True)
                with sp.Fori(1, NG) as g:
                    load_tokens(g)

            @block.gpsimd
            def _(pool):
                def scatter_tokens(g, first=False):
                    for b in range(G):
                        if not first:
                            pool.wait_ge(tok_out[b], g * 32)
                        for k in range(2):
                            pool.tensor_copy(slot_now[k][:, b:b + 1], slot_i[:, bass.ds(g * G + b, 1), k])\
                                .then_inc(slot_copied, 1)
                    for b in range(G):
                        pool.wait_ge(slot_copied, g * 2 * G + 2 * (b + 1))
                        pool.wait_ge(tok_in[b], g * 16 + 16)
                        apart(pool)
                        for k in range(2):
                            pool.indirect_dma_start(
                                out=slots_in[:, :],
                                out_offset=bass.IndirectOffsetOnAxis(ap=slot_now[k][:, b:b + 1], axis=0),
                                in_=xf[:, b, :], in_offset=None).then_inc(tok_out[b], 16)
                scatter_tokens(0, first=True)
                with pool.Fori(1, NG) as g:
                    scatter_tokens(g)
                for b in range(G):
                    pool.wait_ge(tok_out[b], 32 * NG)

        next_phase()
        U = MOE_UNROLL
        NT = NS // U
        at0 = 2 * EXPERTS * KC * HID + 3 * EXPERTS * HID + EXPERTS * D
        carve = carver()
        carve(at0)
        xs = carve(U, D)
        xs_t = carve(U, KC, P)
        h = carve(U, HID)
        act_h = carve(U, HID)
        h_t = carve(U, HK, P)
        y = carve(U, D)
        m_stats = carve(U, 6)
        m_mom = carve(U, 2)
        m_rstd = carve(U)
        xs_in = [sem(f"xs_in{u}") for u in range(U)]
        y_out = [sem(f"y_out{u}", FREE) for u in range(U)]
        xst_psum, xst_ready, h_psum, h_ready = (
            sem("xst_psum"), sem("xst_ready"), sem("h_psum"), sem("h_ready"))
        m_stats_done, m_mom_done, m_eps_done, m_rstd_done = (
            sem("m_stats_done"), sem("m_mom_done"), sem("m_eps_done"), sem("m_rstd_done"))
        h_scaled, h_normed, act_ready = sem("h_scaled"), sem("h_normed"), sem("act_ready")
        ht_psum, ht_ready, y_psum, y_ready = sem("ht_psum"), sem("ht_ready"), sem("y_psum"), sem("y_ready", FREE)

        def expert_of(eng, n, u):
            return eng.value_load(tile_expert[0:1, bass.ds(n * U + u, 1)], min_val=0, max_val=EXPERTS - 1)

        def pick(t, e):
            return t[:, bass.ds(e, 1)]

        with nc.Block() as block:
            @block.sync
            def _(sp):
                def load(n):
                    for u in range(U):
                        sp.dma_start(xs[:, u, :], slots_in[bass.ds(n * (U * P) + u * P, P), :])\
                          .then_inc(xs_in[u], 16)
                load(0)
                with sp.Fori(1, NT) as n:
                    sp.wait_ge(xst_psum, n * U)
                    load(n)
                    for u in range(U):
                        sp.wait_ge(y_ready, (n - 1) * U + (u + 1) + FREE)
                        sp.dma_start(slots_out[bass.ds((n - 1) * (U * P) + u * P, P), :], y[:, u, :])\
                          .then_inc(y_out[u], 16)
                for u in range(U):
                    sp.wait_ge(y_ready, (NT - 1) * U + (u + 1) + FREE)
                    sp.dma_start(slots_out[((NT - 1) * U + u) * P:((NT - 1) * U + u + 1) * P, :], y[:, u, :])\
                      .then_inc(y_out[u], 16)
                for u in range(U):
                    sp.wait_ge(y_out[u], 16 * NT + FREE)

            @block.gpsimd
            def _(pool):
                with pool.Fori(0, NT) as n:
                    pool.wait_ge(m_mom_done, n * U + U)
                    apart(pool)
                    pool.tensor_scalar(m_rstd, m_mom[:, :, 1], EPS, None, ALU.add).then_inc(m_eps_done, 1)
                    pool.wait_ge(m_eps_done, n + 1)
                    pool.tensor_tensor(m_rstd, m_rstd, exponents[:, 0:U], ALU.pow).then_inc(m_rstd_done, 1)

            @block.tensor
            def _(pe):
                def up(n, first=False):
                    if not first:
                        pe.wait_ge(h_ready, n * U)
                    for u in range(U):
                        pe.wait_ge(xs_in[u], n * 16 + 16)
                        for c in range(KC):
                            ins = pe.transpose(ps[u][:, c * P:(c + 1) * P], xs[:, u, c * P:(c + 1) * P],
                                               ident[:, :])
                        ins.then_inc(xst_psum, 1)
                    for u in range(U):
                        e = expert_of(pe, n, u)
                        pe.wait_ge(xst_ready, n * U + (u + 1))
                        for c in range(KC):
                            ins = pe.matmul(ps[u][:, :], xs_t[:, u, c, :],
                                            pick(w1_sb, e)[:, :, c, :].rearrange("p e n -> p (e n)"),
                                            start=(c == 0), stop=(c == KC - 1))
                        ins.then_inc(h_psum, 1)

                def down(n):
                    for u in range(U):
                        pe.wait_ge(act_ready, n * U + (u + 1))
                        if u == 0:
                            pe.wait_ge(y_ready, n * U + FREE)
                        for c in range(HK):
                            ins = pe.transpose(ps[4 + u][:, c * P:(c + 1) * P], act_h[:, u, c * P:(c + 1) * P],
                                               ident[:, :])
                        ins.then_inc(ht_psum, 1)
                    for u in range(U):
                        e = expert_of(pe, n, u)
                        pe.wait_ge(ht_ready, n * U + (u + 1))
                        for c in range(HK):
                            ins = pe.matmul(ps[4 + u][:, 0:D], h_t[:, u, c, :],
                                            pick(w2_sb, e)[:, :, c, :].rearrange("p e n -> p (e n)"),
                                            start=(c == 0), stop=(c == HK - 1))
                        ins.then_inc(y_psum, 1)
                up(0, first=True)
                with pe.Fori(1, NT) as n:
                    up(n)
                    down(n - 1)
                down(NT - 1)

            @block.scalar
            def _(act):
                def up(n):
                    for u in range(U):
                        act.wait_ge(xst_psum, n * U + (u + 1))
                        act.activation(xs_t[:, u, :, :].rearrange("p c n -> p (c n)"), ps[u][:, 0:D], ACT.Copy)\
                           .then_inc(xst_ready, 1)

                def gelus(n):
                    for u in range(U):
                        act.wait_ge(h_normed, n * U + (u + 1))
                        act.activation(act_h[:, u, :], h[:, u, :], ACT.Gelu).then_inc(act_ready, 1)

                def down(n):
                    for u in range(U):
                        act.wait_ge(ht_psum, n * U + (u + 1))
                        act.activation(h_t[:, u, :, :].rearrange("p c n -> p (c n)"), ps[4 + u][:, :], ACT.Copy)\
                           .then_inc(ht_ready, 1)
                up(0)
                gelus(0)
                with act.Fori(1, NT) as n:
                    up(n)
                    down(n - 1)
                    gelus(n)
                down(NT - 1)

            @block.vector
            def _(dve):
                def up(n):
                    for u in range(U):
                        e = expert_of(dve, n, u)
                        dve.wait_ge(h_psum, n * U + (u + 1))
                        dve.tensor_tensor(h[:, u, :].unsqueeze(1), ps[u][:, :].unsqueeze(1), pick(b1_sb, e), ALU.add)\
                           .then_inc(h_ready, 1)
                    for u in range(U):
                        dve.wait_ge(h_ready, n * U + (u + 1))
                        dve.bn_stats(m_stats[:, u, :], h[:, u, :]).then_inc(m_stats_done, 1)
                    for u in range(U):
                        dve.wait_ge(m_stats_done, n * U + (u + 1))
                        apart(dve)
                        dve.bn_aggr(m_mom[:, u, :], m_stats[:, u, :]).then_inc(m_mom_done, 1)
                    for u in range(U):
                        e = expert_of(dve, n, u)
                        dve.wait_ge(m_mom_done, n * U + (u + 1))
                        dve.scalar_tensor_tensor(h[:, u, :].unsqueeze(1), h[:, u, :].unsqueeze(1),
                                                 m_mom[:, u, 0:1], pick(g1_sb, e), ALU.subtract, ALU.mult)\
                           .then_inc(h_scaled, 1)
                    dve.wait_ge(m_rstd_done, n + 1)
                    apart(dve)
                    for u in range(U):
                        e = expert_of(dve, n, u)
                        dve.wait_ge(h_scaled, n * U + (u + 1))
                        dve.scalar_tensor_tensor(h[:, u, :].unsqueeze(1), h[:, u, :].unsqueeze(1),
                                                 m_rstd[:, u:u + 1], pick(be1_sb, e), ALU.mult, ALU.add)\
                           .then_inc(h_normed, 1)

                def down(n):
                    for u in range(U):
                        e = expert_of(dve, n, u)
                        dve.wait_ge(y_psum, n * U + (u + 1))
                        dve.wait_ge(y_out[u], n * 16 + FREE)
                        dve.tensor_tensor(y[:, u, :].unsqueeze(1), ps[4 + u][:, 0:D].unsqueeze(1), pick(b2_sb, e),
                                          ALU.add).then_inc(y_ready, 1)
                up(0)
                with dve.Fori(1, NT) as n:
                    dve.wait_ge(act_ready, n * U)
                    apart(dve)
                    up(n)
                    down(n - 1)
                down(NT - 1)

        next_phase()
        carve = carver()
        y0 = carve(G, D)
        y1 = carve(G, D)
        res = carve(G, D)
        xfc = carve(G, D)
        z = carve(G, D)
        g_sb = carve(D)
        b_sb = carve(D)
        ln_in, res_in, xfc_in = sem("ln_in"), sem("res_in"), sem("xfc_in")
        y0_in = [sem(f"y0_in{b}") for b in range(G)]
        y1_in = [sem(f"y1_in{b}") for b in range(G)]
        slot_copied2 = sem("slot_copied2")
        eps_d = sem("eps_d")
        mix0, mix_sum = sem("mix0", FREE), sem("mix_sum")
        stats_d, moments_d, rstd_d, z_ready = sem("stats_d"), sem("moments_d"), sem("rstd_d"), sem("z_ready", FREE)
        res_ready, z_scaled, out_ready, out_stored = (
            sem("res_ready"), sem("z_scaled"), sem("out_ready", FREE), sem("out_stored", FREE))
        with nc.Block() as block:
            @block.sync
            def _(sp):
                sp.dma_start(g_sb, ln_g.partition_broadcast(P)).then_inc(ln_in, 16)
                sp.dma_start(b_sb, ln_b.partition_broadcast(P)).then_inc(ln_in, 16)
                with sp.Fori(0, NG) as g:
                    seqs = bass.ds(g * G, G)
                    sp.wait_ge(mix0, g * G + FREE)
                    load_group(sp, xfc, xn_dram, g, xfc_in)
                    sp.wait_ge(out_ready, g + FREE)
                    load_group(sp, res, x2_dram, g, res_in)
                    sp.wait_ge(out_ready, g + 1 + FREE)
                    sp.dma_start(out[seqs].rearrange("g p d -> p g d"), z).then_inc(out_stored, 16)
                sp.wait_ge(out_stored, 16 * NG + FREE)

            @block.gpsimd
            def _(pool):
                pool.wait_ge(ln_in, 32)
                def gather_and_scale(g, first=False):
                    for b in range(G):
                        if not first:
                            pool.wait_ge(y0_in[b], g * 16)
                            pool.wait_ge(y1_in[b], g * 16)
                        for k in range(2):
                            pool.tensor_copy(slot_now[k][:, b:b + 1], slot_i[:, bass.ds(g * G + b, 1), k])\
                                .then_inc(slot_copied2, 1)
                    for b in range(G):
                        pool.wait_ge(slot_copied2, g * 2 * G + 2 * (b + 1))
                        pool.wait_ge(z_ready, g * G + FREE)
                        apart(pool)
                        for yk, done, k in ((y0, y0_in, 0), (y1, y1_in, 1)):
                            pool.indirect_dma_start(
                                out=yk[:, b, :], out_offset=None, in_=slots_out[:, :],
                                in_offset=bass.IndirectOffsetOnAxis(ap=slot_now[k][:, b:b + 1], axis=0))\
                                .then_inc(done[b], 16)
                    pool.wait_ge(res_in, g * 32 + 32)
                    pool.tensor_tensor(res, res, b_sb.unsqueeze(1).to_broadcast([P, G, D]), ALU.add)\
                        .then_inc(res_ready, 1)
                    inverse_deviation(pool, g, moments_d, eps_d, rstd_d)
                    pool.wait_ge(z_ready, g * G + G + FREE)
                    pool.tensor_tensor(z, z, g_sb.unsqueeze(1).to_broadcast([P, G, D]), ALU.mult)\
                        .then_inc(z_scaled, 1)
                gather_and_scale(0, first=True)
                with pool.Fori(1, NG) as g:
                    gather_and_scale(g)

            @block.vector
            def _(dve):
                with dve.Fori(0, NG) as g:
                    dve.wait_ge(xfc_in, g * 32 + 32)
                    for b in range(G):
                        dve.wait_ge(y0_in[b], g * 16 + 16)
                        dve.scalar_tensor_tensor(y0[:, b, :], y0[:, b, :], pair_w[:, 0, bass.ds(g * G + b, 1)],
                                                 xfc[:, b, :], ALU.mult, ALU.add).then_inc(mix0, 1)
                    for b in range(G):
                        dve.wait_ge(y1_in[b], g * 16 + 16)
                        dve.wait_ge(mix0, g * G + (b + 1) + FREE)
                        dve.scalar_tensor_tensor(y1[:, b, :], y1[:, b, :], pair_w[:, 1, bass.ds(g * G + b, 1)],
                                                 y0[:, b, :], ALU.mult, ALU.add).then_inc(mix_sum, 1)
                    dve.wait_ge(out_stored, g * 16 + FREE)
                    layer_norm(dve, g, lambda b: y1[:, b, :], lambda b: z[:, b, :],
                               stats_d, moments_d, rstd_d, z_ready,
                               before_tile=lambda b: dve.wait_ge(mix_sum, g * G + (b + 1)))
                    dve.wait_ge(z_ready, g * G + G + FREE)
                    dve.wait_ge(z_scaled, g + 1)
                    dve.wait_ge(res_ready, g + 1)
                    dve.tensor_tensor(z, z, res, ALU.add).then_inc(out_ready, 1)


def kernel(**inputs):
    import numpy as np
    import concourse.bacc as bacc
    from concourse import mybir as mb
    from concourse.bass_utils import run_bass_kernel_spmd

    a = {k: np.asarray(v) for k, v in inputs.items()}
    lay = np.ascontiguousarray
    arrays = {
        "x": a["x"],
        "ctx_rows": a["ctx_1024"],
        "ctx_cols": lay(a["ctx_1024"].transpose(0, 2, 1)),
        "w_qkv": lay(np.concatenate([a["L0_attn_wq"].T, a["L0_attn_wv"].T, a["L0_attn_wk"].T], axis=1)),
        "b_qv": lay(np.concatenate([a["L0_attn_bq"], a["L0_attn_bv"]])),
        "b_k": a["L0_attn_bk"],
        "w_o": lay(a["L0_attn_wo"].T),
        "b_o": a["L0_attn_bo"],
        "gate_w": a["L0_ffn_gate_w"],
        "w1": a["L0_ffn_w1"],
        "b1": a["L0_ffn_b1"],
        "ln1_g": a["L0_ffn_ln1_g"],
        "ln1_b": a["L0_ffn_ln1_b"],
        "w2": a["L0_ffn_w2"],
        "b2": a["L0_ffn_b2"],
        "ln_g": a["L0_ffn_ln_g"],
        "ln_b": a["L0_ffn_ln_b"],
    }
    nc = bacc.Bacc("TRN2", target_bir_lowering=False, num_devices=1)
    aps = [nc.dram_tensor(f"{k}_dram", v.shape, mb.dt.from_np(v.dtype), kind="ExternalInput").ap()
           for k, v in arrays.items()]
    out = nc.dram_tensor("out_dram", a["x"].shape, mb.dt.float32, kind="ExternalOutput").ap()
    decoder_layer(nc, *aps, out)
    r = run_bass_kernel_spmd(nc, [{f"{k}_dram": v for k, v in arrays.items()}], core_ids=[0])
    return r.results[0]["out_dram"]
```

```python
from contextlib import ExitStack

import concourse.bass as bass
from concourse import mybir

F32 = mybir.dt.float32
BF16 = mybir.dt.bfloat16
I32 = mybir.dt.int32
U32 = mybir.dt.uint32
ALU = mybir.AluOpType
ACT = mybir.ActivationFunctionType
AX = mybir.AxisListType

P = 128
D = 256
KC = D // P
HEADS = 16
DK = D // HEADS
HC = HEADS // KC
ROW = D + 2
TOP = 10
MIN_TOP = 3
HU = HC * TOP
G = 8
EXPERTS = 8
HID = 512
HK = HID // P
EPS = 1e-5
BIG = 1e30
MAGIC = 12582912.0
MOE_UNROLL = 4
PATH_UNROLL = 14
FREE = 16
ROWS = 16


def decoder_layer(nc, x, ctx_rows, ctx_cols, w_qkv, b_qv, b_k, w_o, b_o, gate_w, w1, b1, ln1_g, ln1_b,
                  w2, b2, ln_g, ln_b, out):
    B = x.shape[0]
    NG = B // G
    NS = 2 * B + EXPERTS
    NS += -NS % (2 * MOE_UNROLL)
    T = B * P
    REGION = T + P
    NULL_TILE = EXPERTS * REGION // P
    GATE_STEPS = 19
    x1_dram = nc.dram_tensor("x1_scratch", [B, P, D], F32)
    dist_dram = nc.dram_tensor("dist_scratch", [B, P, P], F32)
    x2_dram = nc.dram_tensor("x2_scratch", [B, P, D], F32)
    slots = nc.dram_tensor("slots_scratch", [EXPERTS * REGION + P, ROW], F32)
    pair_out = nc.dram_tensor("pair_out_scratch", [2 * T, D], F32)

    es = ExitStack()
    with es:
        def sb(name, shape, dt=F32):
            return es.enter_context(nc.sbuf_tensor(name, shape, dt))

        phase = []

        def sem(name, start=0):
            phase.append(nc.alloc_semaphore(name=name))
            if start:
                nc.gpsimd.sem_inc(phase[-1], start)
            return phase[-1]

        def next_phase():
            nc.clear_and_free_semaphores(phase)
            nc.all_engine_barrier()
            phase.clear()

        def apart(eng):
            eng.nop(nofuse=True)

        ps = [es.enter_context(nc.psum_tensor(f"bank{i}", [P, 512], F32)) for i in range(8)]

        ident = sb("ident", [P, P])
        iota_f1 = sb("iota_f1", [P, P])
        iota_p1 = sb("iota_p1", [P, 1])
        iota_2j = sb("iota_2j", [P, P])
        iota_256 = sb("iota_256", [P, 2 * P])
        iota_small = sb("iota_small", [P, TOP])
        iota_slot = sb("iota_slot", [P, NS])
        head_block = sb("head_block", [P, KC, HC, TOP])
        head_block2 = sb("head_block2", [HU, HC, DK])
        seq_rows = sb("seq_rows", [P, G, P], BF16)
        first_head = sb("first_head", [P, P], BF16)
        head_of_row = sb("head_of_row", [P, HEADS])
        neg_half = sb("neg_half", [P, P])
        before = sb("before", [P, P], BF16)
        ones_bf = sb("ones_bf", [P, P], BF16)
        tiny = sb("tiny", [P, 1])
        ones8 = sb("ones8", [P, EXPERTS])
        codes = sb("codes", [B, P + 1])
        row_code = sb("row_code", [P, 2, B])
        xf_scale = sb("xf_scale", [P, 2, B])
        tile_expert = sb("tile_expert", [P, NS], I32)
        tile_addr = sb("tile_addr", [P, NS], I32)
        from_8 = sb("from_8", [P, G, EXPERTS])
        stats = sb("stats", [P, G, 6])
        moments = sb("moments", [P, G, 2])
        rstd = sb("rstd", [P, G])
        exponents = sb("exponents", [P, G + 1])

        ARENA = 45200
        arena = sb("arena", [P, ARENA])

        def carver():
            at = [0]

            def carve(*shape, dt=F32, rows=P):
                n = 1
                for s in shape:
                    n *= s
                words = n if dt != BF16 else (n + 1) // 2
                v = arena[0:rows, at[0]:at[0] + words]
                at[0] += words
                assert at[0] <= ARENA, at[0]
                if dt != F32:
                    v = v.bitcast(dt)
                if len(shape) > 1:
                    names = "abcd"[:len(shape)]
                    v = v.rearrange(f"p ({' '.join(names)}) -> p {' '.join(names)}",
                                    **dict(zip(names, shape)))
                return v
            carve.at = lambda: at[0]
            return carve

        made = sem("const_made")
        with nc.Block() as block:
            @block.gpsimd
            def _(pool):
                n = 0

                def step(ins):
                    nonlocal n
                    ins.then_inc(made, 1)
                    n += 1
                    pool.wait_ge(made, n)

                def iota(t, pattern, base, mult):
                    step(pool.iota(t, pattern=pattern, base=base, channel_multiplier=mult,
                                   allow_small_or_imprecise_dtypes=True))

                def keep(t, pattern, base, mult, op, fill):
                    step(pool.affine_select(out=t, in_=t, pattern=pattern, compare_op=op, fill=fill,
                                            base=base, channel_multiplier=mult))

                iota(iota_slot[:, :], [[1, NS]], 0, 0)
                iota(iota_f1[:, :], [[1, P]], 1, 0)
                iota(iota_p1[:, :], [[1, 1]], 1, 1)
                iota(iota_2j[:, :], [[2, P]], 0, 0)
                iota(iota_256[:, :], [[1, 2 * P]], 1, 0)
                iota(iota_small[:, :], [[1, TOP]], 0, 0)
                iota(from_8[:, :, :], [[0, G], [-1, EXPERTS]], EXPERTS, 0)
                step(pool.memset(ident[:, :], 0.0))
                keep(ident[:, :], [[-1, P]], 0, 1, ALU.not_equal, 1.0)
                step(pool.memset(head_block[:, :, :, :], float(DK) ** -0.5))
                for c in range(KC):
                    v = head_block[:, c, :, :]
                    keep(v, [[-DK, HC], [0, TOP]], 0, 1, ALU.is_ge, 0.0)
                    keep(v, [[DK, HC], [0, TOP]], DK - 1, -1, ALU.is_ge, 0.0)
                step(pool.memset(head_block2[:, :, :], 1.0))
                keep(head_block2[:, :, :], [[-TOP, HC], [0, DK]], 0, 1, ALU.is_ge, 0.0)
                keep(head_block2[:, :, :], [[TOP, HC], [0, DK]], TOP - 1, -1, ALU.is_ge, 0.0)
                step(pool.memset(seq_rows[:, :, :], 1.0))
                keep(seq_rows[:, :, :], [[-HEADS, G], [0, P]], 0, 1, ALU.is_ge, 0.0)
                keep(seq_rows[:, :, :], [[HEADS, G], [0, P]], HEADS - 1, -1, ALU.is_ge, 0.0)
                step(pool.memset(first_head[:, :], 1.0))
                keep(first_head[:, :], [[-HEADS, G], [0, HEADS]], 0, 1, ALU.is_equal, 0.0)
                step(pool.memset(before[:, :], 1.0))
                keep(before[:, :], [[1, P]], 0, -1, ALU.is_gt, 0.0)
                step(pool.memset(ones_bf[:, :], 1.0))
                step(pool.memset(neg_half[:, :], -0.5))
                step(pool.memset(tiny[:, :], 1e-9))
                step(pool.memset(ones8[:, :], 1.0))
                step(pool.memset(exponents[:, 0:G], -0.5))
                step(pool.memset(exponents[:, G:G + 1], 0.5))

            @block.vector
            def _(dve):
                dve.wait_ge(made, 9)
                dve.tensor_reduce(head_of_row[:, :], ident[:, :].rearrange("p (s h) -> p h s", h=HEADS),
                                  AX.X, ALU.max).then_inc(sem("head_of_row_made"), 1)

        next_phase()
        carve = carver()
        x_in = carve(G, D)
        x_res = carve(G, D)
        xn = carve(G, D)
        xn_t = carve(G, KC, P)
        qv = carve(G, 2 * D)
        k_t = carve(G, KC, P)
        c1 = carve(G, D)
        c2 = carve(G, D)
        c3 = carve(G, D)
        sel = carve(G, KC * HU)
        q_sel = carve(G, KC * HU)
        a_t = carve(G, KC * HU)
        sel_t = carve(G, KC, P, rows=HU)
        dist = carve(G, P)
        ctx_t = carve(G, KC, P)
        ctx_sq = carve(G, KC, P)
        w_qkv_sb = carve(KC, 3 * D)
        w_o_sb = carve(KC, D)
        b_qv_sb = carve(2 * D)
        b_k_sb = carve(KC)
        b_o_sb = carve(D)
        sum_q = carve(P)
        max_q = carve(P)
        mean_q = carve(P)
        sum_sq = carve(P)
        sum_e = carve(P)
        rec_e = carve(P)
        sum_pl = carve(P)
        mean_sq = carve(P)
        l2 = carve(P)
        score = carve(P)
        score_t = carve(P)
        score_u = carve(P)
        t_stats = carve(6)
        t_mom = carve(2)
        t_a = carve(1)
        t_b = carve(1)
        t_c = carve(1)
        t_dev = carve(1)
        factor = carve(2, dt=BF16)[:, 0:1]
        keep_n = carve(1)
        top8 = carve(2, 8)
        idx_u = carve(2, 8, dt=U32)
        idx_f = carve(2 * 8)
        kept = carve(TOP)
        idx1 = carve(TOP)
        idx_rows = carve(HEADS, TOP, dt=BF16)
        idx_cols = carve(KC, G, rows=HU)
        neg_max = carve(G, KC, rows=HU)
        e_sum = carve(G, KC, rows=HU)
        e_rec = carve(G, KC, rows=HU)
        e_buf, o_sel, m_t = (c.rearrange("p g (c n) -> p g c n", c=KC) for c in (c1, c2, c3))

        weights_in = sem("attn_weights_in")
        x_loaded, ctx_loaded = sem("x_loaded"), sem("ctx_loaded")
        x1_stored, dist_stored = sem("x1_stored", FREE), sem("dist_stored", FREE)
        stats_a, moments_a, rstd_a, xn_ready = sem("stats_a"), sem("moments_a"), sem("rstd_a"), sem("xn_ready")
        x_res_ready = sem("x_res_ready")
        xnt_psum, xnt_ready = sem("xnt_psum"), sem("xnt_ready")
        qv_psum, qv_ready = sem("qv_psum"), sem("qv_ready")
        kt_psum, kt_ready = sem("kt_psum"), sem("kt_ready")
        sum_q_done, max_q_done, mean_q_done = sem("sum_q_done"), sem("max_q_done"), sem("mean_q_done")
        centred, shifted, expd, squared = sem("centred"), sem("shifted"), sem("expd"), sem("squared")
        sum_sq_done, rec_e_done, sum_e_done = sem("sum_sq_done"), sem("rec_e_done"), sem("sum_e_done")
        prob_done, logp_done, plogp_done = sem("prob_done"), sem("logp_done"), sem("plogp_done")
        score_step = sem("score_step")
        l2_in_done, l2_done = sem("l2_in_done"), sem("l2_done")
        score_ready, score_psum = sem("score_ready"), sem("score_psum")
        top_step = sem("top_step")
        sample_var = sem("sample_var")
        eps_a, eps_b = sem("eps_a"), sem("eps_b")
        variance_ready, deviation_ready = sem("variance_ready"), sem("deviation_ready")
        factor_ready, keep_psum = sem("factor_ready"), sem("keep_psum")
        idx_rows_ready, idx_cols_psum, idx_cols_ready = (
            sem("idx_rows_ready"), sem("idx_cols_psum"), sem("idx_cols_ready"))
        sel_t_ready = sem("sel_t_ready")
        idx_psum, sel_ready = sem("idx_psum"), sem("sel_ready")
        qs_psum, qs_ready = sem("qs_psum"), sem("qs_ready")
        s_psum, max_ready, e_ready = sem("s_psum"), sem("max_ready"), sem("e_ready")
        at_psum, at_ready = sem("at_psum"), sem("at_ready")
        o_psum, e_rec_done, o_ready = sem("o_psum"), sem("e_rec_done"), sem("o_ready")
        mt_psum, mt_ready = sem("mt_psum"), sem("mt_ready")
        attn_psum, x1_ready = sem("attn_psum"), sem("x1_ready")
        stats_b, moments_b, rstd_b, yn_ready = sem("stats_b"), sem("moments_b"), sem("rstd_b"), sem("yn_ready")
        ynt_psum, ynt_ready = sem("ynt_psum"), sem("ynt_ready")
        ctx_sq_ready = sem("ctx_sq_ready")
        sem_idx1 = sem("idx1_done")
        dist_psum, dist_sq_ready, dist_ready = sem("dist_psum"), sem("dist_sq_ready"), sem("dist_ready", FREE)

        def layer_norm(dve, g, src, dst, s_stats, s_mom, s_rstd, s_out, before_tile=None):
            for b in range(G):
                if before_tile:
                    before_tile(b)
                dve.bn_stats(stats[:, b, :], src(b)).then_inc(s_stats, 1)
            for b in range(G):
                dve.wait_ge(s_stats, g * G + (b + 1))
                apart(dve)
                dve.bn_aggr(moments[:, b, :], stats[:, b, :]).then_inc(s_mom, 1)
            dve.wait_ge(s_rstd, g + 1)
            for b in range(G):
                dve.tensor_scalar(dst(b), src(b), moments[:, b, 0:1], rstd[:, b:b + 1],
                                  ALU.subtract, ALU.mult).then_inc(s_out, 1)

        def inverse_deviation(pool, g, s_mom, s_eps, s_rstd):
            pool.wait_ge(s_mom, g * G + G)
            apart(pool)
            pool.tensor_scalar(rstd[:, :], moments[:, :, 1], EPS, None, ALU.add).then_inc(s_eps, 1)
            pool.wait_ge(s_eps, g + 1)
            pool.tensor_tensor(rstd[:, :], rstd[:, :], exponents[:, 0:G], ALU.pow).then_inc(s_rstd, 1)

        def load_group(eng, tile, dram, g, done, pattern="g p d -> p g d"):
            for half in range(2):
                eng.dma_start(tile[:, half * G // 2:(half + 1) * G // 2],
                              dram[bass.ds(g * G + half * G // 2, G // 2)].rearrange(pattern, **(
                                  {"p": P} if "(" in pattern else {}))).then_inc(done, 16)

        def heads(t):
            return t.rearrange("p g (h d) -> p g h d", h=HEADS)

        def per_head(t):
            return t.rearrange("p (g h) -> p g h", g=G).unsqueeze(3).to_broadcast([P, G, HEADS, DK])

        with nc.Block() as block:
            @block.sync
            def _(sp):
                sp.dma_start(w_qkv_sb, w_qkv.rearrange("(c p) n -> p c n", p=P)).then_inc(weights_in, 16)
                sp.dma_start(w_o_sb, w_o.rearrange("(c p) n -> p c n", p=P)).then_inc(weights_in, 16)
                sp.dma_start(b_qv_sb, b_qv.partition_broadcast(P)).then_inc(weights_in, 16)
                sp.dma_start(b_o_sb, b_o.partition_broadcast(P)).then_inc(weights_in, 16)
                with nc.allow_non_contiguous_dma(reason="256 biases, one per partition"):
                    sp.dma_start(b_k_sb, b_k.rearrange("(c p) -> p c", p=P)).then_inc(weights_in, 16)
                load_group(sp, x_in, x, 0, x_loaded)
                with sp.Fori(0, NG) as g:
                    following = sp.snap((g + 1) % NG)
                    sp.wait_ge(dist_ready, g * G + FREE)
                    load_group(sp, ctx_t, ctx_cols, g, ctx_loaded, "g (c p) n -> p g c n")
                    sp.wait_ge(xn_ready, g * G + G)
                    apart(sp)
                    sp.wait_ge(x_res_ready, g + 1)
                    apart(sp)
                    load_group(sp, x_in, x, following, x_loaded)
                    sp.wait_ge(x1_ready, g * G + G)
                    sp.dma_start(x1_dram[bass.ds(g * G, G)].rearrange("g p d -> p g d"), x_res)\
                      .then_inc(x1_stored, 16)
                    sp.wait_ge(dist_ready, g * G + G + FREE)
                    sp.dma_start(dist_dram[bass.ds(g * G, G)].rearrange("g p d -> p g d"), dist)\
                      .then_inc(dist_stored, 16)
                sp.wait_ge(x_loaded, 32 * (NG + 1))
                sp.wait_ge(x1_stored, 16 * NG + FREE)
                sp.wait_ge(dist_stored, 16 * NG + FREE)

            @block.gpsimd
            def _(pool):
                pool.wait_ge(weights_in, 16 * 5)
                with pool.Fori(0, NG) as g:
                    inverse_deviation(pool, g, moments_a, eps_a, rstd_a)
                    pool.wait_ge(x_loaded, g * 32 + 32)
                    pool.wait_ge(x1_stored, g * 16 + FREE)
                    pool.tensor_tensor(x_res, x_in, b_o_sb.unsqueeze(1).to_broadcast([P, G, D]), ALU.add)\
                        .then_inc(x_res_ready, 1)
                    pool.wait_ge(ctx_loaded, g * 32 + 32)
                    pool.tensor_tensor(ctx_sq, ctx_t, ctx_t, ALU.mult).then_inc(ctx_sq_ready, 1)
                    q = heads(qv[:, :, 0:D])
                    pool.wait_ge(mean_q_done, g + 1)
                    pool.tensor_tensor(heads(c1), q, per_head(mean_q), ALU.subtract).then_inc(centred, 1)
                    pool.wait_ge(max_q_done, g + 1)
                    pool.tensor_tensor(heads(c2), q, per_head(max_q), ALU.subtract).then_inc(shifted, 1)
                    pool.wait_ge(rec_e_done, g + 1)
                    pool.tensor_tensor(heads(c2), heads(c2), per_head(rec_e), ALU.mult).then_inc(prob_done, 1)
                    pool.wait_ge(prob_done, g + 1)
                    pool.wait_ge(logp_done, g + 1)
                    pool.tensor_tensor(c3, c3, c2, ALU.mult).then_inc(plogp_done, 1)
                    pool.wait_ge(variance_ready, g + 1)
                    apart(pool)
                    pool.tensor_scalar(t_dev, t_mom[:, 1:2], P / (P - 1), None, ALU.mult).then_inc(sample_var, 1)
                    pool.wait_ge(sample_var, g + 1)
                    pool.tensor_tensor(t_dev, t_dev, exponents[:, G:G + 1], ALU.pow).then_inc(deviation_ready, 1)
                    inverse_deviation(pool, g, moments_b, eps_b, rstd_b)

            @block.tensor
            def _(pe):
                pe.wait_ge(weights_in, 16 * 5)
                with pe.Fori(0, NG) as g:
                    def transposes(src, b, done):
                        for c in range(KC):
                            ins = pe.transpose(ps[b][:, c * P:(c + 1) * P], src[:, b, c * P:(c + 1) * P],
                                               ident[:, :])
                        ins.then_inc(done, 1)

                    for b in range(G):
                        pe.wait_ge(xn_ready, g * G + (b + 1))
                        transposes(xn, b, xnt_psum)
                    for b in range(G):
                        pe.wait_ge(xnt_ready, g * G + (b + 1))
                        for c in range(KC):
                            ins = pe.matmul(ps[b][:, :], xn_t[:, b, c, :], w_qkv_sb[:, c, 0:2 * D],
                                            start=(c == 0), stop=(c == KC - 1))
                        ins.then_inc(qv_psum, 1)
                    for b in range(G):
                        pe.wait_ge(qv_ready, g * G + (b + 1))
                        for m in range(KC):
                            for c in range(KC):
                                ins = pe.matmul(ps[b][:, m * P:(m + 1) * P],
                                                w_qkv_sb[:, c, 2 * D + m * P:2 * D + (m + 1) * P],
                                                xn_t[:, b, c, :], start=(c == 0), stop=(c == KC - 1))
                        ins.then_inc(kt_psum, 1)
                    pe.wait_ge(kt_ready, g * G + G)
                    pe.wait_ge(score_ready, g + 1)
                    pe.transpose(ps[0][:, 0:P], score, ident[:, :]).then_inc(score_psum, 1)
                    pe.wait_ge(factor_ready, g + 1)
                    pe.matmul(ps[1][:, 0:1], first_head[:, :], factor, start=True, stop=True)\
                      .then_inc(keep_psum, 1)
                    pe.wait_ge(idx_rows_ready, g + 1)
                    flat_idx = idx_rows.rearrange("p h u -> p (h u)")
                    for c in range(KC):
                        ins = pe.matmul(ps[7][0:HU, c * G:(c + 1) * G], flat_idx[:, c * HU:(c + 1) * HU],
                                        seq_rows[:, :, 0], start=True, stop=True)
                    ins.then_inc(idx_cols_psum, 1)
                    for b in range(G):
                        if b == 7:
                            pe.wait_ge(idx_cols_ready, g + 1)
                        pe.matmul(ps[b][:, 0:KC * HU], seq_rows[:, b, :], flat_idx, start=True, stop=True)\
                          .then_inc(idx_psum, 1)
                    for b in range(G):
                        pe.wait_ge(sel_ready, g * G + (b + 1))
                        for c in range(KC):
                            ins = pe.matmul(ps[b][:, c * HU:(c + 1) * HU], qv[:, b, c * P:(c + 1) * P],
                                            sel[:, b, c * HU:(c + 1) * HU], start=True, stop=True)
                        ins.then_inc(qs_psum, 1)
                    for b in range(G):
                        pe.wait_ge(qs_ready, g * G + (b + 1))
                        for c in range(KC):
                            ins = pe.matmul(ps[b][0:HU, c * P:(c + 1) * P], q_sel[:, b, c * HU:(c + 1) * HU],
                                            k_t[:, b, c, :], start=True, stop=True)
                        ins.then_inc(s_psum, 1)
                    for b in range(G):
                        pe.wait_ge(e_ready, g * G + (b + 1))
                        for c in range(KC):
                            ins = pe.transpose(ps[b][:, c * HU:(c + 1) * HU], e_buf[0:HU, b, c, :],
                                               ident[0:HU, 0:HU])
                        ins.then_inc(at_psum, 1)
                    for b in range(G):
                        pe.wait_ge(at_ready, g * G + (b + 1))
                        for c in range(KC):
                            ins = pe.matmul(ps[b][0:HU, c * P:(c + 1) * P], a_t[:, b, c * HU:(c + 1) * HU],
                                            qv[:, b, D + c * P:D + (c + 1) * P], start=True, stop=True)
                        ins.then_inc(o_psum, 1)
                    pe.wait_ge(sel_t_ready, g + 1)
                    for b in range(G):
                        pe.wait_ge(o_ready, g * G + (b + 1))
                        for c in range(KC):
                            ins = pe.matmul(ps[b][:, c * P:(c + 1) * P], o_sel[0:HU, b, c, :],
                                            sel_t[:, b, c, :], start=True, stop=True)
                        ins.then_inc(mt_psum, 1)
                    for b in range(G):
                        pe.wait_ge(mt_ready, g * G + (b + 1))
                        for c in range(KC):
                            ins = pe.matmul(ps[b][:, 0:D], m_t[:, b, c, :], w_o_sb[:, c, :],
                                            start=(c == 0), stop=(c == KC - 1))
                        ins.then_inc(attn_psum, 1)
                    for b in range(G):
                        pe.wait_ge(yn_ready, g * G + (b + 1))
                        transposes(xn, b, ynt_psum)
                    pe.wait_ge(ctx_sq_ready, g + 1)
                    for b in range(G):
                        pe.wait_ge(ynt_ready, g * G + (b + 1))
                        for c in range(KC):
                            pe.matmul(ps[b][:, P:P + 1], ctx_sq[:, b, c, :], neg_half[:, 0:1],
                                      start=(c == 0), stop=(c == KC - 1))
                        for c in range(KC):
                            pe.matmul(ps[b][:, 0:P], ctx_t[:, b, c, :], xn_t[:, b, c, :],
                                      start=(c == 0), stop=False)
                        for c in range(KC):
                            ins = pe.matmul(ps[b][:, 0:P], neg_half[:, :], e_buf[:, b, c, :],
                                            start=False, stop=(c == KC - 1))
                        ins.then_inc(dist_psum, 1)

            @block.scalar
            def _(act):
                act.wait_ge(weights_in, 16 * 5)
                with act.Fori(0, NG) as g:
                    for b in range(G):
                        act.wait_ge(xnt_psum, g * G + (b + 1))
                        act.activation(xn_t[:, b, :, :].rearrange("p c n -> p (c n)"), ps[b][:, 0:D], ACT.Copy)\
                           .then_inc(xnt_ready, 1)
                    for b in range(G):
                        act.wait_ge(kt_psum, g * G + (b + 1))
                        for c in range(KC):
                            ins = act.activation(k_t[:, b, c, :], ps[b][:, c * P:(c + 1) * P], ACT.Identity,
                                                 bias=b_k_sb[:, c:c + 1])
                        ins.then_inc(kt_ready, 1)
                    act.wait_ge(centred, g + 1)
                    act.activation(c1, c1, ACT.Square).then_inc(squared, 1)
                    act.wait_ge(shifted, g + 1)
                    act.activation(c2, c2, ACT.Exp).then_inc(expd, 1)
                    act.wait_ge(prob_done, g + 1)
                    act.activation(c3, c2, ACT.Ln, bias=tiny[:, 0:1]).then_inc(logp_done, 1)
                    act.wait_ge(l2_in_done, g + 1)
                    act.activation(l2, mean_sq, ACT.Sqrt).then_inc(l2_done, 1)
                    for b in range(G):
                        act.wait_ge(max_ready, g * G + (b + 1))
                        for c in range(KC):
                            ins = act.activation(e_buf[0:HU, b, c, :], ps[b][0:HU, c * P:(c + 1) * P], ACT.Exp,
                                                 bias=neg_max[:, b, c:c + 1], accum_out=e_sum[:, b, c:c + 1])
                        ins.then_inc(e_ready, 1)
                    for b in range(G):
                        act.wait_ge(at_psum, g * G + (b + 1))
                        act.activation(a_t[:, b, :], ps[b][:, 0:KC * HU], ACT.Copy).then_inc(at_ready, 1)
                    for b in range(G):
                        act.wait_ge(mt_psum, g * G + (b + 1))
                        act.activation(m_t[:, b, :, :].rearrange("p c n -> p (c n)"), ps[b][:, 0:D], ACT.Copy)\
                           .then_inc(mt_ready, 1)
                    for b in range(G):
                        act.wait_ge(ynt_psum, g * G + (b + 1))
                        act.activation(xn_t[:, b, :, :].rearrange("p c n -> p (c n)"), ps[b][:, 0:D], ACT.Copy)
                        act.activation(e_buf[:, b, :, :].rearrange("p c n -> p (c n)"), ps[b][:, 0:D],
                                       ACT.Square).then_inc(ynt_ready, 1)
                    act.wait_ge(dist_stored, g * 16 + FREE)
                    for b in range(G):
                        act.wait_ge(dist_sq_ready, g * G + (b + 1))
                        act.activation(dist[:, b, :], dist[:, b, :], ACT.Sqrt, scale=-2.0).then_inc(dist_ready, 1)

            @block.vector
            def _(dve):
                dve.wait_ge(weights_in, 16 * 5)
                with dve.Fori(0, NG) as g:
                    dve.wait_ge(x_loaded, g * 32 + 32)
                    layer_norm(dve, g, lambda b: x_in[:, b, :], lambda b: xn[:, b, :],
                               stats_a, moments_a, rstd_a, xn_ready)
                    for b in range(G):
                        dve.wait_ge(qv_psum, g * G + (b + 1))
                        dve.tensor_tensor(qv[:, b, :], ps[b][:, :], b_qv_sb, ALU.add).then_inc(qv_ready, 1)
                    dve.wait_ge(qv_ready, g * G + G)
                    q = heads(qv[:, :, 0:D])
                    head_grid = lambda t: t.rearrange("p (g h) -> p g h", g=G)
                    dve.tensor_reduce(head_grid(sum_q), q, AX.X, ALU.add).then_inc(sum_q_done, 1)
                    dve.wait_ge(sum_q_done, g + 1)
                    dve.tensor_scalar(mean_q, sum_q, 1.0 / DK, None, ALU.mult).then_inc(mean_q_done, 1)
                    dve.tensor_reduce(head_grid(max_q), q, AX.X, ALU.max).then_inc(max_q_done, 1)
                    dve.wait_ge(squared, g + 1)
                    dve.tensor_reduce(head_grid(sum_sq), heads(c1), AX.X, ALU.add).then_inc(sum_sq_done, 1)
                    dve.wait_ge(expd, g + 1)
                    dve.tensor_reduce(head_grid(sum_e), heads(c2), AX.X, ALU.add).then_inc(sum_e_done, 1)
                    dve.wait_ge(sum_e_done, g + 1)
                    dve.reciprocal(rec_e, sum_e).then_inc(rec_e_done, 1)
                    dve.wait_ge(mean_q_done, g + 1)
                    dve.scalar_tensor_tensor(mean_sq, mean_q, float(DK), mean_q, ALU.mult, ALU.mult)\
                       .then_inc(score_step, 1)
                    dve.wait_ge(score_step, g * 3 + 1)
                    dve.wait_ge(sum_sq_done, g + 1)
                    dve.tensor_tensor(mean_sq, mean_sq, sum_sq, ALU.add).then_inc(l2_in_done, 1)
                    dve.wait_ge(l2_done, g + 1)
                    dve.scalar_tensor_tensor(score, sum_sq, 0.4 / (DK - 1), l2, ALU.mult, ALU.add)\
                       .then_inc(score_step, 1)
                    dve.wait_ge(plogp_done, g + 1)
                    dve.tensor_reduce(head_grid(sum_pl), heads(c3), AX.X, ALU.add).then_inc(score_step, 1)
                    dve.wait_ge(score_step, g * 3 + 3)
                    dve.scalar_tensor_tensor(score, sum_pl, -0.6, score, ALU.mult, ALU.add)\
                       .then_inc(score_ready, 1)
                    TS = 13
                    k = 0

                    def step(ins):
                        nonlocal k
                        ins.then_inc(top_step, 1)
                        k += 1
                        dve.wait_ge(top_step, g * TS + k)
                    dve.wait_ge(score_psum, g + 1)
                    step(dve.tensor_scalar(score_t, ps[0][:, 0:P], 0.5, None, ALU.mult))
                    step(dve.bn_stats(t_stats, score_t))
                    apart(dve)
                    dve.bn_aggr(t_mom, t_stats).then_inc(variance_ready, 1)
                    dve.wait_ge(variance_ready, g + 1)
                    step(dve.tensor_scalar(t_b, t_mom[:, 0:1], 1e-6, None, ALU.add))
                    step(dve.reciprocal(t_b, t_b))
                    dve.wait_ge(deviation_ready, g + 1)
                    step(dve.tensor_tensor(t_c, t_dev, t_b, ALU.mult))
                    step(dve.tensor_scalar(t_a, t_c, float(TOP), float(TOP), ALU.mult, ALU.min))
                    step(dve.tensor_scalar(t_b, t_a, float(MIN_TOP), MAGIC, ALU.max, ALU.add))
                    dve.tensor_scalar(factor, t_b, MAGIC, None, ALU.subtract).then_inc(factor_ready, 1)
                    apart(dve)
                    step(dve.max(top8[:, 0, :], score_t))
                    apart(dve)
                    step(dve.match_replace(score_u, top8[:, 0, :], score_t, -3e38))
                    apart(dve)
                    step(dve.max(top8[:, 1, :], score_u))
                    apart(dve)
                    dve.max_index(idx_u[:, 0, :], top8[:, 0, :], score_t)
                    step(dve.max_index(idx_u[:, 1, :], top8[:, 1, :], score_u))
                    step(dve.tensor_copy(idx_f, idx_u.rearrange("p a b -> p (a b)")))
                    dve.wait_ge(keep_psum, g + 1)
                    step(dve.tensor_scalar(kept, iota_small[:, :], ps[1][:, 0:1], None, ALU.is_lt))
                    assert k == TS
                    dve.scalar_tensor_tensor(idx1, idx_f[:, 0:TOP], 1.0, kept, ALU.add, ALU.mult)\
                       .then_inc(sem_idx1, 1)
                    dve.wait_ge(sem_idx1, g + 1)
                    dve.tensor_tensor(idx_rows, idx1.unsqueeze(1).to_broadcast([P, HEADS, TOP]),
                                      head_of_row[:, :].unsqueeze(2).to_broadcast([P, HEADS, TOP]), ALU.mult)\
                       .then_inc(idx_rows_ready, 1)
                    dve.wait_ge(idx_cols_psum, g + 1)
                    dve.tensor_copy(idx_cols, ps[7][0:HU, 0:KC * G].rearrange("p (c g) -> p c g", c=KC))\
                       .then_inc(idx_cols_ready, 1)
                    for b in range(G):
                        dve.wait_ge(idx_psum, g * G + (b + 1))
                        dve.tensor_scalar(sel[:, b, :], ps[b][:, 0:KC * HU], iota_p1[:, 0:1], None,
                                          ALU.is_equal).then_inc(sel_ready, 1)
                    dve.wait_ge(idx_cols_ready, g + 1)
                    for c in range(KC):
                        ins = dve.tensor_tensor(sel_t[:, :, c, :],
                                                iota_f1[0:HU, :].unsqueeze(1).to_broadcast([HU, G, P]),
                                                idx_cols[:, c, :].unsqueeze(2).to_broadcast([HU, G, P]),
                                                ALU.is_equal)
                    ins.then_inc(sel_t_ready, 1)
                    for b in range(G):
                        dve.wait_ge(qs_psum, g * G + (b + 1))
                        dve.tensor_tensor(q_sel[:, b, :], ps[b][:, 0:KC * HU],
                                          head_block[:, :, :, :].rearrange("p c h u -> p (c h u)"),
                                          ALU.mult).then_inc(qs_ready, 1)
                    for b in range(G):
                        dve.wait_ge(s_psum, g * G + (b + 1))
                        dve.tensor_reduce(neg_max[:, b, :], ps[b][0:HU, 0:D].rearrange("p (c n) -> p c n", c=KC),
                                          AX.X, ALU.max, negate=True).then_inc(max_ready, 1)
                    dve.wait_ge(e_ready, g * G + G)
                    dve.reciprocal(e_rec, e_sum).then_inc(e_rec_done, 1)
                    dve.wait_ge(e_rec_done, g + 1)
                    for b in range(G):
                        dve.wait_ge(o_psum, g * G + (b + 1))
                        for c in range(KC):
                            ins = dve.scalar_tensor_tensor(
                                o_sel[0:HU, b, c, :], ps[b][0:HU, c * P:(c + 1) * P], e_rec[:, b, c:c + 1],
                                head_block2[:, :, :].rearrange("p h d -> p (h d)"), ALU.mult, ALU.mult)
                        ins.then_inc(o_ready, 1)
                    dve.wait_ge(x_res_ready, g + 1)
                    for b in range(G):
                        dve.wait_ge(attn_psum, g * G + (b + 1))
                        dve.tensor_tensor(x_res[:, b, :], x_res[:, b, :], ps[b][:, 0:D], ALU.add)\
                           .then_inc(x1_ready, 1)
                    layer_norm(dve, g, lambda b: x_res[:, b, :], lambda b: xn[:, b, :],
                               stats_b, moments_b, rstd_b, yn_ready,
                               before_tile=lambda b: dve.wait_ge(x1_ready, g * G + (b + 1)))
                    dve.wait_ge(dist_stored, g * 16 + FREE)
                    for b in range(G):
                        dve.wait_ge(dist_psum, g * G + (b + 1))
                        dve.tensor_scalar(dist[:, b, :], ps[b][:, 0:P], ps[b][:, P:P + 1], 0.0,
                                          ALU.add, ALU.min).then_inc(dist_sq_ready, 1)
        next_phase()
        carve = carver()
        cost = carve(P + 1, P + 1, rows=B)
        upper = carve(P, P, rows=B)
        code = carve(P, P, dt=BF16, rows=B)
        junk = carve(P, 2, rows=B)
        upper_flat = upper.rearrange("p i j -> p (i j)")
        code_flat = code.rearrange("p i j -> p (i j)")
        TURNS = P // ROWS

        edge_made = sem("edge_made")
        cost_loaded = [sem(f"cost_loaded{c}") for c in range(TURNS)]
        sem_sign = sem("sign_done")
        upper_done, row_done = sem("upper_done"), sem("row_done", FREE)
        diff_done, is_up_done, code_done = sem("diff_done"), sem("is_up_done"), sem("code_done")
        left_done, gated_done, scan_done, path_step = (
            sem("left_done"), sem("gated_done"), sem("scan_done"), sem("path_step"))

        with nc.Block() as block:
            @block.sync
            def _(sp):
                for c in range(TURNS):
                    sp.dma_start(cost[:, 1 + c * ROWS:1 + (c + 1) * ROWS, 1:P + 1],
                                 dist_dram[:, c * ROWS:(c + 1) * ROWS, :]).then_inc(cost_loaded[c], 16)

            @block.gpsimd
            def _(pool):
                pool.memset(cost[:, 0, 1:P + 1], BIG).then_inc(edge_made, 1)
                pool.memset(cost[:, 1:P + 1, 0], BIG).then_inc(edge_made, 1)
                pool.memset(cost[:, 0, 0:1], 0.0).then_inc(edge_made, 1)
                pool.memset(codes[:, 0:1], 0.0).then_inc(edge_made, 1)
                pool.memset(codes[:, P:P + 1], 2.0 * P - 1).then_inc(edge_made, 1)
                with pool.Fori(0, TURNS) as t:
                    pool.wait_ge(row_done, t * ROWS + ROWS + FREE)
                    apart(pool)
                    rows = bass.ds(t * ROWS, ROWS)
                    pool.tensor_tensor(code[:, rows, :], cost[:, rows, 1:P + 1], cost[:, rows, 0:P],
                                       ALU.subtract).then_inc(diff_done, 1)
                    pool.wait_ge(is_up_done, t + 1)
                    apart(pool)
                    pool.tensor_tensor(code[:, rows, :], code[:, rows, :],
                                       iota_2j[0:B, :].unsqueeze(1).to_broadcast([B, ROWS, P]), ALU.add)\
                        .then_inc(code_done, 1)

            @block.scalar
            def _(act):
                with act.Fori(0, TURNS) as t:
                    flat = code_flat[:, bass.ds(t * ROWS * P, ROWS * P)]
                    act.wait_ge(diff_done, t + 1)
                    apart(act)
                    act.activation(flat, flat, ACT.Sign, scale=-1.0).then_inc(sem_sign, 1)
                    act.wait_ge(sem_sign, t + 1)
                    apart(act)
                    act.activation(flat, flat, ACT.Relu).then_inc(is_up_done, 1)

            @block.vector
            def _(dve):
                dve.wait_ge(edge_made, 5)
                for c in range(TURNS):
                    dve.wait_ge(cost_loaded[c], 16)
                with dve.Fori(0, TURNS) as t:
                    for r in range(ROWS):
                        i = t * ROWS + r
                        if r == 0:
                            dve.wait_ge(row_done, t * ROWS + FREE)
                        else:
                            dve.wait_ge(row_done, t * ROWS + r + FREE)
                        dve.tensor_tensor(upper[:, i, :], cost[:, i, 1:P + 1], cost[:, i, 0:P], ALU.min)\
                           .then_inc(upper_done, 1)
                        dve.wait_ge(upper_done, t * ROWS + (r + 1))
                        dve.tensor_tensor_scan(cost[:, i + 1, 1:P + 1], upper[:, i, :], cost[:, i + 1, 1:P + 1],
                                               BIG, ALU.min, ALU.add).then_inc(row_done, 1)
                dve.wait_ge(row_done, P + FREE)
                for h in range(4):
                    rows = slice(h * P // 4, (h + 1) * P // 4)
                    at = slice(h * P * P // 4, (h + 1) * P * P // 4)
                    dve.tensor_tensor(upper[:, rows, :], upper[:, rows, :],
                                      cost[:, 1 + h * P // 4:1 + (h + 1) * P // 4, 0:P], ALU.is_gt)\
                       .then_inc(left_done, 1)
                    dve.wait_ge(left_done, h + 1)
                    dve.wait_ge(code_done, (h + 1) * TURNS // 4)
                    dve.scalar_tensor_tensor(code_flat[:, at], upper_flat[:, at], 1.0, code_flat[:, at],
                                             ALU.is_lt, ALU.mult).then_inc(gated_done, 1)
                    dve.wait_ge(gated_done, h + 1)
                    dve.tensor_tensor_scan(upper_flat[:, at], upper_flat[:, at], code_flat[:, at],
                                           0.0, ALU.mult, ALU.add).then_inc(scan_done, 1)
                dve.wait_ge(scan_done, 4)

                def follow(i, before_it):
                    dve.wait_ge(path_step, before_it)
                    if not isinstance(i, int):
                        apart(dve)
                    dve.scalar_tensor_tensor(
                        junk, iota_256[0:B, :].rearrange("p (j t) -> p j t", t=2), codes[:, at_col(i + 1)],
                        upper[:, at_row(i), :].unsqueeze(2).to_broadcast([B, P, 2]),
                        ALU.is_equal, ALU.mult, accum_out=codes[:, at_col(i)]).then_inc(path_step, 1)

                def at_col(i):
                    return bass.ds(i, 1) if not isinstance(i, int) else slice(i, i + 1)

                def at_row(i):
                    return i
                for i in range(P - 1, P - 1 - (P - 1) % PATH_UNROLL, -1):
                    follow(i, P - 1 - i)
                done = (P - 1) % PATH_UNROLL
                with dve.Fori(0, (P - 1) // PATH_UNROLL) as t:
                    for k in range(PATH_UNROLL):
                        follow(P - 1 - done - k - t * PATH_UNROLL, t * PATH_UNROLL + (done + k))
                dve.wait_ge(path_step, P - 1)

        next_phase()
        carve = carver()
        w1_sb = carve(EXPERTS, KC, HID)
        w2_sb = carve(EXPERTS, HK, D)
        b1_sb = carve(EXPERTS, HID)
        g1_sb = carve(EXPERTS, HID)
        be1_sb = carve(EXPERTS, HID)
        b2_sb = carve(EXPERTS, D)
        after_weights = carve.at()
        ctx = carve(G, D)
        x2 = carve(G, D)
        rows = [carve(G, ROW) for _ in range(2)]
        xf_t = carve(G, KC, P)
        mask = carve(G, P)
        gate_sb = carve(KC, EXPERTS)
        null_row = carve(ROW)
        logits = carve(G, EXPERTS)
        masked = carve(G, EXPERTS)
        hit = carve(G, EXPERTS)
        hot = [carve(G, EXPERTS) for _ in range(2)]
        hot_both = carve(G, EXPERTS, dt=BF16)
        place = carve(G, EXPERTS)
        picked = carve(G, EXPERTS)
        best = [carve(G) for _ in range(2)]
        rank = [carve(G) for _ in range(2)]
        spot = carve(2, G)
        spot_i = carve(2, G, dt=I32)
        gap = carve(G)
        ratio = carve(G)
        fill = carve(EXPERTS)
        first_row = carve(EXPERTS)
        count = carve(EXPERTS)
        tiles = carve(EXPERTS)
        tile_end = carve(EXPERTS)
        skip = carve(EXPERTS)
        tail_f = carve(EXPERTS)
        tail_i = carve(EXPERTS, dt=I32)
        tile_f = carve(NS)
        addr_f = carve(NS)
        used = carve(NS)
        pair_row = carve(2, G)

        tables_made = sem("tables_made")
        gate_in, moe_weights_in = sem("gate_in"), sem("moe_weights_in")
        ctx_in, x1_in = sem("ctx_in"), sem("x1_in")
        x2_stored = sem("x2_stored", FREE)
        codes_psum, codes_ready = sem("codes_psum"), sem("codes_ready")
        mask_half, mask_ready = sem("mask_half"), sem("mask_ready")
        warp_psum, x2_ready = sem("warp_psum"), sem("x2_ready", FREE)
        stats_c, moments_c, rstd_c, xf_ready = sem("stats_c"), sem("moments_c"), sem("rstd_c"), sem("xf_ready", FREE)
        eps_c = sem("eps_c")
        xf_copied, kept_moments = sem("xf_copied"), sem("kept_moments")
        xft_psum, xft_ready = sem("xft_psum"), sem("xft_ready")
        logit_psum, gate_step = sem("logit_psum"), sem("gate_step", FREE)
        hot_ready, place_psum = sem("hot_ready"), sem("place_psum")
        gap_ready, ratio_ready = sem("gap_ready"), sem("ratio_ready")
        spots_ready, weights_ready = sem("spots_ready"), sem("weights_ready")
        pair_rows_put, pair_rows_moved = sem("pair_rows_put"), sem("pair_rows_moved")
        tail_ready, tails_out, null_out = sem("tail_ready"), sem("tails_out"), sem("null_out")
        scattered = [[sem(f"scattered{k}_{b}") for b in range(G)] for k in range(2)]

        with nc.Block() as block:
            @block.sync
            def _(sp):
                sp.dma_start(gate_sb, gate_w.rearrange("(c p) e -> p c e", p=P)).then_inc(gate_in, 16)
                sp.wait_ge(tables_made, 6)
                sp.dma_start(slots[NULL_TILE * P:(NULL_TILE + 1) * P, :], null_row).then_inc(null_out, 16)
                with sp.Fori(0, NG) as g:
                    seqs = bass.ds(g * G, G)
                    sp.wait_ge(x2_ready, g * G + FREE)
                    load_group(sp, ctx, ctx_rows, g, ctx_in)
                    sp.wait_ge(x2_stored, g * 16 + FREE)
                    sp.wait_ge(xf_ready, g * G + FREE)
                    load_group(sp, x2, x1_dram, g, x1_in)
                    sp.wait_ge(x2_ready, g * G + (G + FREE))
                    sp.dma_start(x2_dram[seqs].rearrange("g p d -> p g d"), x2).then_inc(x2_stored, 16)
                sp.wait_ge(x2_stored, 16 * NG + FREE)
                sp.wait_ge(null_out, 16)

            @block.gpsimd
            def _(pool):
                pool.iota(first_row, pattern=[[REGION, EXPERTS]], base=0, channel_multiplier=0,
                          allow_small_or_imprecise_dtypes=True).then_inc(tables_made, 1)
                pool.iota(fill, pattern=[[REGION, EXPERTS]], base=0, channel_multiplier=0,
                          allow_small_or_imprecise_dtypes=True).then_inc(tables_made, 1)
                for k in range(2):
                    pool.iota(pair_row[:, k, :], pattern=[[P, G]], base=k * T, channel_multiplier=1,
                              allow_small_or_imprecise_dtypes=True).then_inc(tables_made, 1)
                pool.memset(null_row[:, 0:D + 1], 0.0).then_inc(tables_made, 1)
                pool.memset(null_row[:, D + 1:ROW], float(4 * T)).then_inc(tables_made, 1)
                for t, src in ((b1_sb, b1), (g1_sb, ln1_g), (be1_sb, ln1_b), (b2_sb, b2)):
                    pool.dma_start(t, src.partition_broadcast(P)).then_inc(moe_weights_in, 16)
                for e in range(EXPERTS):
                    pool.dma_start(w1_sb[:, e, :, :], w1[e].rearrange("(c p) n -> p c n", p=P))\
                        .then_inc(moe_weights_in, 16)
                    pool.dma_start(w2_sb[:, e, :, :], w2[e].rearrange("(c p) n -> p c n", p=P))\
                        .then_inc(moe_weights_in, 16)
                pool.wait_ge(tables_made, 6)

                def group(g, first=False):
                    inverse_deviation(pool, g, moments_c, eps_c, rstd_c)
                    for k in range(2):
                        for b in range(G):
                            if not first:
                                pool.wait_ge(scattered[k][b], g * 16)
                        apart(pool)
                        pool.tensor_copy(rows[k][:, :, D + 1], pair_row[:, k, :]).then_inc(pair_rows_put, 1)
                    pool.wait_ge(pair_rows_put, g * 2 + 2)
                    apart(pool)
                    pool.tensor_scalar(pair_row, pair_row, float(G * P), None, ALU.add)\
                        .then_inc(pair_rows_moved, 1)
                    pool.wait_ge(pair_rows_moved, g + 1)
                    pool.wait_ge(spots_ready, g + 1)
                    pool.wait_ge(weights_ready, g * 2 + 2)
                    for b in range(G):
                        for k in range(2):
                            pool.wait_ge(xf_copied, g * G + (b + 1))
                            apart(pool)
                            pool.indirect_dma_start(
                                out=slots[:, :],
                                out_offset=bass.IndirectOffsetOnAxis(ap=spot_i[:, k, b:b + 1], axis=0),
                                in_=rows[k][:, b, :], in_offset=None).then_inc(scattered[k][b], 16)
                group(0, first=True)
                with pool.Fori(1, NG) as g:
                    group(g)
                pool.wait_ge(tail_ready, 1)
                for e in range(EXPERTS):
                    pool.indirect_dma_start(
                        out=slots[:, :], out_offset=bass.IndirectOffsetOnAxis(ap=tail_i[:, e:e + 1], axis=0),
                        in_=null_row, in_offset=None).then_inc(tails_out, 16)
                pool.wait_ge(tails_out, 16 * EXPERTS)
                for k in range(2):
                    for b in range(G):
                        pool.wait_ge(scattered[k][b], 16 * NG)
                pool.wait_ge(moe_weights_in, 16 * (4 + 2 * EXPERTS))

            @block.tensor
            def _(pe):
                pe.transpose(ps[0][:, 0:B], codes[:, 1:P + 1], ident[0:B, 0:B]).then_inc(codes_psum, 1)
                pe.transpose(ps[1][:, 0:B], codes[:, 0:P], ident[0:B, 0:B]).then_inc(codes_psum, 1)
                pe.wait_ge(gate_in, 16)
                pe.wait_ge(codes_ready, 2)
                flat = hot_both.rearrange("p g e -> p (g e)")
                with pe.Fori(0, NG) as g:
                    pe.wait_ge(ctx_in, g * 32 + 32)
                    pe.wait_ge(gate_step, g * GATE_STEPS + FREE)
                    for b in range(G):
                        pe.wait_ge(mask_ready, g * G + (b + 1))
                        pe.matmul(ps[b][:, 0:D], mask[:, b, :], ctx[:, b, :], start=True, stop=True)\
                          .then_inc(warp_psum, 1)
                    for b in range(G):
                        pe.wait_ge(xf_ready, g * G + (b + 1 + FREE))
                        for c in range(KC):
                            ins = pe.transpose(ps[b][:, c * P:(c + 1) * P], rows[0][:, b, c * P:(c + 1) * P],
                                               ident[:, :])
                        ins.then_inc(xft_psum, 1)
                    pe.wait_ge(xft_ready, g * G + G)
                    for b in range(G):
                        for c in range(KC):
                            ins = pe.matmul(ps[0][:, b * EXPERTS:(b + 1) * EXPERTS], xf_t[:, b, c, :],
                                            gate_sb[:, c, :], start=(c == 0), stop=(c == KC - 1))
                    ins.then_inc(logit_psum, 1)
                    pe.wait_ge(hot_ready, g + 1)
                    n = G * EXPERTS
                    pe.matmul(ps[1][:, 0:n], before[:, :], flat, start=True, stop=False)
                    for b in range(1, G):
                        pe.matmul(ps[1][:, b * EXPERTS:n], ones_bf[:, :], flat[:, 0:n - b * EXPERTS],
                                  start=False, stop=(b == G - 1))
                    for b in range(G):
                        ins = pe.matmul(ps[2][:, 0:EXPERTS], ones_bf[:, :], flat[:, b * EXPERTS:(b + 1) * EXPERTS],
                                        start=(b == 0), stop=(b == G - 1))
                    ins.then_inc(place_psum, 1)

            @block.scalar
            def _(act):
                def group(g, first=False):
                    for b in range(G):
                        act.wait_ge(xft_psum, g * G + (b + 1))
                        act.activation(xf_t[:, b, :, :].rearrange("p c n -> p (c n)"), ps[b][:, 0:D], ACT.Copy)\
                           .then_inc(xft_ready, 1)
                    for b in range(G):
                        if not first:
                            act.wait_ge(scattered[1][b], g * 16)
                        act.wait_ge(xf_ready, g * G + (b + 1 + FREE))
                        act.activation(rows[1][:, b, 0:D], rows[0][:, b, 0:D], ACT.Copy).then_inc(xf_copied, 1)
                    act.wait_ge(gap_ready, g + 1)
                    act.activation(ratio, gap, ACT.Exp).then_inc(ratio_ready, 1)
                group(0, first=True)
                with act.Fori(1, NG) as g:
                    group(g)

            @block.vector
            def _(dve):
                dve.wait_ge(codes_psum, 2)
                for k in range(2):
                    dve.tensor_copy(row_code[:, k, :], ps[k][:, 0:B]).then_inc(codes_ready, 1)
                dve.wait_ge(codes_ready, 2)
                dve.wait_ge(tables_made, 6)
                odd = iota_256[:, :].rearrange("p (j t) -> p j t", t=2)[:, :, 0]

                def wide(t):
                    return t.unsqueeze(2).to_broadcast([P, G, EXPERTS])

                def group(g, first=False):
                    for b in range(G):
                        dve.tensor_scalar(mask[:, b, :], iota_2j[:, :], row_code[:, 0, bass.ds(g * G + b, 1)],
                                          None, ALU.is_lt).then_inc(mask_half, 1)
                    for b in range(G):
                        dve.wait_ge(mask_half, g * G + (b + 1))
                        dve.scalar_tensor_tensor(mask[:, b, :], odd, row_code[:, 1, bass.ds(g * G + b, 1)],
                                                 mask[:, b, :], ALU.is_ge, ALU.mult).then_inc(mask_ready, 1)
                    dve.wait_ge(x1_in, g * 32 + 32)
                    for b in range(G):
                        dve.wait_ge(warp_psum, g * G + (b + 1))
                        dve.tensor_tensor(x2[:, b, :], x2[:, b, :], ps[b][:, 0:D], ALU.add).then_inc(x2_ready, 1)
                    if not first:
                        for b in range(G):
                            dve.wait_ge(scattered[0][b], g * 16)
                    layer_norm(dve, g, lambda b: x2[:, b, :], lambda b: rows[0][:, b, 0:D],
                               stats_c, moments_c, rstd_c, xf_ready,
                               before_tile=lambda b: dve.wait_ge(x2_ready, g * G + (b + 1 + FREE)))
                    dve.tensor_copy(xf_scale[:, 0, bass.ds(g * G, G)], rstd[:, :])
                    dve.scalar_tensor_tensor(xf_scale[:, 1, bass.ds(g * G, G)], moments[:, :, 0], -1.0,
                                             rstd[:, :], ALU.mult, ALU.mult).then_inc(kept_moments, 1)
                    dve.wait_ge(logit_psum, g + 1)
                    n = 0

                    def step(ins):
                        nonlocal n
                        ins.then_inc(gate_step, 1)
                        n += 1
                        dve.wait_ge(gate_step, g * GATE_STEPS + (n + FREE))
                    step(dve.tensor_copy(logits, ps[0][:, 0:G * EXPERTS].rearrange("p (g e) -> p g e", g=G)))
                    src = logits
                    for k in range(2):
                        step(dve.tensor_reduce(best[k], src, AX.X, ALU.max))
                        step(dve.tensor_tensor(hit, src, wide(best[k]), ALU.is_equal))
                        step(dve.tensor_tensor(hit, hit, from_8[:, :, :], ALU.mult))
                        step(dve.tensor_reduce(rank[k], hit, AX.X, ALU.max))
                        step(dve.tensor_tensor(hot[k], from_8[:, :, :], wide(rank[k]), ALU.is_equal))
                        if k == 0:
                            step(dve.scalar_tensor_tensor(masked, hot[0], -3e38, logits, ALU.mult, ALU.add))
                            src = masked
                    dve.tensor_tensor(hot_both, hot[0], hot[1], ALU.add).then_inc(hot_ready, 1)
                    dve.tensor_tensor(gap, best[1], best[0], ALU.subtract).then_inc(gap_ready, 1)
                    dve.wait_ge(place_psum, g + 1)
                    step(dve.tensor_tensor(place, ps[1][:, 0:G * EXPERTS].rearrange("p (g e) -> p g e", g=G),
                                           fill.unsqueeze(1).to_broadcast([P, G, EXPERTS]), ALU.add))
                    step(dve.tensor_tensor(fill, fill, ps[2][:, 0:EXPERTS], ALU.add))
                    for k in range(2):
                        step(dve.tensor_tensor(picked, place, hot[k], ALU.mult))
                        step(dve.tensor_reduce(spot[:, k, :], picked, AX.X, ALU.add))
                    if not first:
                        for b in range(G):
                            dve.wait_ge(scattered[1][b], g * 16)
                    dve.tensor_copy(spot_i, spot).then_inc(spots_ready, 1)
                    dve.wait_ge(ratio_ready, g + 1)
                    step(dve.tensor_scalar(gap, ratio, 1.0, None, ALU.add))
                    dve.reciprocal(rows[0][:, :, D], gap).then_inc(weights_ready, 1)
                    dve.wait_ge(weights_ready, g * 2 + 1)
                    dve.tensor_tensor(rows[1][:, :, D], ratio, rows[0][:, :, D], ALU.mult)\
                       .then_inc(weights_ready, 1)
                    assert n == GATE_STEPS
                group(0, first=True)
                with dve.Fori(1, NG) as g:
                    group(g)

                m = 0

                def step(ins):
                    nonlocal m
                    ins.then_inc(gate_step, 1)
                    m += 1
                    dve.wait_ge(gate_step, NG * GATE_STEPS + FREE + m)
                step(dve.tensor_tensor(count, fill, first_row, ALU.subtract))
                step(dve.tensor_scalar(tail_f, fill, iota_p1[:, 0:1], -1.0, ALU.add, ALU.add))
                dve.tensor_copy(tail_i, tail_f).then_inc(tail_ready, 1)
                step(dve.tensor_scalar(tiles, count, 1.0 / P, (P - 1) / (2.0 * P), ALU.mult, ALU.add))
                step(dve.tensor_scalar(tiles, tiles, MAGIC, None, ALU.add))
                step(dve.tensor_scalar(tiles, tiles, MAGIC, None, ALU.subtract))
                step(dve.tensor_tensor_scan(tile_end, ones8[:, :], tiles, 0.0, ALU.mult, ALU.add))
                step(dve.tensor_scalar(skip, tiles, -1.0, REGION / P, ALU.mult, ALU.add))
                step(dve.tensor_scalar(tile_f, iota_slot[:, :], tile_end[:, 0:1], None, ALU.is_ge))
                step(dve.scalar_tensor_tensor(addr_f, tile_f, skip[:, 0:1], iota_slot[:, :], ALU.mult, ALU.add))
                for e in range(1, EXPERTS - 1):
                    step(dve.tensor_scalar(used, iota_slot[:, :], tile_end[:, e:e + 1], None, ALU.is_ge))
                    step(dve.scalar_tensor_tensor(addr_f, used, skip[:, e:e + 1], addr_f, ALU.mult, ALU.add))
                    step(dve.tensor_tensor(tile_f, tile_f, used, ALU.add))
                step(dve.tensor_scalar(used, iota_slot[:, :], tile_end[:, EXPERTS - 1:EXPERTS], None, ALU.is_lt))
                step(dve.scalar_tensor_tensor(addr_f, addr_f, float(NULL_TILE), used, ALU.subtract, ALU.mult))
                step(dve.tensor_scalar(addr_f, addr_f, float(NULL_TILE), None, ALU.add))
                step(dve.tensor_copy(tile_addr[:, :], addr_f))
                step(dve.tensor_copy(tile_expert[:, :], tile_f))

        next_phase()
        U = MOE_UNROLL
        NU = NS // U
        carve = carver()
        carve(after_weights)
        xs = [carve(U, ROW) for _ in range(2)]
        xs_t = carve(U, KC, P)
        h = [carve(U, HID) for _ in range(2)]
        h_t = carve(U, HK, P)
        y = [carve(U, D) for _ in range(2)]
        gate_now = [carve(U) for _ in range(2)]
        dest_now = [carve(U, dt=I32) for _ in range(2)]
        m_stats = carve(U, 6)
        m_mom = carve(U, 2)
        m_rstd = carve(U)
        xs_in = [[sem(f"xs_in{j}_{u}") for u in range(U)] for j in range(2)]
        y_out = [[sem(f"y_out{j}_{u}") for u in range(U)] for j in range(2)]
        xst_psum, xst_ready, h_psum, h_ready = (
            sem("xst_psum"), sem("xst_ready"), sem("h_psum"), sem("h_ready"))
        m_stats_done, m_mom_done, m_eps_done, m_rstd_done = (
            sem("m_stats_done"), sem("m_mom_done"), sem("m_eps_done"), sem("m_rstd_done"))
        h_scaled, h_normed, act_ready = sem("h_scaled"), sem("h_normed"), sem("act_ready")
        ht_psum, ht_ready, y_psum, y_biased, y_ready = (
            sem("ht_psum"), sem("ht_ready"), sem("y_psum"), sem("y_biased"), sem("y_ready"))
        meta_ready = sem("meta_ready")

        def uses(m, j):
            return (m - j) // 2 if isinstance(m, int) else None

        def table(eng, which, t, m):
            _, values = nc.values_load_multi_w_load_instructions(
                t[0:1, m * U:(m + 1) * U] if isinstance(m, int) else t[0:1, bass.ds(m * U, U)],
                engines=[which], min_val=0, max_val=(EXPERTS - 1 if t is tile_expert else NULL_TILE),
                skip_runtime_bounds_check_because="both tables are made above, within these bounds")
            return values

        def pick(t, e):
            return t[:, bass.ds(e, 1)]

        def units(eng, unit):
            for m in range(3):
                unit(m, m % 2, m // 2)
            with eng.Fori(1, (NU - 2) // 2) as n:
                unit(n * 2 + 1, 1, n)
                unit(n * 2 + 2, 0, n + 1)
            for m in range(NU - 1 - (NU % 2), NU):
                unit(m, m % 2, m // 2)

        with nc.Block() as block:
            @block.sync
            def _(sp):
                def unit(m, j, before):
                    addr = table(sp, mybir.EngineType.SP, tile_addr, m)
                    for u in range(U):
                        if not (isinstance(m, int) and m < 2):
                            sp.wait_ge(xst_psum, m * U - (2 * U - 1 - u))
                            apart(sp)
                            sp.wait_ge(meta_ready, m * 2 - 2)
                            apart(sp)
                        sp.dma_start(xs[j][:, u, :], slots[bass.ds(addr[u] * P, P), :]).then_inc(xs_in[j][u], 16)
                units(sp, unit)

            @block.gpsimd
            def _(pool):
                def scatter(m, j, before):
                    for u in range(U):
                        pool.wait_ge(y_ready, m * U + (u + 1))
                        apart(pool)
                        pool.indirect_dma_start(
                            out=pair_out[:, :], out_offset=bass.IndirectOffsetOnAxis(
                                ap=dest_now[j][:, u:u + 1], axis=0),
                            in_=y[j][:, u, :], in_offset=None, bounds_check=2 * T - 1, oob_is_err=False)\
                            .then_inc(y_out[j][u], 16)

                def unit(m, j, before):
                    for u in range(U):
                        pool.wait_ge(xs_in[j][u], before * 16 + 16)
                        if not (isinstance(m, int) and m < 2):
                            pool.wait_ge(y_out[j][u], before * 16)
                    apart(pool)
                    pool.tensor_copy(dest_now[j], xs[j][:, :, D + 1]).then_inc(meta_ready, 1)
                    pool.tensor_copy(gate_now[j], xs[j][:, :, D]).then_inc(meta_ready, 1)
                    pool.wait_ge(m_mom_done, m * U + U)
                    apart(pool)
                    pool.tensor_scalar(m_rstd, m_mom[:, :, 1], EPS, None, ALU.add).then_inc(m_eps_done, 1)
                    pool.wait_ge(m_eps_done, m + 1)
                    pool.tensor_tensor(m_rstd, m_rstd, exponents[:, 0:U], ALU.pow).then_inc(m_rstd_done, 1)
                    if not (isinstance(m, int) and m < 1):
                        scatter(m - 1, 1 - j, None)
                units(pool, unit)
                scatter(NU - 1, (NU - 1) % 2, None)
                for j in range(2):
                    for u in range(U):
                        pool.wait_ge(y_out[j][u], 16 * (NU // 2 + (NU % 2 and j == 0)))

            @block.tensor
            def _(pe):
                def transpose_in(m, j, before):
                    for u in range(U):
                        pe.wait_ge(xs_in[j][u], before * 16 + 16)
                        if not (isinstance(m, int) and m < 1):
                            pe.wait_ge(h_ready, m * U - (U - 1 - u))
                        for c in range(KC):
                            ins = pe.transpose(ps[u][:, c * P:(c + 1) * P], xs[j][:, u, c * P:(c + 1) * P],
                                               ident[:, :])
                        ins.then_inc(xst_psum, 1)

                def up(m):
                    e = table(pe, mybir.EngineType.PE, tile_expert, m)
                    for u in range(U):
                        pe.wait_ge(xst_ready, m * U + (u + 1))
                        for c in range(KC):
                            ins = pe.matmul(ps[u][:, :], xs_t[:, u, c, :],
                                            pick(w1_sb, e[u])[:, :, c, :].rearrange("p e n -> p (e n)"),
                                            start=(c == 0), stop=(c == KC - 1))
                        ins.then_inc(h_psum, 1)

                def down(m, j):
                    e = table(pe, mybir.EngineType.PE, tile_expert, m)
                    for u in range(U):
                        pe.wait_ge(act_ready, m * U + (u + 1))
                        if not (isinstance(m, int) and m < 1):
                            pe.wait_ge(y_biased, m * U - (U - 1 - u))
                        for c in range(HK):
                            ins = pe.transpose(ps[4 + u][:, c * P:(c + 1) * P], h[j][:, u, c * P:(c + 1) * P],
                                               ident[:, :])
                        ins.then_inc(ht_psum, 1)
                    for u in range(U):
                        pe.wait_ge(ht_ready, m * U + (u + 1))
                        for c in range(HK):
                            ins = pe.matmul(ps[4 + u][:, 0:D], h_t[:, u, c, :],
                                            pick(w2_sb, e[u])[:, :, c, :].rearrange("p e n -> p (e n)"),
                                            start=(c == 0), stop=(c == HK - 1))
                        ins.then_inc(y_psum, 1)

                def unit(m, j, before):
                    up(m)
                    if not (isinstance(m, int) and m == NU - 1):
                        transpose_in(m + 1, 1 - j, before + j)
                    if not (isinstance(m, int) and m < 1):
                        down(m - 1, 1 - j)
                transpose_in(0, 0, 0)
                units(pe, unit)
                down(NU - 1, (NU - 1) % 2)

            @block.scalar
            def _(act):
                def inputs(m):
                    for u in range(U):
                        act.wait_ge(xst_psum, m * U + (u + 1))
                        act.activation(xs_t[:, u, :, :].rearrange("p c n -> p (c n)"), ps[u][:, 0:D], ACT.Copy)\
                           .then_inc(xst_ready, 1)

                def hidden(m):
                    for u in range(U):
                        act.wait_ge(ht_psum, m * U + (u + 1))
                        act.activation(h_t[:, u, :, :].rearrange("p c n -> p (c n)"), ps[4 + u][:, :], ACT.Copy)\
                           .then_inc(ht_ready, 1)

                def outputs(m, j):
                    for u in range(U):
                        act.wait_ge(y_biased, m * U + (u + 1))
                        act.wait_ge(meta_ready, m * 2 + 2)
                        act.activation(y[j][:, u, :], y[j][:, u, :], ACT.Copy, scale=gate_now[j][:, u:u + 1])\
                           .then_inc(y_ready, 1)

                def unit(m, j, before):
                    if not (isinstance(m, int) and m == NU - 1):
                        inputs(m + 1)
                    if not (isinstance(m, int) and m < 1):
                        hidden(m - 1)
                    for u in range(U):
                        act.wait_ge(h_normed, m * U + (u + 1))
                        act.activation(h[j][:, u, :], h[j][:, u, :], ACT.Gelu).then_inc(act_ready, 1)
                    if not (isinstance(m, int) and m < 1):
                        outputs(m - 1, 1 - j)
                inputs(0)
                units(act, unit)
                hidden(NU - 1)
                outputs(NU - 1, (NU - 1) % 2)

            @block.vector
            def _(dve):
                def outputs(m, j, e, before):
                    for u in range(U):
                        dve.wait_ge(y_psum, m * U + (u + 1))
                        if not (isinstance(m, int) and m < 2):
                            dve.wait_ge(y_out[j][u], before * 16)
                        dve.tensor_tensor(y[j][:, u, :].unsqueeze(1), ps[4 + u][:, 0:D].unsqueeze(1),
                                          pick(b2_sb, e[u]), ALU.add).then_inc(y_biased, 1)

                def unit(m, j, before):
                    e = table(dve, mybir.EngineType.DVE, tile_expert, m)
                    hu = lambda u: h[j][:, u, :].unsqueeze(1)
                    for u in range(U):
                        dve.wait_ge(h_psum, m * U + (u + 1))
                        if not (isinstance(m, int) and m < 2):
                            dve.wait_ge(ht_psum, m * U - (2 * U - 1 - u))
                        dve.tensor_tensor(hu(u), ps[u][:, :].unsqueeze(1), pick(b1_sb, e[u]), ALU.add)\
                           .then_inc(h_ready, 1)
                    for u in range(U):
                        dve.wait_ge(h_ready, m * U + (u + 1))
                        dve.bn_stats(m_stats[:, u, :], h[j][:, u, :]).then_inc(m_stats_done, 1)
                    for u in range(U):
                        dve.wait_ge(m_stats_done, m * U + (u + 1))
                        apart(dve)
                        dve.bn_aggr(m_mom[:, u, :], m_stats[:, u, :]).then_inc(m_mom_done, 1)
                    for u in range(U):
                        dve.wait_ge(m_mom_done, m * U + (u + 1))
                        dve.scalar_tensor_tensor(hu(u), hu(u), m_mom[:, u, 0:1], pick(g1_sb, e[u]),
                                                 ALU.subtract, ALU.mult).then_inc(h_scaled, 1)
                    dve.wait_ge(m_rstd_done, m + 1)
                    for u in range(U):
                        dve.wait_ge(h_scaled, m * U + (u + 1))
                        dve.scalar_tensor_tensor(hu(u), hu(u), m_rstd[:, u:u + 1], pick(be1_sb, e[u]),
                                                 ALU.mult, ALU.add).then_inc(h_normed, 1)
                    if not (isinstance(m, int) and m < 1):
                        e = table(dve, mybir.EngineType.DVE, tile_expert, m - 1)
                        outputs(m - 1, 1 - j, e, before - 1 + j)
                units(dve, unit)
                e = table(dve, mybir.EngineType.DVE, tile_expert, NU - 1)
                outputs(NU - 1, (NU - 1) % 2, e, (NU - 1) // 2)

        next_phase()
        carve = carver()
        SETS = 2
        ya = [carve(G, D) for _ in range(SETS)]
        yb = [carve(G, D) for _ in range(SETS)]
        res = [carve(G, D) for _ in range(SETS)]
        xfc = carve(G, D)
        mix = carve(G, D)
        z = [carve(G, D) for _ in range(SETS)]
        g_sb = carve(D)
        b_sb = carve(D)
        shift = carve(G)
        ln_in = sem("ln_in")
        ya_in, yb_in, res_in = ([sem(f"{n}_in{j}") for j in range(SETS)] for n in ("ya", "yb", "res"))
        out_stored = [sem(f"out_stored{j}", FREE) for j in range(SETS)]
        xf_again, mixed = sem("xf_again"), sem("mixed")
        mix_done = sem("mix_done", FREE)
        stats_d, moments_d, rstd_d = sem("stats_d"), sem("moments_d"), sem("rstd_d")
        eps_d, shift_done, z_normed, z_scaled = sem("eps_d"), sem("shift_done"), sem("z_normed"), sem("z_scaled")
        res_ready, out_ready = sem("res_ready"), sem("out_ready", FREE)
        y_rows = pair_out.rearrange("(k s p) d -> k s p d", k=2, p=P)
        with nc.Block() as block:
            @block.sync
            def _(sp):
                sp.dma_start(g_sb, ln_g.partition_broadcast(P)).then_inc(ln_in, 16)
                sp.dma_start(b_sb, ln_b.partition_broadcast(P)).then_inc(ln_in, 16)

                def load(g, j):
                    load_group(sp, res[j], x2_dram, g, res_in[j])
                    load_group(sp, ya[j], y_rows[0], g, ya_in[j])
                    load_group(sp, yb[j], y_rows[1], g, yb_in[j])
                for g in range(SETS):
                    load(g, g)
                with sp.Fori(0, NG // SETS - 1) as n:
                    for j in range(SETS):
                        sp.wait_ge(out_ready, n * SETS + (j + 1 + FREE))
                        apart(sp)
                        load(n * SETS + (j + SETS), j)

            @block.gpsimd
            def _(pool):
                pool.wait_ge(ln_in, 32)
                with pool.Fori(0, NG // SETS) as n:
                    for j in range(SETS):
                        g = n * SETS + j
                        pool.wait_ge(xf_again, n * (SETS * G) + (j + 1) * G)
                        pool.wait_ge(res_in[j], n * 32 + 32)
                        pool.tensor_tensor(res[j], res[j], b_sb.unsqueeze(1).to_broadcast([P, G, D]), ALU.add)\
                            .then_inc(res_ready, 1)
                        inverse_deviation(pool, g, moments_d, eps_d, rstd_d)

            @block.scalar
            def _(act):
                with act.Fori(0, NG // SETS) as n:
                    for j in range(SETS):
                        g = n * SETS + j
                        act.wait_ge(res_in[j], n * 32 + 32)
                        act.wait_ge(mix_done, n * SETS + (j + FREE))
                        apart(act)
                        for b in range(G):
                            at = n * (SETS * G) + (j * G + b)
                            act.activation(xfc[:, b, :], res[j][:, b, :], ACT.Identity,
                                           bias=xf_scale[:, 1, bass.ds(at, 1)],
                                           scale=xf_scale[:, 0, bass.ds(at, 1)]).then_inc(xf_again, 1)
                        act.wait_ge(shift_done, n * SETS + (j + 1))
                        act.wait_ge(out_stored[j], n * 16 + FREE)
                        for b in range(G):
                            act.activation(z[j][:, b, :], mix[:, b, :], ACT.Identity, bias=shift[:, b:b + 1],
                                           scale=rstd[:, b:b + 1]).then_inc(z_normed, 1)
                        act.wait_ge(out_ready, n * SETS + (j + 1 + FREE))
                        apart(act)
                        act.dma_start(out[bass.ds(g * G, G)].rearrange("g p d -> p g d"), z[j])\
                           .then_inc(out_stored[j], 16)
                for j in range(SETS):
                    act.wait_ge(out_stored[j], 16 * (NG // SETS) + FREE)

            @block.vector
            def _(dve):
                dve.wait_ge(ln_in, 32)
                with dve.Fori(0, NG // SETS) as n:
                    for j in range(SETS):
                        g = n * SETS + j
                        dve.wait_ge(ya_in[j], n * 32 + 32)
                        dve.wait_ge(yb_in[j], n * 32 + 32)
                        dve.tensor_tensor(ya[j], ya[j], yb[j], ALU.add).then_inc(mixed, 1)
                        dve.wait_ge(mixed, n * SETS + (j + 1))
                        dve.wait_ge(xf_again, n * (SETS * G) + (j + 1) * G)
                        dve.tensor_tensor(mix, ya[j], xfc, ALU.add).then_inc(mix_done, 1)
                        dve.wait_ge(mix_done, n * SETS + (j + 1 + FREE))
                        for b in range(G):
                            dve.bn_stats(stats[:, b, :], mix[:, b, :]).then_inc(stats_d, 1)
                        for b in range(G):
                            dve.wait_ge(stats_d, n * (SETS * G) + (j * G + b + 1))
                            apart(dve)
                            dve.bn_aggr(moments[:, b, :], stats[:, b, :]).then_inc(moments_d, 1)
                        dve.wait_ge(rstd_d, n * SETS + (j + 1))
                        dve.scalar_tensor_tensor(shift, moments[:, :, 0], -1.0, rstd[:, :], ALU.mult, ALU.mult)\
                           .then_inc(shift_done, 1)
                        dve.wait_ge(z_normed, n * (SETS * G) + (j + 1) * G)
                        dve.tensor_tensor(z[j], z[j], g_sb.unsqueeze(1).to_broadcast([P, G, D]), ALU.mult)\
                           .then_inc(z_scaled, 1)
                        dve.wait_ge(z_scaled, n * SETS + (j + 1))
                        dve.wait_ge(res_ready, n * SETS + (j + 1))
                        dve.tensor_tensor(z[j], z[j], res[j], ALU.add).then_inc(out_ready, 1)


def kernel(**inputs):
    import numpy as np
    import concourse.bacc as bacc
    from concourse import mybir as mb
    from concourse.bass_utils import run_bass_kernel_spmd

    a = {k: np.asarray(v) for k, v in inputs.items()}
    lay = np.ascontiguousarray
    arrays = {
        "x": a["x"],
        "ctx_rows": a["ctx_1024"],
        "ctx_cols": lay(a["ctx_1024"].transpose(0, 2, 1)),
        "w_qkv": lay(np.concatenate([a["L0_attn_wq"].T, a["L0_attn_wv"].T, a["L0_attn_wk"].T], axis=1)),
        "b_qv": lay(np.concatenate([a["L0_attn_bq"], a["L0_attn_bv"]])),
        "b_k": a["L0_attn_bk"],
        "w_o": lay(a["L0_attn_wo"].T),
        "b_o": a["L0_attn_bo"],
        "gate_w": a["L0_ffn_gate_w"],
        "w1": a["L0_ffn_w1"],
        "b1": a["L0_ffn_b1"],
        "ln1_g": a["L0_ffn_ln1_g"],
        "ln1_b": a["L0_ffn_ln1_b"],
        "w2": a["L0_ffn_w2"],
        "b2": a["L0_ffn_b2"],
        "ln_g": a["L0_ffn_ln_g"],
        "ln_b": a["L0_ffn_ln_b"],
    }
    nc = bacc.Bacc("TRN2", target_bir_lowering=False, num_devices=1)
    aps = [nc.dram_tensor(f"{k}_dram", v.shape, mb.dt.from_np(v.dtype), kind="ExternalInput").ap()
           for k, v in arrays.items()]
    out = nc.dram_tensor("out_dram", a["x"].shape, mb.dt.float32, kind="ExternalOutput").ap()
    decoder_layer(nc, *aps, out)
    r = run_bass_kernel_spmd(nc, [{f"{k}_dram": v for k, v in arrays.items()}], core_ids=[0])
    return r.results[0]["out_dram"]
```

```python
from contextlib import ExitStack

import concourse.bass as bass
from concourse import mybir

F32 = mybir.dt.float32
BF16 = mybir.dt.bfloat16
I32 = mybir.dt.int32
U32 = mybir.dt.uint32
ALU = mybir.AluOpType
ACT = mybir.ActivationFunctionType
AX = mybir.AxisListType

P = 128
D = 256
KC = D // P
HEADS = 16
DK = D // HEADS
HC = HEADS // KC
ROW = D + 2
TOP = 10
MIN_TOP = 3
HU = HC * TOP
G = 8
EXPERTS = 8
HID = 512
HK = HID // P
EPS = 1e-5
BIG = 1e30
MAGIC = 12582912.0
MOE_UNROLL = 4
HOP = 7
FREE = 16
ROWS = 8


def decoder_layer(nc, x, ctx_rows, ctx_cols, w_qkv, b_qv, b_k, w_o, b_o, gate_w, w1, b1, ln1_g, ln1_b,
                  w2, b2, ln_g, ln_b, out):
    B = x.shape[0]
    NG = B // G
    NS = 2 * B + EXPERTS
    NS += -NS % (2 * MOE_UNROLL)
    T = B * P
    REGION = T + P
    NULL_TILE = EXPERTS * REGION // P
    GATE_STEPS = 19
    PLACED = 14
    x1_dram = nc.dram_tensor("x1_scratch", [B, P, D], F32)
    dist_dram = nc.dram_tensor("dist_scratch", [B, P, P], F32)
    x2_dram = nc.dram_tensor("x2_scratch", [B, P, D], F32)
    slots = nc.dram_tensor("slots_scratch", [EXPERTS * REGION + P, ROW], F32)
    pair_out = nc.dram_tensor("pair_out_scratch", [2 * T, D], F32)

    es = ExitStack()
    with es:
        def sb(name, shape, dt=F32):
            return es.enter_context(nc.sbuf_tensor(name, shape, dt))

        phase = []

        def sem(name, start=0):
            phase.append(nc.alloc_semaphore(name=name))
            if start:
                nc.gpsimd.sem_inc(phase[-1], start)
            return phase[-1]

        def next_phase():
            nc.clear_and_free_semaphores(phase)
            nc.all_engine_barrier()
            phase.clear()

        def apart(eng):
            eng.nop(nofuse=True)

        ps = [es.enter_context(nc.psum_tensor(f"bank{i}", [P, 512], F32)) for i in range(8)]

        ident = sb("ident", [P, P])
        iota_f1 = sb("iota_f1", [P, P])
        iota_p1 = sb("iota_p1", [P, 1])
        iota_2j = sb("iota_2j", [P, P])
        iota_256 = sb("iota_256", [P, 2 * P])
        iota_small = sb("iota_small", [P, TOP])
        iota_slot = sb("iota_slot", [P, NS])
        head_block = sb("head_block", [P, KC, HC, TOP])
        head_block2 = sb("head_block2", [HU, HC, DK])
        seq_rows = sb("seq_rows", [P, G, P], BF16)
        first_head = sb("first_head", [P, P], BF16)
        head_of_row = sb("head_of_row", [P, HEADS])
        neg_half = sb("neg_half", [P, P])
        before = sb("before", [P, P], BF16)
        ones_bf = sb("ones_bf", [P, P], BF16)
        tiny = sb("tiny", [P, 1])
        ones8 = sb("ones8", [P, EXPERTS])
        codes = sb("codes", [B, P + 1])
        row_code = sb("row_code", [P, 2, B])
        xf_scale = sb("xf_scale", [P, 2, B])
        tile_expert = sb("tile_expert", [P, NS], I32)
        tile_addr = sb("tile_addr", [P, NS], I32)
        from_8 = sb("from_8", [P, G, EXPERTS])
        stats = sb("stats", [P, G, 6])
        moments = sb("moments", [P, G, 2])
        rstd = sb("rstd", [P, G])
        norm = (stats, moments, rstd)
        exponents = sb("exponents", [P, G + 1])

        ARENA = 46400
        arena = sb("arena", [P, ARENA])

        def carver():
            at = [0]

            def carve(*shape, dt=F32, rows=P):
                n = 1
                for s in shape:
                    n *= s
                words = n if dt != BF16 else (n + 1) // 2
                v = arena[0:rows, at[0]:at[0] + words]
                at[0] += words
                assert at[0] <= ARENA, at[0]
                if dt != F32:
                    v = v.bitcast(dt)
                if len(shape) > 1:
                    names = "abcd"[:len(shape)]
                    v = v.rearrange(f"p ({' '.join(names)}) -> p {' '.join(names)}",
                                    **dict(zip(names, shape)))
                return v
            carve.at = lambda: at[0]
            return carve

        carve = carver()
        x_in = carve(G, D)
        x_res = carve(G, D)
        xn = carve(G, D)
        yn = carve(G, D)
        xn_t = carve(G, KC, P)
        q_buf = carve(G, D)
        v_buf = carve(G, D)
        k_t = carve(G, KC, P)
        c1 = carve(G, D)
        c2 = carve(G, D)
        c3 = carve(G, D)
        sel = carve(G, KC * HU)
        q_sel = carve(G, KC * HU)
        a_t = carve(G, KC * HU)
        sel_t = carve(G, KC, P, rows=HU)
        dist = carve(G, P)
        ctx_t = carve(G, KC, P)
        ctx_row = carve(G, D)
        w_qkv_sb = carve(KC, 3 * D)
        w_o_sb = carve(KC, D)
        b_qv_sb = carve(2 * D)
        b_k_sb = carve(KC)
        b_o_sb = carve(D)
        sum_q = carve(P)
        max_q = carve(P)
        mean_q = carve(P)
        sum_sq = carve(P)
        sum_e = carve(P)
        rec_e = carve(P)
        norm_next = (carve(G, 6), carve(G, 2), carve(G))
        ctx_norm = carve(G)
        sum_pl = carve(P)
        mean_sq = carve(P)
        l2 = carve(P)
        score = carve(P)
        score_t = carve(P)
        score_u = carve(P)
        t_stats = carve(6)
        t_mom = carve(2)
        t_a = carve(1)
        t_b = carve(1)
        t_c = carve(1)
        t_dev = carve(1)
        factor = carve(2, dt=BF16)[:, 0:1]
        top8 = carve(2, 8)
        idx_u = carve(2, 8, dt=U32)
        idx_f = carve(2 * 8)
        kept = carve(TOP)
        idx1 = carve(TOP)
        idx_rows = carve(HEADS, TOP, dt=BF16)
        idx_cols = carve(KC, G, rows=HU)
        neg_max = carve(G, KC, rows=HU)
        e_sum = carve(G, KC, rows=HU)
        e_rec = carve(G, KC, rows=HU)

        def load_group(eng, tile, dram, g, done, pattern="g p d -> p g d"):
            for half in range(2):
                eng.dma_start(tile[:, half * G // 2:(half + 1) * G // 2],
                              dram[bass.ds(g * G + half * G // 2, G // 2)].rearrange(pattern, **(
                                  {"p": P} if "(" in pattern else {}))).then_inc(done, 16)

        made = sem("const_made")
        weights_in, first_x_in = sem("attn_weights_in"), sem("first_x_in")
        with nc.Block() as block:
            @block.sync
            def _(sp):
                sp.dma_start(w_qkv_sb, w_qkv.rearrange("(c p) n -> p c n", p=P)).then_inc(weights_in, 16)
                sp.dma_start(w_o_sb, w_o.rearrange("(c p) n -> p c n", p=P)).then_inc(weights_in, 16)
                sp.dma_start(b_qv_sb, b_qv.partition_broadcast(P)).then_inc(weights_in, 16)
                sp.dma_start(b_o_sb, b_o.partition_broadcast(P)).then_inc(weights_in, 16)
                with nc.allow_non_contiguous_dma(reason="256 biases, one per partition"):
                    sp.dma_start(b_k_sb, b_k.rearrange("(c p) -> p c", p=P)).then_inc(weights_in, 16)
                load_group(sp, x_in, x, 0, first_x_in)
                sp.wait_ge(weights_in, 16 * 5)
                sp.wait_ge(first_x_in, 32)

            @block.gpsimd
            def _(pool):
                n = 0

                def step(ins):
                    nonlocal n
                    ins.then_inc(made, 1)
                    n += 1
                    pool.wait_ge(made, n)

                def iota(t, pattern, base, mult):
                    step(pool.iota(t, pattern=pattern, base=base, channel_multiplier=mult,
                                   allow_small_or_imprecise_dtypes=True))

                def keep(t, pattern, base, mult, op, fill):
                    step(pool.affine_select(out=t, in_=t, pattern=pattern, compare_op=op, fill=fill,
                                            base=base, channel_multiplier=mult))

                iota(iota_slot[:, :], [[1, NS]], 0, 0)
                iota(iota_f1[:, :], [[1, P]], 1, 0)
                iota(iota_p1[:, :], [[1, 1]], 1, 1)
                iota(iota_2j[:, :], [[2, P]], 0, 0)
                iota(iota_256[:, :], [[1, 2 * P]], 1, 0)
                iota(iota_small[:, :], [[1, TOP]], 0, 0)
                iota(from_8[:, :, :], [[0, G], [-1, EXPERTS]], EXPERTS, 0)
                step(pool.memset(ident[:, :], 0.0))
                keep(ident[:, :], [[-1, P]], 0, 1, ALU.not_equal, 1.0)
                step(pool.memset(head_block[:, :, :, :], float(DK) ** -0.5))
                for c in range(KC):
                    v = head_block[:, c, :, :]
                    keep(v, [[-DK, HC], [0, TOP]], 0, 1, ALU.is_ge, 0.0)
                    keep(v, [[DK, HC], [0, TOP]], DK - 1, -1, ALU.is_ge, 0.0)
                step(pool.memset(head_block2[:, :, :], 1.0))
                keep(head_block2[:, :, :], [[-TOP, HC], [0, DK]], 0, 1, ALU.is_ge, 0.0)
                keep(head_block2[:, :, :], [[TOP, HC], [0, DK]], TOP - 1, -1, ALU.is_ge, 0.0)
                step(pool.memset(seq_rows[:, :, :], 1.0))
                keep(seq_rows[:, :, :], [[-HEADS, G], [0, P]], 0, 1, ALU.is_ge, 0.0)
                keep(seq_rows[:, :, :], [[HEADS, G], [0, P]], HEADS - 1, -1, ALU.is_ge, 0.0)
                step(pool.memset(first_head[:, :], 1.0))
                keep(first_head[:, :], [[-HEADS, G], [0, HEADS]], 0, 1, ALU.is_equal, 0.0)
                step(pool.memset(before[:, :], 1.0))
                keep(before[:, :], [[1, P]], 0, -1, ALU.is_gt, 0.0)
                step(pool.memset(ones_bf[:, :], 1.0))
                step(pool.memset(neg_half[:, :], -0.5))
                step(pool.memset(tiny[:, :], 1e-9))
                step(pool.memset(ones8[:, :], 1.0))
                step(pool.memset(exponents[:, 0:G], -0.5))
                step(pool.memset(exponents[:, G:G + 1], 0.5))

            @block.vector
            def _(dve):
                dve.wait_ge(made, 9)
                dve.tensor_reduce(head_of_row[:, :], ident[:, :].rearrange("p (s h) -> p h s", h=HEADS),
                                  AX.X, ALU.max).then_inc(sem("head_of_row_made"), 1)

        next_phase()
        BANKS = 4
        e_buf = carve(G, KC, P)
        o_sel = carve(G, KC, P)
        m_t = carve(G, KC, P)

        def bank(side, b):
            return ps[side * BANKS + b % BANKS][:, 0:D]

        def operands_and_bank(pe, g, b, ready, done, done_start=0):
            if b < BANKS:
                pe.wait_ge(ready, g * G + (b + BANKS + 1))
            else:
                pe.wait_ge(ready, g * G + (b + 1))
                pe.wait_ge(done, g * G + (b - BANKS + 1 + done_start))

        x_loaded, ctx_loaded = sem("x_loaded", 32), sem("ctx_loaded")
        x1_stored, dist_stored = sem("x1_stored", FREE), sem("dist_stored", FREE)
        stats_a, moments_a, rstd_a, xn_ready = sem("stats_a"), sem("moments_a"), sem("rstd_a"), sem("xn_ready")
        x_res_ready = sem("x_res_ready")
        xnt_psum, xnt_ready = sem("xnt_psum"), sem("xnt_ready")
        q_psum, q_ready = sem("q_psum"), sem("q_ready")
        v_psum, v_ready = sem("v_psum"), sem("v_ready")
        x_res_loaded = sem("x_res_loaded")
        kt_psum, kt_ready = sem("kt_psum"), sem("kt_ready")
        sum_q_done, max_q_done, mean_q_done = sem("sum_q_done"), sem("max_q_done"), sem("mean_q_done")
        centred, shifted, expd, squared = sem("centred"), sem("shifted"), sem("expd"), sem("squared")
        sum_sq_done, rec_e_done, sum_e_done = sem("sum_sq_done"), sem("rec_e_done"), sem("sum_e_done")
        prob_done, logp_done, plogp_done = sem("prob_done"), sem("logp_done"), sem("plogp_done")
        score_step = sem("score_step")
        l2_in_done, l2_done = sem("l2_in_done"), sem("l2_done")
        score_ready, score_psum = sem("score_ready"), sem("score_psum")
        top_step = sem("top_step")
        sample_var = sem("sample_var")
        eps_a, eps_b = sem("eps_a"), sem("eps_b")
        variance_ready, deviation_ready = sem("variance_ready"), sem("deviation_ready")
        factor_ready, keep_psum = sem("factor_ready"), sem("keep_psum")
        idx_rows_ready, idx_cols_psum, idx_cols_ready = (
            sem("idx_rows_ready"), sem("idx_cols_psum"), sem("idx_cols_ready"))
        sel_t_ready = sem("sel_t_ready")
        idx_psum, sel_ready = sem("idx_psum"), sem("sel_ready")
        qs_psum, qs_ready = sem("qs_psum"), sem("qs_ready")
        s_psum, max_ready, e_ready = sem("s_psum"), sem("max_ready"), sem("e_ready")
        at_psum, at_ready = sem("at_psum"), sem("at_ready")
        o_psum, e_rec_done, o_ready = sem("o_psum"), sem("e_rec_done"), sem("o_ready")
        mt_psum, mt_ready = sem("mt_psum"), sem("mt_ready")
        attn_psum, x1_ready = sem("attn_psum"), sem("x1_ready")
        stats_b, moments_b, rstd_b, yn_ready = (
            sem("stats_b"), sem("moments_b"), sem("rstd_b"), sem("yn_ready", FREE))
        ynt_psum, ynt_ready = sem("ynt_psum"), sem("ynt_ready")
        norm_ready, ctx_row_loaded = sem("norm_ready", FREE), sem("ctx_row_loaded")
        sem_idx1 = sem("idx1_done")
        dist_psum, dist_sq_ready, dist_ready = sem("dist_psum"), sem("dist_sq_ready", FREE), sem("dist_ready", FREE)

        def moments_of(dve, g, src, s_stats, s_mom, before_tile=None, norm=norm):
            stats, moments, _ = norm
            for b in range(G):
                if before_tile:
                    before_tile(b)
                dve.bn_stats(stats[:, b, :], src(b)).then_inc(s_stats, 1)
            for b in range(G):
                dve.wait_ge(s_stats, g * G + (b + 1))
                apart(dve)
                dve.bn_aggr(moments[:, b, :], stats[:, b, :]).then_inc(s_mom, 1)

        def normalise(dve, g, src, dst, s_rstd, s_out, norm=norm):
            _, moments, rstd = norm
            dve.wait_ge(s_rstd, g + 1)
            for b in range(G):
                dve.tensor_scalar(dst(b), src(b), moments[:, b, 0:1], rstd[:, b:b + 1],
                                  ALU.subtract, ALU.mult).then_inc(s_out, 1)

        def inverse_deviation(pool, g, s_mom, s_eps, s_rstd, norm=norm):
            _, moments, rstd = norm
            pool.wait_ge(s_mom, g * G + G)
            apart(pool)
            pool.tensor_scalar(rstd[:, 0:G], moments[:, :, 1], EPS, None, ALU.add).then_inc(s_eps, 1)
            pool.wait_ge(s_eps, g + 1)
            pool.tensor_tensor(rstd[:, 0:G], rstd[:, 0:G], exponents[:, 0:G], ALU.pow).then_inc(s_rstd, 1)

        def heads(t):
            return t.rearrange("p g (h d) -> p g h d", h=HEADS)

        def per_head(t):
            return t.rearrange("p (g h) -> p g h", g=G).unsqueeze(3).to_broadcast([P, G, HEADS, DK])

        def evacuate(eng, g, buf, bias, psum, done, seqs):
            for b in seqs:
                eng.wait_ge(psum, g * G + (b + 1))
                eng.tensor_tensor(buf[:, b, :], bank(0, b), bias, ALU.add).then_inc(done, 1)

        with nc.Block() as block:
            @block.sync
            def _(sp):
                def turn(k, n, following):
                    if k is not None:
                        sp.wait_ge(x1_stored, k * 16 + FREE)
                        apart(sp)
                        sp.wait_ge(yn_ready, k * G + FREE)
                        load_group(sp, x_res, x, k, x_res_loaded)
                        sp.wait_ge(norm_ready, k * G + FREE)
                        load_group(sp, ctx_row, ctx_rows, k, ctx_row_loaded)
                        sp.wait_ge(dist_ready, k + FREE)
                        load_group(sp, ctx_t, ctx_cols, k, ctx_loaded, "g (c p) n -> p g c n")
                    if n is not None:
                        sp.wait_ge(xn_ready, n * G + G)
                        apart(sp)
                        load_group(sp, x_in, x, following, x_loaded)
                    if k is not None:
                        seqs = bass.ds(k * G, G)
                        sp.wait_ge(x1_ready, k * G + G)
                        sp.dma_start(x1_dram[seqs].rearrange("g p d -> p g d"), x_res).then_inc(x1_stored, 16)
                        sp.wait_ge(dist_ready, k + (1 + FREE))
                        sp.dma_start(dist_dram[seqs].rearrange("g p d -> p g d"), dist)\
                          .then_inc(dist_stored, 16)
                turn(None, 0, 1)
                turn(None, 1, 2)
                with sp.Fori(0, NG - 2) as g:
                    following = sp.snap((g + 3) % NG)
                    turn(g, g + 2, following)
                turn(NG - 2, None, None)
                turn(NG - 1, None, None)
                sp.wait_ge(x_loaded, 32 * (NG + 1))
                sp.wait_ge(x1_stored, 16 * NG + FREE)
                sp.wait_ge(dist_stored, 16 * NG + FREE)

            @block.gpsimd
            def _(pool):

                def turn(f, k, n):
                    if f is not None:
                        q = heads(q_buf)
                        pool.wait_ge(mean_q_done, f + 1)
                        pool.tensor_tensor(heads(c1), q, per_head(mean_q), ALU.subtract).then_inc(centred, 1)
                        pool.wait_ge(max_q_done, f + 1)
                        pool.tensor_tensor(heads(c2), q, per_head(max_q), ALU.subtract).then_inc(shifted, 1)
                    if n is not None:
                        inverse_deviation(pool, n, moments_a, eps_a, rstd_a, norm_next)
                    if k is not None:
                        pool.wait_ge(x_res_loaded, k * 32 + 32)
                        pool.tensor_tensor(x_res, x_res, b_o_sb.unsqueeze(1).to_broadcast([P, G, D]), ALU.add)\
                            .then_inc(x_res_ready, 1)
                    if f is not None:
                        pool.wait_ge(rec_e_done, f + 1)
                        pool.tensor_tensor(heads(c2), heads(c2), per_head(rec_e), ALU.mult).then_inc(prob_done, 1)
                    if k is not None:
                        inverse_deviation(pool, k, moments_b, eps_b, rstd_b)
                    if f is not None:
                        pool.wait_ge(prob_done, f + 1)
                        pool.wait_ge(logp_done, f + 1)
                        pool.tensor_tensor(c3, c3, c2, ALU.mult).then_inc(plogp_done, 1)
                        pool.wait_ge(variance_ready, f + 1)
                        apart(pool)
                        pool.tensor_scalar(t_dev, t_mom[:, 1:2], P / (P - 1), None, ALU.mult)\
                            .then_inc(sample_var, 1)
                        pool.wait_ge(sample_var, f + 1)
                        pool.tensor_tensor(t_dev, t_dev, exponents[:, G:G + 1], ALU.pow)\
                            .then_inc(deviation_ready, 1)
                turn(None, None, 0)
                turn(0, None, 1)
                with pool.Fori(0, NG - 2) as g:
                    turn(g + 1, g, g + 2)
                turn(NG - 1, NG - 2, None)
                turn(None, NG - 1, None)

            @block.tensor
            def _(pe):
                flat_idx = idx_rows.rearrange("p h u -> p (h u)")

                def transposes(side, g, rows, ready, head, read, done):
                    for b in range(G):
                        pe.wait_ge(ready, g * G + (b + 1 + head))
                        if b >= BANKS:
                            pe.wait_ge(read, g * G + (b - BANKS + 1))
                        for c in range(KC):
                            ins = pe.transpose(bank(side, b)[:, c * P:(c + 1) * P], rows[:, b, c * P:(c + 1) * P],
                                               ident[:, :])
                        ins.then_inc(done, 1)

                def project_rows(g, column, ready, read, done):
                    for b in range(G):
                        operands_and_bank(pe, g, b, ready, read)
                        for c in range(KC):
                            ins = pe.matmul(bank(0, b), xn_t[:, b, c, :], w_qkv_sb[:, c, column:column + D],
                                            start=(c == 0), stop=(c == KC - 1))
                        ins.then_inc(done, 1)

                def distances(k, seqs):
                    for b in seqs:
                        operands_and_bank(pe, k, b, ynt_ready, dist_sq_ready, FREE)
                        for c in range(KC):
                            pe.matmul(bank(1, b)[:, 0:P], ctx_t[:, b, c, :], xn_t[:, b, c, :],
                                      start=(c == 0), stop=False)
                        for c in range(KC):
                            ins = pe.matmul(bank(1, b)[:, 0:P], neg_half[:, :], e_buf[:, b, c, :],
                                            start=False, stop=(c == KC - 1))
                        ins.then_inc(dist_psum, 1)

                def kept_queries(b):
                    pe.matmul(bank(1, b)[:, 0:KC * HU], seq_rows[:, b, :], flat_idx,
                              start=True, stop=True).then_inc(idx_psum, 1)

                def turn(f, k, n):
                    if k is not None:
                        for b in range(BANKS, G):
                            pe.wait_ge(sel_ready, k * G + (b - BANKS + 1))
                            kept_queries(b)
                        for b in range(G):
                            operands_and_bank(pe, k, b, sel_ready, qs_ready)
                            for c in range(KC):
                                ins = pe.matmul(bank(1, b)[:, c * HU:(c + 1) * HU], q_buf[:, b, c * P:(c + 1) * P],
                                                sel[:, b, c * HU:(c + 1) * HU], start=True, stop=True)
                            ins.then_inc(qs_psum, 1)
                    if f is not None:
                        project_rows(f, 0, xnt_ready, q_ready, q_psum)
                    if k is not None:
                        for b in range(G):
                            operands_and_bank(pe, k, b, qs_ready, e_ready)
                            for c in range(KC):
                                ins = pe.matmul(bank(1, b)[0:HU, c * P:(c + 1) * P],
                                                q_sel[:, b, c * HU:(c + 1) * HU], k_t[:, b, c, :],
                                                start=True, stop=True)
                            ins.then_inc(s_psum, 1)
                    if f is not None:
                        for b in range(G):
                            operands_and_bank(pe, f, b, q_ready, kt_ready)
                            for m in range(KC):
                                for c in range(KC):
                                    ins = pe.matmul(bank(0, b)[:, m * P:(m + 1) * P],
                                                    w_qkv_sb[:, c, 2 * D + m * P:2 * D + (m + 1) * P],
                                                    xn_t[:, b, c, :], start=(c == 0), stop=(c == KC - 1))
                            ins.then_inc(kt_psum, 1)
                    if k is not None:
                        for b in range(G):
                            operands_and_bank(pe, k, b, e_ready, at_ready)
                            for c in range(KC):
                                ins = pe.transpose(bank(1, b)[:, c * HU:(c + 1) * HU], e_buf[0:HU, b, c, :],
                                                   ident[0:HU, 0:HU])
                            ins.then_inc(at_psum, 1)
                        for b in range(G):
                            operands_and_bank(pe, k, b, at_ready, o_ready)
                            for c in range(KC):
                                ins = pe.matmul(bank(1, b)[0:HU, c * P:(c + 1) * P],
                                                a_t[:, b, c * HU:(c + 1) * HU],
                                                v_buf[:, b, c * P:(c + 1) * P], start=True, stop=True)
                            ins.then_inc(o_psum, 1)
                        pe.wait_ge(sel_t_ready, k + 1)
                        for b in range(G):
                            operands_and_bank(pe, k, b, o_ready, mt_ready)
                            for c in range(KC):
                                ins = pe.matmul(bank(1, b)[:, c * P:(c + 1) * P], o_sel[0:HU, b, c, :],
                                                sel_t[:, b, c, :], start=True, stop=True)
                            ins.then_inc(mt_psum, 1)
                        for b in range(G):
                            operands_and_bank(pe, k, b, mt_ready, x1_ready)
                            for c in range(KC):
                                ins = pe.matmul(bank(1, b), m_t[:, b, c, :], w_o_sb[:, c, :],
                                                start=(c == 0), stop=(c == KC - 1))
                            ins.then_inc(attn_psum, 1)
                    if f is not None:
                        project_rows(f, D, kt_ready, v_ready, v_psum)
                    if k is not None:
                        transposes(1, k, yn, yn_ready, FREE, ynt_ready, ynt_psum)
                        pe.wait_ge(ctx_loaded, k * 32 + 32)
                        distances(k, range(BANKS))
                    if f is not None:
                        pe.wait_ge(v_ready, f * G + G)
                        pe.wait_ge(score_ready, f + 1)
                        pe.transpose(bank(0, 0)[:, 0:P], score, ident[:, :]).then_inc(score_psum, 1)
                    if k is not None:
                        distances(k, range(BANKS, G))
                    if f is not None:
                        pe.wait_ge(factor_ready, f + 1)
                        pe.matmul(bank(0, 1)[:, 0:1], first_head[:, :], factor, start=True, stop=True)\
                          .then_inc(keep_psum, 1)
                        pe.wait_ge(idx_rows_ready, f + 1)
                        for c in range(KC):
                            ins = pe.matmul(bank(0, 2)[0:HU, c * G:(c + 1) * G], flat_idx[:, c * HU:(c + 1) * HU],
                                            seq_rows[:, :, 0], start=True, stop=True)
                        ins.then_inc(idx_cols_psum, 1)
                        if k is not None:
                            pe.wait_ge(dist_sq_ready, k * G + (G + FREE))
                        for b in range(BANKS):
                            kept_queries(b)
                        pe.wait_ge(idx_cols_ready, f + 1)
                    if n is not None:
                        transposes(0, n, xn, xn_ready, 0, xnt_ready, xnt_psum)
                turn(None, None, 0)
                turn(0, None, 1)
                with pe.Fori(0, NG - 2) as g:
                    turn(g + 1, g, g + 2)
                turn(NG - 1, NG - 2, None)
                turn(None, NG - 1, None)

            @block.scalar
            def _(act):

                def turn(f, k, n):
                    if k is not None:
                        for b in range(G):
                            act.wait_ge(max_ready, k * G + (b + 1))
                            for c in range(KC):
                                ins = act.activation(e_buf[0:HU, b, c, :], bank(1, b)[0:HU, c * P:(c + 1) * P],
                                                     ACT.Exp, bias=neg_max[:, b, c:c + 1],
                                                     accum_out=e_sum[:, b, c:c + 1])
                            ins.then_inc(e_ready, 1)
                    if f is not None:
                        for b in range(G):
                            act.wait_ge(kt_psum, f * G + (b + 1))
                            for c in range(KC):
                                ins = act.activation(k_t[:, b, c, :], bank(0, b)[:, c * P:(c + 1) * P],
                                                     ACT.Identity, bias=b_k_sb[:, c:c + 1])
                            ins.then_inc(kt_ready, 1)
                    if k is not None:
                        for b in range(G):
                            act.wait_ge(at_psum, k * G + (b + 1))
                            act.activation(a_t[:, b, :], bank(1, b)[:, 0:KC * HU], ACT.Copy).then_inc(at_ready, 1)
                    if f is not None:
                        act.wait_ge(centred, f + 1)
                        act.activation(c1, c1, ACT.Square).then_inc(squared, 1)
                        act.wait_ge(shifted, f + 1)
                        act.activation(c2, c2, ACT.Exp).then_inc(expd, 1)
                    if k is not None:
                        for b in range(G):
                            act.wait_ge(mt_psum, k * G + (b + 1))
                            act.activation(m_t[:, b, :, :].rearrange("p c n -> p (c n)"), bank(1, b), ACT.Copy)\
                               .then_inc(mt_ready, 1)
                    if f is not None:
                        act.wait_ge(prob_done, f + 1)
                        act.activation(c3, c2, ACT.Ln, bias=tiny[:, 0:1]).then_inc(logp_done, 1)
                    if k is not None:
                        act.wait_ge(ctx_row_loaded, k * 32 + 32)
                        for b in range(G):
                            act.activation(ctx_row[:, b, :], ctx_row[:, b, :], ACT.Square,
                                           accum_out=ctx_norm[:, b:b + 1]).then_inc(norm_ready, 1)
                        for b in range(G):
                            act.wait_ge(ynt_psum, k * G + (b + 1))
                            act.activation(xn_t[:, b, :, :].rearrange("p c n -> p (c n)"), bank(1, b), ACT.Copy)
                            act.activation(e_buf[:, b, :, :].rearrange("p c n -> p (c n)"), bank(1, b),
                                           ACT.Square).then_inc(ynt_ready, 1)
                    if f is not None:
                        act.wait_ge(l2_in_done, f + 1)
                        act.activation(l2, mean_sq, ACT.Sqrt).then_inc(l2_done, 1)
                    if k is not None:
                        act.wait_ge(norm_ready, k * G + (G + FREE))
                        act.wait_ge(dist_stored, k * 16 + FREE)
                        for b in range(G):
                            act.wait_ge(dist_psum, k * G + (b + 1))
                            act.activation(dist[:, b, :], bank(1, b)[:, 0:P], ACT.Relu,
                                           bias=ctx_norm[:, b:b + 1], scale=-2.0).then_inc(dist_sq_ready, 1)
                    if n is not None:
                        for b in range(G):
                            act.wait_ge(xnt_psum, n * G + (b + 1))
                            act.activation(xn_t[:, b, :, :].rearrange("p c n -> p (c n)"), bank(0, b), ACT.Copy)\
                               .then_inc(xnt_ready, 1)
                    if k is not None:
                        act.wait_ge(dist_sq_ready, k * G + (G + FREE))
                        act.activation(dist, dist, ACT.Sqrt).then_inc(dist_ready, 1)
                turn(None, None, 0)
                turn(0, None, 1)
                with act.Fori(0, NG - 2) as g:
                    turn(g + 1, g, g + 2)
                turn(NG - 1, NG - 2, None)
                turn(None, NG - 1, None)

            @block.vector
            def _(dve):
                head_grid = lambda t: t.rearrange("p (g h) -> p g h", g=G)

                def top_queries(f):
                    TS = 13
                    n = 0

                    def step(ins):
                        nonlocal n
                        ins.then_inc(top_step, 1)
                        n += 1
                        dve.wait_ge(top_step, f * TS + n)
                    dve.wait_ge(score_psum, f + 1)
                    step(dve.tensor_scalar(score_t, bank(0, 0)[:, 0:P], 0.5, None, ALU.mult))
                    step(dve.bn_stats(t_stats, score_t))
                    apart(dve)
                    dve.bn_aggr(t_mom, t_stats).then_inc(variance_ready, 1)
                    apart(dve)
                    step(dve.max(top8[:, 0, :], score_t))
                    apart(dve)
                    step(dve.match_replace(score_u, top8[:, 0, :], score_t, -3e38))
                    apart(dve)
                    step(dve.max(top8[:, 1, :], score_u))
                    apart(dve)
                    dve.max_index(idx_u[:, 0, :], top8[:, 0, :], score_t)
                    step(dve.max_index(idx_u[:, 1, :], top8[:, 1, :], score_u))
                    step(dve.tensor_copy(idx_f, idx_u.rearrange("p a b -> p (a b)")))
                    dve.wait_ge(variance_ready, f + 1)
                    step(dve.tensor_scalar(t_b, t_mom[:, 0:1], 1e-6, None, ALU.add))
                    step(dve.reciprocal(t_b, t_b))
                    dve.wait_ge(deviation_ready, f + 1)
                    step(dve.tensor_tensor(t_c, t_dev, t_b, ALU.mult))
                    step(dve.tensor_scalar(t_a, t_c, float(TOP), float(TOP), ALU.mult, ALU.min))
                    step(dve.tensor_scalar(t_b, t_a, float(MIN_TOP), MAGIC, ALU.max, ALU.add))
                    dve.tensor_scalar(factor, t_b, MAGIC, None, ALU.subtract).then_inc(factor_ready, 1)
                    dve.wait_ge(keep_psum, f + 1)
                    step(dve.tensor_scalar(kept, iota_small[:, :], bank(0, 1)[:, 0:1], None, ALU.is_lt))
                    assert n == TS
                    dve.scalar_tensor_tensor(idx1, idx_f[:, 0:TOP], 1.0, kept, ALU.add, ALU.mult)\
                       .then_inc(sem_idx1, 1)
                    dve.wait_ge(sem_idx1, f + 1)
                    dve.tensor_tensor(idx_rows, idx1.unsqueeze(1).to_broadcast([P, HEADS, TOP]),
                                      head_of_row[:, :].unsqueeze(2).to_broadcast([P, HEADS, TOP]), ALU.mult)\
                       .then_inc(idx_rows_ready, 1)
                    dve.wait_ge(idx_cols_psum, f + 1)
                    dve.tensor_copy(idx_cols, bank(0, 2)[0:HU, 0:KC * G].rearrange("p (c g) -> p c g", c=KC))\
                       .then_inc(idx_cols_ready, 1)

                def turn(f, k, n):
                    if k is not None:
                        for b in range(G):
                            dve.wait_ge(idx_psum, k * G + (b + 1))
                            dve.tensor_scalar(sel[:, b, :], bank(1, b)[:, 0:KC * HU], iota_p1[:, 0:1], None,
                                              ALU.is_equal).then_inc(sel_ready, 1)
                        for b in range(G):
                            dve.wait_ge(qs_psum, k * G + (b + 1))
                            dve.tensor_tensor(q_sel[:, b, :], bank(1, b)[:, 0:KC * HU],
                                              head_block[:, :, :, :].rearrange("p c h u -> p (c h u)"),
                                              ALU.mult).then_inc(qs_ready, 1)
                        dve.wait_ge(idx_cols_ready, k + 1)
                        for c in range(KC):
                            ins = dve.tensor_tensor(sel_t[:, :, c, :],
                                                    iota_f1[0:HU, :].unsqueeze(1).to_broadcast([HU, G, P]),
                                                    idx_cols[:, c, :].unsqueeze(2).to_broadcast([HU, G, P]),
                                                    ALU.is_equal)
                        ins.then_inc(sel_t_ready, 1)
                    if f is not None:
                        evacuate(dve, f, q_buf, b_qv_sb[:, 0:D], q_psum, q_ready, range(G))
                    if k is not None:
                        for b in range(G):
                            dve.wait_ge(s_psum, k * G + (b + 1))
                            dve.tensor_reduce(neg_max[:, b, :],
                                              bank(1, b)[0:HU, :].rearrange("p (c n) -> p c n", c=KC),
                                              AX.X, ALU.max, negate=True).then_inc(max_ready, 1)
                    if f is not None:
                        dve.wait_ge(q_ready, f * G + G)
                        q = heads(q_buf)
                        dve.tensor_reduce(head_grid(sum_q), q, AX.X, ALU.add).then_inc(sum_q_done, 1)
                        dve.wait_ge(sum_q_done, f + 1)
                        dve.tensor_scalar(mean_q, sum_q, 1.0 / DK, None, ALU.mult).then_inc(mean_q_done, 1)
                        dve.tensor_reduce(head_grid(max_q), q, AX.X, ALU.max).then_inc(max_q_done, 1)
                    if n is not None:
                        dve.wait_ge(x_loaded, n * 32 + 32)
                        moments_of(dve, n, lambda b: x_in[:, b, :], stats_a, moments_a, norm=norm_next)
                    if k is not None:
                        dve.wait_ge(e_ready, k * G + G)
                        dve.reciprocal(e_rec, e_sum).then_inc(e_rec_done, 1)
                        dve.wait_ge(e_rec_done, k + 1)
                        for b in range(G):
                            dve.wait_ge(o_psum, k * G + (b + 1))
                            for c in range(KC):
                                ins = dve.scalar_tensor_tensor(
                                    o_sel[0:HU, b, c, :], bank(1, b)[0:HU, c * P:(c + 1) * P],
                                    e_rec[:, b, c:c + 1], head_block2[:, :, :].rearrange("p h d -> p (h d)"),
                                    ALU.mult, ALU.mult)
                            ins.then_inc(o_ready, 1)
                    if f is not None:
                        dve.wait_ge(expd, f + 1)
                        dve.tensor_reduce(head_grid(sum_e), heads(c2), AX.X, ALU.add).then_inc(sum_e_done, 1)
                        dve.wait_ge(sum_e_done, f + 1)
                        dve.reciprocal(rec_e, sum_e).then_inc(rec_e_done, 1)
                    if k is not None:
                        dve.wait_ge(x_res_ready, k + 1)
                        for b in range(G):
                            dve.wait_ge(attn_psum, k * G + (b + 1))
                            dve.tensor_tensor(x_res[:, b, :], x_res[:, b, :], bank(1, b), ALU.add)\
                               .then_inc(x1_ready, 1)
                        moments_of(dve, k, lambda b: x_res[:, b, :], stats_b, moments_b,
                                   before_tile=lambda b: dve.wait_ge(x1_ready, k * G + (b + 1)))
                    if f is not None:
                        evacuate(dve, f, v_buf, b_qv_sb[:, D:2 * D], v_psum, v_ready, range(G))
                    if k is not None:
                        normalise(dve, k, lambda b: x_res[:, b, :], lambda b: yn[:, b, :], rstd_b, yn_ready)
                    if f is not None:
                        dve.wait_ge(squared, f + 1)
                        dve.tensor_reduce(head_grid(sum_sq), heads(c1), AX.X, ALU.add).then_inc(sum_sq_done, 1)
                        dve.wait_ge(mean_q_done, f + 1)
                        dve.scalar_tensor_tensor(mean_sq, mean_q, float(DK), mean_q, ALU.mult, ALU.mult)\
                           .then_inc(score_step, 1)
                        dve.wait_ge(score_step, f * 3 + 1)
                        dve.wait_ge(sum_sq_done, f + 1)
                        dve.tensor_tensor(mean_sq, mean_sq, sum_sq, ALU.add).then_inc(l2_in_done, 1)
                    if f is not None:
                        dve.wait_ge(plogp_done, f + 1)
                        dve.tensor_reduce(head_grid(sum_pl), heads(c3), AX.X, ALU.add).then_inc(score_step, 1)
                        dve.wait_ge(l2_done, f + 1)
                        dve.scalar_tensor_tensor(score, sum_sq, 0.4 / (DK - 1), l2, ALU.mult, ALU.add)\
                           .then_inc(score_step, 1)
                        dve.wait_ge(score_step, f * 3 + 3)
                        dve.scalar_tensor_tensor(score, sum_pl, -0.6, score, ALU.mult, ALU.add)\
                           .then_inc(score_ready, 1)
                        top_queries(f)
                    if n is not None:
                        normalise(dve, n, lambda b: x_in[:, b, :], lambda b: xn[:, b, :], rstd_a, xn_ready,
                                  norm_next)
                turn(None, None, 0)
                turn(0, None, 1)
                with dve.Fori(0, NG - 2) as g:
                    turn(g + 1, g, g + 2)
                turn(NG - 1, NG - 2, None)
                turn(None, NG - 1, None)

        next_phase()
        carve = carver()
        w1_sb = carve(EXPERTS, KC, HID)
        w2_sb = carve(EXPERTS, HK, D)
        b1_sb = carve(EXPERTS, HID)
        g1_sb = carve(EXPERTS, HID)
        be1_sb = carve(EXPERTS, HID)
        b2_sb = carve(EXPERTS, D)
        after_weights = carve.at()

        def load_experts(eng, rows, done):
            for t, src in ((b1_sb, b1), (g1_sb, ln1_g), (b2_sb, b2)):
                eng.dma_start(t[rows], src.partition_broadcast(rows.stop - rows.start)).then_inc(done, 16)
            for e in range(EXPERTS):
                for t, src in ((w1_sb, w1), (w2_sb, w2)):
                    eng.dma_start(t[rows, e, :, :], src[e].rearrange("(c p) n -> p c n", p=P)[rows])\
                       .then_inc(done, 16)
        EXPERT_LOADS = 3 + 2 * EXPERTS

        carve = carver()
        cost = carve(P + 1, P + 1, rows=B)
        upper = carve(P, P, rows=B)
        code = carve(P, P, dt=BF16, rows=B)
        junk = carve(P, 2, rows=B)
        row_cells = [carve(HOP, P, rows=B) for _ in range(2)]
        row_codes = carve(2 * HOP, rows=B)
        PATH_TURNS = (P - 1) // (2 * HOP)
        assert P - 1 == PATH_TURNS * 2 * HOP + 1
        upper_flat = upper.rearrange("p i j -> p (i j)")
        code_flat = code.rearrange("p i j -> p (i j)")
        TURNS = P // ROWS
        SPREADS = (TURNS - 2) * ROWS // 2 + 1

        edge_made, experts_in = sem("edge_made"), sem("experts_in")
        cost_loaded = [sem(f"cost_loaded{c}") for c in range(TURNS)]
        sem_sign = sem("sign_done")
        upper_done, row_done = sem("upper_done"), sem("row_done", FREE)
        diff_done, is_up_done, code_done = sem("diff_done"), sem("is_up_done"), sem("code_done")
        left_done, gated_done, scan_done = sem("left_done"), sem("gated_done"), sem("scan_done")
        followed = [sem(f"followed{k}", FREE) for k in range(2 * HOP)]
        cells_in = [sem(f"cells_in{h}") for h in range(2)]
        codes_out = [sem(f"codes_out{h}", FREE) for h in range(2)]
        last_row_out = sem("last_row_out")

        def first_row_of(t, h):
            return P - 1 - HOP * (h + 1) - t * (2 * HOP)

        with nc.Block() as block:
            @block.sync
            def _(sp):
                for c in range(TURNS):
                    sp.dma_start(cost[:, 1 + c * ROWS:1 + (c + 1) * ROWS, 1:P + 1],
                                 dist_dram[:, c * ROWS:(c + 1) * ROWS, :]).then_inc(cost_loaded[c], 16)
                load_experts(sp, slice(B, P), experts_in)
                sp.wait_ge(experts_in, 16 * EXPERT_LOADS)

            @block.gpsimd
            def _(pool):
                pool.memset(cost[:, 0, 1:P + 1], BIG).then_inc(edge_made, 1)
                pool.memset(cost[:, 1:P + 1, 0], BIG).then_inc(edge_made, 1)
                pool.memset(cost[:, 0, 0:1], 0.0).then_inc(edge_made, 1)
                pool.memset(codes[:, 0:1], 0.0).then_inc(edge_made, 1)
                pool.memset(codes[:, P:P + 1], 2.0 * P - 1).then_inc(edge_made, 1)
                with pool.Fori(0, TURNS) as t:
                    pool.wait_ge(row_done, t * ROWS + ROWS + FREE)
                    apart(pool)
                    rows = bass.ds(t * ROWS, ROWS)
                    pool.tensor_tensor(code[:, rows, :], cost[:, rows, 1:P + 1], cost[:, rows, 0:P],
                                       ALU.subtract).then_inc(diff_done, 1)
                    pool.wait_ge(is_up_done, t + 1)
                    apart(pool)
                    pool.tensor_tensor(code[:, rows, :], code[:, rows, :],
                                       iota_2j[0:B, :].unsqueeze(1).to_broadcast([B, ROWS, P]), ALU.add)\
                        .then_inc(code_done, 1)
                pool.wait_ge(followed[-1], 1 + FREE)
                pool.tensor_copy(codes[:, P - 1:P], row_codes[:, 0:1]).then_inc(last_row_out, 1)
                with pool.Fori(0, PATH_TURNS) as t:
                    for h in range(2):
                        pool.wait_ge(followed[(h + 1) * HOP - 1], t + (1 + h + FREE))
                        apart(pool)
                        pool.tensor_copy(codes[:, bass.ds(first_row_of(t, h), HOP)],
                                         row_codes[:, (1 - h) * HOP:(2 - h) * HOP]).then_inc(codes_out[h], 1)

            @block.scalar
            def _(act):
                with act.Fori(0, TURNS) as t:
                    flat = code_flat[:, bass.ds(t * ROWS * P, ROWS * P)]
                    act.wait_ge(diff_done, t + 1)
                    apart(act)
                    act.activation(flat, flat, ACT.Sign, scale=-1.0).then_inc(sem_sign, 1)
                    act.wait_ge(sem_sign, t + 1)
                    apart(act)
                    act.activation(flat, flat, ACT.Relu).then_inc(is_up_done, 1)
                act.wait_ge(scan_done, SPREADS)
                with act.Fori(0, PATH_TURNS) as t:
                    for h in range(2):
                        act.wait_ge(followed[(h + 1) * HOP - 1], t + (h + FREE))
                        apart(act)
                        act.activation(row_cells[h].rearrange("p i j -> p (i j)"),
                                       upper_flat[:, bass.ds(first_row_of(t, h) * P, HOP * P)],
                                       ACT.Copy).then_inc(cells_in[h], 1)

            @block.vector
            def _(dve):
                dve.wait_ge(edge_made, 5)

                def turn(t, q):
                    if q is not None:
                        dve.wait_ge(code_done, q + 1)
                    for r in range(ROWS):
                        i = t * ROWS + r
                        dve.wait_ge(row_done, t * ROWS + (r + FREE))
                        dve.tensor_tensor(upper[:, i, :], cost[:, i, 1:P + 1], cost[:, i, 0:P], ALU.min)\
                           .then_inc(upper_done, 1)
                        if q is not None and r % 2 == 0:
                            left(q * ROWS + r, 2)
                        dve.wait_ge(upper_done, t * ROWS + (r + 1))
                        dve.tensor_tensor_scan(cost[:, i + 1, 1:P + 1], upper[:, i, :], cost[:, i + 1, 1:P + 1],
                                               BIG, ALU.min, ALU.add).then_inc(row_done, 1)
                        if q is not None and r % 2 == 0:
                            gated(q * ROWS + r, q * (ROWS // 2) + (r // 2 + 1), 2)
                        elif q is not None:
                            spread(q * ROWS + r - 1, q * (ROWS // 2) + (r // 2 + 1), 2)

                def left(i, n):
                    rows = bass.ds(i, n)
                    dve.tensor_tensor(upper[:, rows, :], upper[:, rows, :], cost[:, bass.ds(i + 1, n), 0:P],
                                      ALU.is_gt).then_inc(left_done, 1)

                def gated(i, lefts, n):
                    at = bass.ds(i * P, n * P)
                    dve.wait_ge(left_done, lefts)
                    apart(dve)
                    dve.scalar_tensor_tensor(code_flat[:, at], upper_flat[:, at], 1.0, code_flat[:, at],
                                             ALU.is_lt, ALU.mult).then_inc(gated_done, 1)

                def spread(i, gates, n):
                    at = bass.ds(i * P, n * P)
                    dve.wait_ge(gated_done, gates)
                    dve.tensor_tensor_scan(upper_flat[:, at], upper_flat[:, at], code_flat[:, at],
                                           0.0, ALU.mult, ALU.add).then_inc(scan_done, 1)
                for t in range(2):
                    dve.wait_ge(cost_loaded[t], 16)
                    turn(t, None)
                for c in range(2, TURNS):
                    dve.wait_ge(cost_loaded[c], 16)
                with dve.Fori(2, TURNS) as t:
                    turn(t, t - 2)
                dve.wait_ge(row_done, P + FREE)
                dve.wait_ge(code_done, TURNS)
                before_last = (TURNS - 2) * ROWS
                left(before_last, 2 * ROWS)
                gated(before_last, before_last // 2 + 1, 2 * ROWS)
                spread(before_last, before_last // 2 + 1, 2 * ROWS)
                dve.wait_ge(scan_done, SPREADS)

                def follow(cells, code, exit_code, step):
                    dve.scalar_tensor_tensor(
                        junk, iota_256[0:B, :].rearrange("p (j t) -> p j t", t=2), code,
                        cells.unsqueeze(2).to_broadcast([B, P, 2]),
                        ALU.is_equal, ALU.mult, accum_out=exit_code).then_inc(followed[step], 1)

                follow(upper[:, P - 1, :], codes[:, P:P + 1], row_codes[:, 0:1], 2 * HOP - 1)
                dve.wait_ge(last_row_out, 1)
                with dve.Fori(0, PATH_TURNS) as t:
                    for step in range(2 * HOP):
                        h, k = step // HOP, step % HOP
                        c = 2 * HOP - 1 - step
                        if k == 0:
                            dve.wait_ge(cells_in[h], t + 1)
                            dve.wait_ge(codes_out[h], t + FREE)
                        dve.wait_ge(followed[step - 1], t + (1 + FREE))
                        follow(row_cells[h][:, HOP - 1 - k, :],
                               row_codes[:, (c + 1) % (2 * HOP):(c + 1) % (2 * HOP) + 1],
                               row_codes[:, c:c + 1], step)
                for h in range(2):
                    dve.wait_ge(codes_out[h], PATH_TURNS + FREE)

        next_phase()
        carve = carver()
        carve(after_weights)
        x2_even = carve(G, D)
        xf_t = carve(G, KC, P)
        flat_table = be1_sb.rearrange("p e n -> p (e n)")
        assert EXPERTS * HID >= 2 * G * D
        ctx, x2_odd = (flat_table[:, h * G * D:(h + 1) * G * D].rearrange("p (g d) -> p g d", g=G)
                       for h in range(2))
        x2 = [x2_even, x2_odd]
        pair_rows = [[carve(G, ROW) for _ in range(2)] for _ in range(2)]
        mask = carve(G, P)
        gate_sb = carve(KC, EXPERTS)
        null_row = carve(ROW)
        logits = carve(G, EXPERTS)
        masked = carve(G, EXPERTS)
        hit = carve(G, EXPERTS)
        hot = [carve(G, EXPERTS) for _ in range(2)]
        hot_both = carve(G, EXPERTS, dt=BF16)
        place = carve(G, EXPERTS)
        picked = carve(G, EXPERTS)
        best = [carve(G) for _ in range(2)]
        rank = [carve(G) for _ in range(2)]
        spot = carve(2, G)
        spots = [carve(2, G, dt=I32) for _ in range(2)]
        gap = carve(G)
        ratio = carve(G)
        fill = carve(EXPERTS)
        first_row = carve(EXPERTS)
        count = carve(EXPERTS)
        tiles = carve(EXPERTS)
        tile_end = carve(EXPERTS)
        skip = carve(EXPERTS)
        tail = carve(EXPERTS, dt=I32)
        tile_f = carve(NS)
        addr_f = carve(NS)
        used = carve(NS)
        pair_row = carve(2, G)

        tables_made = sem("tables_made")
        gate_in, moe_weights_in, last_table_in = sem("gate_in"), sem("moe_weights_in"), sem("last_table_in")
        ctx_in, x1_in = sem("ctx_in"), [sem(f"x1_in{j}") for j in range(2)]
        x2_stored = sem("x2_stored", FREE)
        codes_psum, codes_ready = sem("codes_psum"), sem("codes_ready")
        mask_half, mask_ready = sem("mask_half"), sem("mask_ready")
        warp_psum, x2_ready = sem("warp_psum", FREE), sem("x2_ready", FREE)
        stats_c, moments_c, rstd_c, xf_ready = sem("stats_c"), sem("moments_c"), sem("rstd_c"), sem("xf_ready", FREE)
        eps_c = sem("eps_c")
        xf_copied, kept_moments = sem("xf_copied"), sem("kept_moments")
        xft_psum, xft_ready = sem("xft_psum"), sem("xft_ready")
        logit_psum, gate_step = sem("logit_psum"), sem("gate_step", FREE)
        hot_ready, place_psum = sem("hot_ready"), sem("place_psum")
        gap_ready, ratio_ready = sem("gap_ready"), sem("ratio_ready")
        spots_ready, weights_ready = sem("spots_ready"), sem("weights_ready")
        pair_rows_put, pair_rows_moved = sem("pair_rows_put"), sem("pair_rows_moved")
        tail_ready, tails_out, null_out = sem("tail_ready"), sem("tails_out"), sem("null_out")
        scattered = [[[sem(f"scattered{p}_{k}_{b}") for b in range(G)] for k in range(2)] for p in range(2)]

        PAIR = G // 2

        def turns(eng, turn):
            turn(0, 0, None, 2)
            turn(1, 1, None, 2)
            with eng.Fori(1, NG // 2 - 1) as u:
                turn(2 * u, 0, u, 2)
                turn(2 * u + 1, 1, u, 2)
            turn(NG - 2, 0, NG // 2 - 1, 1)
            turn(NG - 1, 1, NG // 2 - 1, 0)

        with nc.Block() as block:
            @block.sync
            def _(sp):
                sp.dma_start(gate_sb, gate_w.rearrange("(c p) e -> p c e", p=P)).then_inc(gate_in, 16)
                sp.wait_ge(tables_made, 6)
                sp.dma_start(slots[NULL_TILE * P:(NULL_TILE + 1) * P, :], null_row).then_inc(null_out, 16)

                def store(g, parity):
                    sp.wait_ge(x2_ready, g * PAIR + (PAIR + FREE))
                    sp.dma_start(x2_dram[bass.ds(g * G, G)].rearrange("g p d -> p g d"), x2[parity])\
                      .then_inc(x2_stored, 16)

                def turn(g, parity, use, ahead):
                    if ahead > 1:
                        sp.wait_ge(warp_psum, g * PAIR + (2 * PAIR + FREE))
                        apart(sp)
                        load_group(sp, ctx, ctx_rows, g + 2, ctx_in)
                        sp.wait_ge(x2_stored, g * 16 + (16 + FREE))
                        apart(sp)
                        sp.wait_ge(xf_ready, g * G + (G + FREE))
                        apart(sp)
                        load_group(sp, x2[parity], x1_dram, g + 2, x1_in[parity])
                    if ahead > 0:
                        store(g + 1, 1 - parity)
                load_group(sp, ctx, ctx_rows, 0, ctx_in)
                load_group(sp, x2[0], x1_dram, 0, x1_in[0])
                load_group(sp, x2[1], x1_dram, 1, x1_in[1])
                sp.wait_ge(warp_psum, PAIR + FREE)
                load_group(sp, ctx, ctx_rows, 1, ctx_in)
                store(0, 0)
                turns(sp, turn)
                sp.wait_ge(tail_ready, 1)
                _, starts = nc.values_load_multi_w_load_instructions(
                    tail[0:1, :], engines=[mybir.EngineType.SP], min_val=0, max_val=EXPERTS * REGION - P,
                    skip_runtime_bounds_check_because="a region holds all tokens and a tile of null rows")
                for start in starts:
                    sp.dma_start(slots[bass.ds(start, P), :], null_row).then_inc(tails_out, 16)
                sp.wait_ge(tails_out, 16 * EXPERTS)
                sp.wait_ge(x2_stored, 16 * NG + FREE)
                sp.wait_ge(xf_ready, NG * G + FREE)
                sp.dma_start(be1_sb, ln1_b.partition_broadcast(P)).then_inc(last_table_in, 16)
                sp.wait_ge(last_table_in, 16)
                sp.wait_ge(null_out, 16)

            @block.gpsimd
            def _(pool):
                pool.iota(first_row, pattern=[[REGION, EXPERTS]], base=0, channel_multiplier=0,
                          allow_small_or_imprecise_dtypes=True).then_inc(tables_made, 1)
                pool.iota(fill, pattern=[[REGION, EXPERTS]], base=0, channel_multiplier=0,
                          allow_small_or_imprecise_dtypes=True).then_inc(tables_made, 1)
                for k in range(2):
                    pool.iota(pair_row[:, k, :], pattern=[[P, G]], base=k * T, channel_multiplier=1,
                              allow_small_or_imprecise_dtypes=True).then_inc(tables_made, 1)
                pool.memset(null_row[:, 0:D + 1], 0.0).then_inc(tables_made, 1)
                pool.memset(null_row[:, D + 1:ROW], float(4 * T)).then_inc(tables_made, 1)
                pool.wait_ge(tables_made, 6)

                def turn(g, parity, use, ahead):
                    if ahead > 0:
                        inverse_deviation(pool, g + 1, moments_c, eps_c, rstd_c)
                    for pair in range(2):
                        if use is not None:
                            for b in range(G):
                                pool.wait_ge(scattered[parity][pair][b], use * 16)
                        apart(pool)
                        pool.tensor_copy(pair_rows[parity][pair][:, :, D + 1], pair_row[:, pair, :])\
                            .then_inc(pair_rows_put, 1)
                    pool.wait_ge(pair_rows_put, g * 2 + 2)
                    apart(pool)
                    pool.tensor_scalar(pair_row, pair_row, float(G * P), None, ALU.add)\
                        .then_inc(pair_rows_moved, 1)
                    pool.wait_ge(pair_rows_moved, g + 1)
                    pool.wait_ge(spots_ready, g + 1)
                    pool.wait_ge(weights_ready, g * 2 + 2)
                    for b in range(G):
                        for pair in range(2):
                            pool.wait_ge(xf_copied, g * G + (b + 1))
                            apart(pool)
                            pool.indirect_dma_start(
                                out=slots[:, :],
                                out_offset=bass.IndirectOffsetOnAxis(ap=spots[parity][:, pair, b:b + 1], axis=0),
                                in_=pair_rows[parity][pair][:, b, :], in_offset=None)\
                                .then_inc(scattered[parity][pair][b], 16)
                inverse_deviation(pool, 0, moments_c, eps_c, rstd_c)
                turns(pool, turn)
                for parity in range(2):
                    for pair in range(2):
                        for b in range(G):
                            pool.wait_ge(scattered[parity][pair][b], 16 * NG // 2)

            @block.tensor
            def _(pe):
                pe.transpose(ps[0][:, 0:B], codes[:, 1:P + 1], ident[0:B, 0:B]).then_inc(codes_psum, 1)
                pe.transpose(ps[1][:, 0:B], codes[:, 0:P], ident[0:B, 0:B]).then_inc(codes_psum, 1)
                pe.wait_ge(gate_in, 16)
                pe.wait_ge(codes_ready, 2)
                flat = hot_both.rearrange("p g e -> p (g e)")
                def warp(g):
                    pe.wait_ge(ctx_in, g * 32 + 32)
                    pe.wait_ge(x2_ready, g * PAIR + FREE)
                    for b in range(G):
                        pe.wait_ge(mask_ready, g * G + (b + 1))
                        ins = pe.matmul(ps[PAIR + b // 2][:, (b % 2) * D:(b % 2 + 1) * D], mask[:, b, :],
                                        ctx[:, b, :], start=True, stop=True)
                        if b % 2 == 1:
                            ins.then_inc(warp_psum, 1)

                def turn(g, parity, use, ahead):
                    for b in range(G):
                        pe.wait_ge(xf_ready, g * G + (b + 1 + FREE))
                        for c in range(KC):
                            ins = pe.transpose(ps[b // 2][:, (b % 2) * D + c * P:(b % 2) * D + (c + 1) * P],
                                               pair_rows[parity][0][:, b, c * P:(c + 1) * P], ident[:, :])
                        if b % 2 == 1:
                            ins.then_inc(xft_psum, 1)
                    pe.wait_ge(xft_ready, g * PAIR + PAIR)
                    for b in range(G):
                        for c in range(KC):
                            ins = pe.matmul(ps[0][:, b * EXPERTS:(b + 1) * EXPERTS], xf_t[:, b, c, :],
                                            gate_sb[:, c, :], start=(c == 0), stop=(c == KC - 1))
                    ins.then_inc(logit_psum, 1)
                    pe.wait_ge(hot_ready, g + 1)
                    n = G * EXPERTS
                    pe.matmul(ps[1][:, 0:n], before[:, :], flat, start=True, stop=False)
                    for b in range(1, G):
                        pe.matmul(ps[1][:, b * EXPERTS:n], ones_bf[:, :], flat[:, 0:n - b * EXPERTS],
                                  start=False, stop=(b == G - 1))
                    for b in range(G):
                        ins = pe.matmul(ps[2][:, 0:EXPERTS], ones_bf[:, :],
                                        flat[:, b * EXPERTS:(b + 1) * EXPERTS],
                                        start=(b == 0), stop=(b == G - 1))
                    ins.then_inc(place_psum, 1)
                    if ahead > 1:
                        warp(g + 2)
                warp(0)
                warp(1)
                turns(pe, turn)

            @block.scalar
            def _(act):
                def turn(g, parity, use, ahead):
                    for b in range(0, G, 2):
                        act.wait_ge(xft_psum, g * PAIR + (b // 2 + 1))
                        act.activation(xf_t[:, b:b + 2, :, :].rearrange("p g c n -> p (g c n)"),
                                       ps[b // 2][:, :], ACT.Copy).then_inc(xft_ready, 1)
                    for b in range(G):
                        if use is not None:
                            act.wait_ge(scattered[parity][1][b], use * 16)
                        act.wait_ge(xf_ready, g * G + (b + 1 + FREE))
                        act.activation(pair_rows[parity][1][:, b, 0:D], pair_rows[parity][0][:, b, 0:D],
                                       ACT.Copy).then_inc(xf_copied, 1)
                    act.wait_ge(gap_ready, g + 1)
                    act.activation(ratio, gap, ACT.Exp).then_inc(ratio_ready, 1)
                act.wait_ge(ctx_in, 32)
                for j in range(2):
                    act.wait_ge(x1_in[j], 32)
                load_experts(act, slice(0, B), moe_weights_in)
                turns(act, turn)
                act.wait_ge(moe_weights_in, 16 * EXPERT_LOADS)

            @block.vector
            def _(dve):
                dve.wait_ge(codes_psum, 2)
                for k in range(2):
                    dve.tensor_copy(row_code[:, k, :], ps[k][:, 0:B]).then_inc(codes_ready, 1)
                dve.wait_ge(codes_ready, 2)
                dve.wait_ge(tables_made, 6)
                odd = iota_256[:, :].rearrange("p (j t) -> p j t", t=2)[:, :, 0]

                def wide(t):
                    return t.unsqueeze(2).to_broadcast([P, G, EXPERTS])

                def masks(g):
                    for b in range(G):
                        dve.tensor_scalar(mask[:, b, :], iota_2j[:, :], row_code[:, 0, bass.ds(g * G + b, 1)],
                                          None, ALU.is_lt).then_inc(mask_half, 1)
                    for b in range(G):
                        dve.wait_ge(mask_half, g * G + (b + 1))
                        dve.scalar_tensor_tensor(mask[:, b, :], odd, row_code[:, 1, bass.ds(g * G + b, 1)],
                                                 mask[:, b, :], ALU.is_ge, ALU.mult).then_inc(mask_ready, 1)

                def add_warped(g, parity, filled):
                    dve.wait_ge(x1_in[parity], filled * 32 + 32)
                    for b in range(0, G, 2):
                        dve.wait_ge(warp_psum, g * PAIR + (b // 2 + 1 + FREE))
                        two = x2[parity][:, b:b + 2, :].rearrange("p g d -> p (g d)")
                        dve.tensor_tensor(two, two, ps[PAIR + b // 2][:, :], ALU.add).then_inc(x2_ready, 1)
                    moments_of(dve, g, lambda b: x2[parity][:, b, :], stats_c, moments_c,
                               before_tile=lambda b: dve.wait_ge(x2_ready, g * PAIR + (b // 2 + 1 + FREE)))

                def turn(g, parity, use, ahead):
                    if use is not None:
                        for b in range(G):
                            dve.wait_ge(scattered[parity][0][b], use * 16)
                    normalise(dve, g, lambda b: x2[parity][:, b, :], lambda b: pair_rows[parity][0][:, b, 0:D],
                              rstd_c, xf_ready)
                    dve.tensor_copy(xf_scale[:, 0, bass.ds(g * G, G)], rstd[:, :])
                    dve.scalar_tensor_tensor(xf_scale[:, 1, bass.ds(g * G, G)], moments[:, :, 0], -1.0,
                                             rstd[:, :], ALU.mult, ALU.mult).then_inc(kept_moments, 1)
                    if ahead > 0:
                        filled = 0 if use is None else use
                        add_warped(g + 1, 1 - parity, filled + parity)
                    dve.wait_ge(logit_psum, g + 1)
                    n = 0

                    def step(ins):
                        nonlocal n
                        ins.then_inc(gate_step, 1)
                        n += 1
                        dve.wait_ge(gate_step, g * GATE_STEPS + (n + FREE))
                    step(dve.tensor_copy(logits, ps[0][:, 0:G * EXPERTS].rearrange("p (g e) -> p g e", g=G)))
                    src = logits
                    for pair in range(2):
                        step(dve.tensor_reduce(best[pair], src, AX.X, ALU.max))
                        step(dve.tensor_tensor(hit, src, wide(best[pair]), ALU.is_equal))
                        step(dve.tensor_tensor(hit, hit, from_8[:, :, :], ALU.mult))
                        step(dve.tensor_reduce(rank[pair], hit, AX.X, ALU.max))
                        step(dve.tensor_tensor(hot[pair], from_8[:, :, :], wide(rank[pair]), ALU.is_equal))
                        if pair == 0:
                            step(dve.scalar_tensor_tensor(masked, hot[0], -3e38, logits, ALU.mult, ALU.add))
                            src = masked
                    dve.tensor_tensor(hot_both, hot[0], hot[1], ALU.add).then_inc(hot_ready, 1)
                    dve.tensor_tensor(gap, best[1], best[0], ALU.subtract).then_inc(gap_ready, 1)
                    dve.wait_ge(place_psum, g + 1)
                    step(dve.tensor_tensor(place, ps[1][:, 0:G * EXPERTS].rearrange("p (g e) -> p g e", g=G),
                                           fill.unsqueeze(1).to_broadcast([P, G, EXPERTS]), ALU.add))
                    step(dve.tensor_tensor(fill, fill, ps[2][:, 0:EXPERTS], ALU.add))
                    for pair in range(2):
                        step(dve.tensor_tensor(picked, place, hot[pair], ALU.mult))
                        step(dve.tensor_reduce(spot[:, pair, :], picked, AX.X, ALU.add))
                    assert n == PLACED + 4
                    if use is not None:
                        for b in range(G):
                            dve.wait_ge(scattered[parity][1][b], use * 16)
                    dve.tensor_copy(spots[parity], spot).then_inc(spots_ready, 1)
                    dve.wait_ge(ratio_ready, g + 1)
                    step(dve.tensor_scalar(gap, ratio, 1.0, None, ALU.add))
                    dve.reciprocal(pair_rows[parity][0][:, :, D], gap).then_inc(weights_ready, 1)
                    dve.wait_ge(weights_ready, g * 2 + 1)
                    dve.tensor_tensor(pair_rows[parity][1][:, :, D], ratio, pair_rows[parity][0][:, :, D], ALU.mult)\
                       .then_inc(weights_ready, 1)
                    assert n == GATE_STEPS
                    if ahead > 1:
                        masks(g + 2)
                masks(0)
                add_warped(0, 0, 0)
                masks(1)
                turns(dve, turn)

                m = 0

                def step(ins):
                    nonlocal m
                    ins.then_inc(gate_step, 1)
                    m += 1
                    dve.wait_ge(gate_step, NG * GATE_STEPS + FREE + m)
                step(dve.tensor_tensor(count, fill, first_row, ALU.subtract))
                dve.tensor_copy(tail, fill).then_inc(tail_ready, 1)
                step(dve.tensor_scalar(tiles, count, 1.0 / P, (P - 1) / (2.0 * P), ALU.mult, ALU.add))
                step(dve.tensor_scalar(tiles, tiles, MAGIC, None, ALU.add))
                step(dve.tensor_scalar(tiles, tiles, MAGIC, None, ALU.subtract))
                step(dve.tensor_tensor_scan(tile_end, ones8[:, :], tiles, 0.0, ALU.mult, ALU.add))
                step(dve.tensor_scalar(skip, tiles, -1.0, REGION / P, ALU.mult, ALU.add))
                step(dve.tensor_scalar(tile_f, iota_slot[:, :], tile_end[:, 0:1], None, ALU.is_ge))
                step(dve.scalar_tensor_tensor(addr_f, tile_f, skip[:, 0:1], iota_slot[:, :], ALU.mult, ALU.add))
                for e in range(1, EXPERTS - 1):
                    step(dve.tensor_scalar(used, iota_slot[:, :], tile_end[:, e:e + 1], None, ALU.is_ge))
                    step(dve.scalar_tensor_tensor(addr_f, used, skip[:, e:e + 1], addr_f, ALU.mult, ALU.add))
                    step(dve.tensor_tensor(tile_f, tile_f, used, ALU.add))
                step(dve.tensor_scalar(used, iota_slot[:, :], tile_end[:, EXPERTS - 1:EXPERTS], None, ALU.is_lt))
                step(dve.scalar_tensor_tensor(addr_f, addr_f, float(NULL_TILE), used, ALU.subtract, ALU.mult))
                step(dve.tensor_scalar(addr_f, addr_f, float(NULL_TILE), None, ALU.add))
                step(dve.tensor_copy(tile_addr[:, :], addr_f))
                step(dve.tensor_copy(tile_expert[:, :], tile_f))

        next_phase()
        U = MOE_UNROLL
        NU = NS // U
        carve = carver()
        carve(after_weights)
        xs = [carve(U, ROW) for _ in range(2)]
        xs_t = carve(U, KC, P)
        h = [carve(U, HID) for _ in range(2)]
        h_t = carve(U, HK, P)
        y = [carve(U, D) for _ in range(2)]
        gate_now = [carve(U) for _ in range(2)]
        dest_now = [carve(U, dt=I32) for _ in range(2)]
        m_stats = carve(U, 6)
        m_mom = carve(U, 2)
        m_rstd = carve(U)
        xs_in = [[sem(f"xs_in{j}_{u}") for u in range(U)] for j in range(2)]
        y_out = [[sem(f"y_out{j}_{u}") for u in range(U)] for j in range(2)]
        xst_psum, xst_ready, h_psum, h_ready = (
            sem("xst_psum"), sem("xst_ready"), sem("h_psum"), sem("h_ready"))
        m_stats_done, m_mom_done, m_eps_done, m_rstd_done = (
            sem("m_stats_done"), sem("m_mom_done"), sem("m_eps_done"), sem("m_rstd_done"))
        h_scaled, h_normed, act_ready = sem("h_scaled"), sem("h_normed"), sem("act_ready")
        ht_psum, ht_ready, y_psum, y_biased, y_ready = (
            sem("ht_psum"), sem("ht_ready"), sem("y_psum"), sem("y_biased"), sem("y_ready"))
        meta_ready = sem("meta_ready")

        def table(eng, which, t, m):
            _, values = nc.values_load_multi_w_load_instructions(
                t[0:1, m * U:(m + 1) * U] if isinstance(m, int) else t[0:1, bass.ds(m * U, U)],
                engines=[which], min_val=0, max_val=(EXPERTS - 1 if t is tile_expert else NULL_TILE),
                skip_runtime_bounds_check_because="both tables are made above, within these bounds")
            return values

        def pick(t, e):
            return t[:, bass.ds(e, 1)]

        def units(eng, unit):
            for m in range(3):
                unit(m, m % 2, m // 2)
            with eng.Fori(1, (NU - 2) // 2) as n:
                unit(n * 2 + 1, 1, n)
                unit(n * 2 + 2, 0, n + 1)
            for m in range(NU - 1 - (NU % 2), NU):
                unit(m, m % 2, m // 2)

        with nc.Block() as block:
            @block.sync
            def _(sp):
                def unit(m, j, before):
                    addr = table(sp, mybir.EngineType.SP, tile_addr, m)
                    for u in range(U):
                        if not (isinstance(m, int) and m < 2):
                            sp.wait_ge(xst_psum, m * U - (2 * U - 1 - u))
                            apart(sp)
                            sp.wait_ge(meta_ready, m * 2 - 2)
                            apart(sp)
                        sp.dma_start(xs[j][:, u, :], slots[bass.ds(addr[u] * P, P), :]).then_inc(xs_in[j][u], 16)
                units(sp, unit)

            @block.gpsimd
            def _(pool):
                def scatter(m, j, before):
                    for u in range(U):
                        pool.wait_ge(y_ready, m * U + (u + 1))
                        apart(pool)
                        pool.indirect_dma_start(
                            out=pair_out[:, :], out_offset=bass.IndirectOffsetOnAxis(
                                ap=dest_now[j][:, u:u + 1], axis=0),
                            in_=y[j][:, u, :], in_offset=None, bounds_check=2 * T - 1, oob_is_err=False)\
                            .then_inc(y_out[j][u], 16)

                def unit(m, j, before):
                    for u in range(U):
                        pool.wait_ge(xs_in[j][u], before * 16 + 16)
                        if not (isinstance(m, int) and m < 2):
                            pool.wait_ge(y_out[j][u], before * 16)
                    apart(pool)
                    pool.tensor_copy(dest_now[j], xs[j][:, :, D + 1]).then_inc(meta_ready, 1)
                    pool.tensor_copy(gate_now[j], xs[j][:, :, D]).then_inc(meta_ready, 1)
                    pool.wait_ge(m_mom_done, m * U + U)
                    apart(pool)
                    pool.tensor_scalar(m_rstd, m_mom[:, :, 1], EPS, None, ALU.add).then_inc(m_eps_done, 1)
                    pool.wait_ge(m_eps_done, m + 1)
                    pool.tensor_tensor(m_rstd, m_rstd, exponents[:, 0:U], ALU.pow).then_inc(m_rstd_done, 1)
                    if not (isinstance(m, int) and m < 1):
                        scatter(m - 1, 1 - j, None)
                units(pool, unit)
                scatter(NU - 1, (NU - 1) % 2, None)
                for j in range(2):
                    for u in range(U):
                        pool.wait_ge(y_out[j][u], 16 * (NU // 2 + (NU % 2 and j == 0)))

            @block.tensor
            def _(pe):
                def transpose_in(m, j, before):
                    for u in range(U):
                        pe.wait_ge(xs_in[j][u], before * 16 + 16)
                        if not (isinstance(m, int) and m < 1):
                            pe.wait_ge(h_ready, m * U - (U - 1 - u))
                        for c in range(KC):
                            ins = pe.transpose(ps[u][:, c * P:(c + 1) * P], xs[j][:, u, c * P:(c + 1) * P],
                                               ident[:, :])
                        ins.then_inc(xst_psum, 1)

                def up(m):
                    e = table(pe, mybir.EngineType.PE, tile_expert, m)
                    for u in range(U):
                        pe.wait_ge(xst_ready, m * U + (u + 1))
                        for c in range(KC):
                            ins = pe.matmul(ps[u][:, :], xs_t[:, u, c, :],
                                            pick(w1_sb, e[u])[:, :, c, :].rearrange("p e n -> p (e n)"),
                                            start=(c == 0), stop=(c == KC - 1))
                        ins.then_inc(h_psum, 1)

                def down(m, j):
                    e = table(pe, mybir.EngineType.PE, tile_expert, m)
                    for u in range(U):
                        pe.wait_ge(act_ready, m * U + (u + 1))
                        if not (isinstance(m, int) and m < 1):
                            pe.wait_ge(y_biased, m * U - (U - 1 - u))
                        for c in range(HK):
                            ins = pe.transpose(ps[4 + u][:, c * P:(c + 1) * P], h[j][:, u, c * P:(c + 1) * P],
                                               ident[:, :])
                        ins.then_inc(ht_psum, 1)
                    for u in range(U):
                        pe.wait_ge(ht_ready, m * U + (u + 1))
                        for c in range(HK):
                            ins = pe.matmul(ps[4 + u][:, 0:D], h_t[:, u, c, :],
                                            pick(w2_sb, e[u])[:, :, c, :].rearrange("p e n -> p (e n)"),
                                            start=(c == 0), stop=(c == HK - 1))
                        ins.then_inc(y_psum, 1)

                def unit(m, j, before):
                    up(m)
                    if not (isinstance(m, int) and m == NU - 1):
                        transpose_in(m + 1, 1 - j, before + j)
                    if not (isinstance(m, int) and m < 1):
                        down(m - 1, 1 - j)
                transpose_in(0, 0, 0)
                units(pe, unit)
                down(NU - 1, (NU - 1) % 2)

            @block.scalar
            def _(act):
                def inputs(m):
                    for u in range(U):
                        act.wait_ge(xst_psum, m * U + (u + 1))
                        act.activation(xs_t[:, u, :, :].rearrange("p c n -> p (c n)"), ps[u][:, 0:D], ACT.Copy)\
                           .then_inc(xst_ready, 1)

                def hidden(m):
                    for u in range(U):
                        act.wait_ge(ht_psum, m * U + (u + 1))
                        act.activation(h_t[:, u, :, :].rearrange("p c n -> p (c n)"), ps[4 + u][:, :], ACT.Copy)\
                           .then_inc(ht_ready, 1)

                def outputs(m, j):
                    for u in range(U):
                        act.wait_ge(y_biased, m * U + (u + 1))
                        act.wait_ge(meta_ready, m * 2 + 2)
                        act.activation(y[j][:, u, :], y[j][:, u, :], ACT.Copy, scale=gate_now[j][:, u:u + 1])\
                           .then_inc(y_ready, 1)

                def unit(m, j, before):
                    if not (isinstance(m, int) and m == NU - 1):
                        inputs(m + 1)
                    if not (isinstance(m, int) and m < 1):
                        hidden(m - 1)
                    for u in range(U):
                        act.wait_ge(h_normed, m * U + (u + 1))
                        act.activation(h[j][:, u, :], h[j][:, u, :], ACT.Gelu).then_inc(act_ready, 1)
                    if not (isinstance(m, int) and m < 1):
                        outputs(m - 1, 1 - j)
                inputs(0)
                units(act, unit)
                hidden(NU - 1)
                outputs(NU - 1, (NU - 1) % 2)

            @block.vector
            def _(dve):
                def outputs(m, j, e, before):
                    for u in range(U):
                        dve.wait_ge(y_psum, m * U + (u + 1))
                        if not (isinstance(m, int) and m < 2):
                            dve.wait_ge(y_out[j][u], before * 16)
                        dve.tensor_tensor(y[j][:, u, :].unsqueeze(1), ps[4 + u][:, 0:D].unsqueeze(1),
                                          pick(b2_sb, e[u]), ALU.add).then_inc(y_biased, 1)

                def unit(m, j, before):
                    e = table(dve, mybir.EngineType.DVE, tile_expert, m)
                    hu = lambda u: h[j][:, u, :].unsqueeze(1)
                    for u in range(U):
                        dve.wait_ge(h_psum, m * U + (u + 1))
                        if not (isinstance(m, int) and m < 2):
                            dve.wait_ge(ht_psum, m * U - (2 * U - 1 - u))
                        dve.tensor_tensor(hu(u), ps[u][:, :].unsqueeze(1), pick(b1_sb, e[u]), ALU.add)\
                           .then_inc(h_ready, 1)
                    for u in range(U):
                        dve.wait_ge(h_ready, m * U + (u + 1))
                        dve.bn_stats(m_stats[:, u, :], h[j][:, u, :]).then_inc(m_stats_done, 1)
                    for u in range(U):
                        dve.wait_ge(m_stats_done, m * U + (u + 1))
                        apart(dve)
                        dve.bn_aggr(m_mom[:, u, :], m_stats[:, u, :]).then_inc(m_mom_done, 1)
                    for u in range(U):
                        dve.wait_ge(m_mom_done, m * U + (u + 1))
                        dve.scalar_tensor_tensor(hu(u), hu(u), m_mom[:, u, 0:1], pick(g1_sb, e[u]),
                                                 ALU.subtract, ALU.mult).then_inc(h_scaled, 1)
                    dve.wait_ge(m_rstd_done, m + 1)
                    for u in range(U):
                        dve.wait_ge(h_scaled, m * U + (u + 1))
                        dve.scalar_tensor_tensor(hu(u), hu(u), m_rstd[:, u:u + 1], pick(be1_sb, e[u]),
                                                 ALU.mult, ALU.add).then_inc(h_normed, 1)
                    if not (isinstance(m, int) and m < 1):
                        e = table(dve, mybir.EngineType.DVE, tile_expert, m - 1)
                        outputs(m - 1, 1 - j, e, before - 1 + j)
                units(dve, unit)
                e = table(dve, mybir.EngineType.DVE, tile_expert, NU - 1)
                outputs(NU - 1, (NU - 1) % 2, e, (NU - 1) // 2)

        next_phase()
        carve = carver()
        ya, yb, res, res_b, xfc, mix, z = ([carve(G, D) for _ in range(2)] for _ in range(7))
        norms = [(carve(G, 6), carve(G, 2), carve(G)) for _ in range(2)]
        shift = [carve(G) for _ in range(2)]
        g_sb = carve(D)
        b_sb = carve(D)
        ln_in = sem("ln_in")
        ya_in, yb_in, res_in = ([sem(f"{n}_in{j}") for j in range(2)] for n in ("ya", "yb", "res"))
        out_stored = [sem(f"out_stored{j}", FREE) for j in range(2)]
        xf_again, mixed = sem("xf_again"), sem("mixed")
        mix_done = sem("mix_done", FREE)
        stats_d, moments_d, rstd_d = sem("stats_d"), sem("moments_d"), sem("rstd_d")
        eps_d, shift_done, z_normed, z_scaled = (
            sem("eps_d"), sem("shift_done"), sem("z_normed", FREE), sem("z_scaled"))
        res_ready, out_ready = sem("res_ready"), sem("out_ready", FREE)
        y_rows = pair_out.rearrange("(k s p) d -> k s p d", k=2, p=P)

        def turns(eng, turn):
            turn(0, None, 0, 0)
            with eng.Fori(0, NG // 2 - 1) as n:
                turn(n * 2 + 1, n * 2, 1, n)
                turn(n * 2 + 2, n * 2 + 1, 0, n + 1)
            turn(NG - 1, NG - 2, 1, NG // 2 - 1)
            turn(None, NG - 1, 0, NG // 2)

        with nc.Block() as block:
            @block.sync
            def _(sp):
                sp.dma_start(g_sb, ln_g.partition_broadcast(P)).then_inc(ln_in, 16)
                sp.dma_start(b_sb, ln_b.partition_broadcast(P)).then_inc(ln_in, 16)

                def store(g, j):
                    sp.wait_ge(out_ready, g + (1 + FREE))
                    apart(sp)
                    sp.dma_start(out[bass.ds(g * G, G)].rearrange("g p d -> p g d"), z[j])\
                      .then_inc(out_stored[j], 16)
                def load(g, j):
                    load_group(sp, res[j], x2_dram, g, res_in[j])
                    load_group(sp, ya[j], y_rows[0], g, ya_in[j])
                    load_group(sp, yb[j], y_rows[1], g, yb_in[j])

                def refill(g, j):
                    sp.wait_ge(mix_done, g + (1 + FREE))
                    apart(sp)
                    sp.wait_ge(res_ready, g + 1)
                    apart(sp)
                    load(g + 2, j)
                load(0, 0)
                load(1, 1)
                refill(0, 0)
                with sp.Fori(0, NG // 2 - 2) as n:
                    refill(n * 2 + 1, 1)
                    store(n * 2, 0)
                    refill(n * 2 + 2, 0)
                    store(n * 2 + 1, 1)
                refill(NG - 3, 1)
                for g in range(NG - 4, NG):
                    store(g, g % 2)
                for j in range(2):
                    sp.wait_ge(out_stored[j], 16 * (NG // 2) + FREE)

            @block.gpsimd
            def _(pool):
                pool.wait_ge(ln_in, 32)

                def turn(f, k, j, u):
                    if f is not None:
                        pool.wait_ge(res_in[j], u * 32 + 32)
                        pool.wait_ge(out_ready, f + (FREE - 1))
                        pool.tensor_tensor(res_b[j], res[j], b_sb.unsqueeze(1).to_broadcast([P, G, D]), ALU.add)\
                            .then_inc(res_ready, 1)
                        inverse_deviation(pool, f, moments_d, eps_d, rstd_d, norms[j])
                turns(pool, turn)

            @block.scalar
            def _(act):
                def inputs(g, j, u):
                    act.wait_ge(res_in[j], u * 32 + 32)
                    act.wait_ge(mix_done, g + (FREE - 1))
                    apart(act)
                    for b in range(G):
                        act.activation(xfc[j][:, b, :], res[j][:, b, :], ACT.Identity,
                                       bias=xf_scale[:, 1, bass.ds(g * G + b, 1)],
                                       scale=xf_scale[:, 0, bass.ds(g * G + b, 1)]).then_inc(xf_again, 1)

                def normed(g, j, u):
                    act.wait_ge(shift_done, g + 1)
                    act.wait_ge(out_stored[j], u * 16 + FREE)
                    for b in range(G):
                        act.activation(z[j][:, b, :], mix[j][:, b, :], ACT.Identity, bias=shift[j][:, b:b + 1],
                                       scale=norms[j][2][:, b:b + 1]).then_inc(z_normed, 1)

                inputs(0, 0, 0)
                with act.Fori(0, NG // 2 - 1) as n:
                    inputs(n * 2 + 1, 1, n)
                    normed(n * 2, 0, n)
                    inputs(n * 2 + 2, 0, n + 1)
                    normed(n * 2 + 1, 1, n)
                inputs(NG - 1, 1, NG // 2 - 1)
                normed(NG - 2, 0, NG // 2 - 1)
                normed(NG - 1, 1, NG // 2 - 1)

            @block.vector
            def _(dve):
                dve.wait_ge(ln_in, 32)

                def turn(f, k, j, u):
                    if f is not None:
                        stats, moments, rstd = norms[j]
                        dve.wait_ge(ya_in[j], u * 32 + 32)
                        dve.wait_ge(yb_in[j], u * 32 + 32)
                        dve.tensor_tensor(ya[j], ya[j], yb[j], ALU.add).then_inc(mixed, 1)
                        dve.wait_ge(mixed, f + 1)
                        dve.wait_ge(xf_again, f * G + G)
                        dve.wait_ge(z_normed, f * G + (FREE - G))
                        dve.tensor_tensor(mix[j], ya[j], xfc[j], ALU.add).then_inc(mix_done, 1)
                        dve.wait_ge(mix_done, f + (1 + FREE))
                        for b in range(G):
                            dve.bn_stats(stats[:, b, :], mix[j][:, b, :]).then_inc(stats_d, 1)
                        for b in range(G):
                            dve.wait_ge(stats_d, f * G + (b + 1))
                            apart(dve)
                            dve.bn_aggr(moments[:, b, :], stats[:, b, :]).then_inc(moments_d, 1)
                    if k is not None:
                        dve.wait_ge(z_normed, k * G + (G + FREE))
                        dve.tensor_tensor(z[1 - j], z[1 - j], g_sb.unsqueeze(1).to_broadcast([P, G, D]), ALU.mult)\
                           .then_inc(z_scaled, 1)
                        dve.wait_ge(z_scaled, k + 1)
                        dve.wait_ge(res_ready, k + 1)
                        dve.tensor_tensor(z[1 - j], z[1 - j], res_b[1 - j], ALU.add).then_inc(out_ready, 1)
                    if f is not None:
                        dve.wait_ge(rstd_d, f + 1)
                        dve.scalar_tensor_tensor(shift[j], moments[:, :, 0], -1.0, rstd, ALU.mult, ALU.mult)\
                           .then_inc(shift_done, 1)
                turns(dve, turn)


def kernel(**inputs):
    import numpy as np
    import concourse.bacc as bacc
    from concourse import mybir as mb
    from concourse.bass_utils import run_bass_kernel_spmd

    a = {k: np.asarray(v) for k, v in inputs.items()}
    lay = np.ascontiguousarray
    arrays = {
        "x": a["x"],
        "ctx_rows": a["ctx_1024"],
        "ctx_cols": lay(a["ctx_1024"].transpose(0, 2, 1)),
        "w_qkv": lay(np.concatenate([a["L0_attn_wq"].T, a["L0_attn_wv"].T, a["L0_attn_wk"].T], axis=1)),
        "b_qv": lay(np.concatenate([a["L0_attn_bq"], a["L0_attn_bv"]])),
        "b_k": a["L0_attn_bk"],
        "w_o": lay(a["L0_attn_wo"].T),
        "b_o": a["L0_attn_bo"],
        "gate_w": a["L0_ffn_gate_w"],
        "w1": a["L0_ffn_w1"],
        "b1": a["L0_ffn_b1"],
        "ln1_g": a["L0_ffn_ln1_g"],
        "ln1_b": a["L0_ffn_ln1_b"],
        "w2": a["L0_ffn_w2"],
        "b2": a["L0_ffn_b2"],
        "ln_g": a["L0_ffn_ln_g"],
        "ln_b": a["L0_ffn_ln_b"],
    }
    nc = bacc.Bacc("TRN2", target_bir_lowering=False, num_devices=1)
    aps = [nc.dram_tensor(f"{k}_dram", v.shape, mb.dt.from_np(v.dtype), kind="ExternalInput").ap()
           for k, v in arrays.items()]
    out = nc.dram_tensor("out_dram", a["x"].shape, mb.dt.float32, kind="ExternalOutput").ap()
    decoder_layer(nc, *aps, out)
    r = run_bass_kernel_spmd(nc, [{f"{k}_dram": v for k, v in arrays.items()}], core_ids=[0])
    return r.results[0]["out_dram"]
```
